# Optimizing a Trainium2 kernel written in Bass

```python
import numpy as np
import jax
import jax.numpy as jnp

def _softmax(x, axis=-1):
    return jax.nn.softmax(x, axis=axis)

def _gelu(x):
    return jax.nn.gelu(x, approximate=True)

def _silu(x):
    return jax.nn.silu(x)

def _sigmoid(x):
    return jax.nn.sigmoid(x)

def _layernorm(x, axis=-1, eps=1e-05):
    m = jnp.mean(x, axis=axis, keepdims=True)
    v = jnp.var(x, axis=axis, keepdims=True)
    return (x - m) / jnp.sqrt(v + eps)

def _scatter_add(tgt, idx, src, axis=0):
    return tgt.at[idx].add(src)

def _segment_sum(src, seg, n):
    return jax.ops.segment_sum(src, seg, n)
kernel_name = 'mk_macaron_d2_jaxref_r8_6e575e'

def setup_inputs(seed: int=0):
    np.random.seed(seed)
    _w = jnp.asarray

    def _L0_attn_setup():
        import jax, jax.numpy as jnp
        import numpy as np
        B, T = (4, 256)
        D_MODEL = 128
        N_HEADS = 8
        HEAD_DIM = 32
        KV_LRANK = 64

        def _orthogonalize_per_head(w):
            chunks = w.reshape(N_HEADS, HEAD_DIM, D_MODEL)

            def ns(m):
                A = m @ m.T
                Bm = 1.5 * jnp.eye(HEAD_DIM, dtype=m.dtype) - 0.5 * A
                return Bm @ m
            return jax.vmap(ns)(chunks).reshape(w.shape)
        key = jax.random.key(seed)
        ks = jax.random.split(key, 6)

        def lin(k, out_dim, in_dim):
            bound = 1.0 / np.sqrt(in_dim)
            return jax.random.uniform(k, (out_dim, in_dim), jnp.float32, -bound, bound)
        Wq = _orthogonalize_per_head(lin(ks[0], N_HEADS * HEAD_DIM, D_MODEL))
        return {'x': jax.random.normal(ks[1], (B, T, D_MODEL), jnp.float32), 'Wq': Wq, 'Wkv_down': lin(ks[2], KV_LRANK, D_MODEL), 'Wk_up': lin(ks[3], N_HEADS * HEAD_DIM, KV_LRANK), 'Wv_up': lin(ks[4], N_HEADS * HEAD_DIM, KV_LRANK), 'Wo': lin(ks[5], D_MODEL, N_HEADS * HEAD_DIM)}
    _L0_attn_in = _L0_attn_setup()

    def _L0_ffn_setup():
        import jax, jax.numpy as jnp
        import numpy as np
        B, S, D, E = (4, 256, 128, 8)
        key = jax.random.key(seed)
        ks = jax.random.split(key, 5)
        s = 0.02
        return {'hidden_states': jax.random.normal(ks[0], (B, S, D), dtype=jnp.float32), 'Wr': jax.random.normal(ks[1], (D, E), dtype=jnp.float32) * s, 'br': jnp.zeros((E,), dtype=jnp.float32), 'W1': jax.random.normal(ks[2], (E, D, 4 * D), dtype=jnp.float32) * s, 'b1': jnp.zeros((E, 4 * D), dtype=jnp.float32), 'W2': jax.random.normal(ks[3], (E, 4 * D, 2 * D), dtype=jnp.float32) * s, 'b2': jnp.zeros((E, 2 * D), dtype=jnp.float32), 'W3': jax.random.normal(ks[4], (E, 2 * D, D), dtype=jnp.float32) * s, 'b3': jnp.zeros((E, D), dtype=jnp.float32)}
    _L0_ffn_in = _L0_ffn_setup()

    def _L1_attn_setup():
        import jax, jax.numpy as jnp
        import numpy as np
        B, L, D = (2, 256, 128)
        H = 16
        DH = D // H

        def rope_tables(seq_len, dim):
            inv_freq = 1.0 / 10000.0 ** (jnp.arange(0, dim, 2, dtype=jnp.float32) / dim)
            t = jnp.arange(seq_len, dtype=jnp.float32)
            freqs = jnp.outer(t, inv_freq)
            emb = jnp.concatenate([freqs, freqs], -1)
            return (jnp.cos(emb), jnp.sin(emb))

        def rotate_half(x):
            x1, x2 = (x[..., :x.shape[-1] // 2], x[..., x.shape[-1] // 2:])
            return jnp.concatenate([-x2, x1], axis=-1)
        key = jax.random.key(seed)
        k1, k2, k3 = jax.random.split(key, 3)
        x = jax.random.normal(k1, (B, L, D), dtype=jnp.float32)
        Wqkv = jax.random.normal(k2, (D, 3 * D), dtype=jnp.float32) / np.sqrt(D)
        Wo = jax.random.normal(k3, (D, D), dtype=jnp.float32) / np.sqrt(D)
        return {'x': x, 'Wqkv': Wqkv, 'Wo': Wo}
    _L1_attn_in = _L1_attn_setup()

    def _L1_ffn_setup():
        import jax, jax.numpy as jnp
        import numpy as np
        TOPK = 4
        key = jax.random.key(seed)
        ks = jax.random.split(key, 9)
        B, T, D = (4, 256, 128)
        E, H = (32, 128)
        HS = H * TOPK
        s = lambda k, shape, fan: jax.random.normal(k, shape, dtype=jnp.float32) / np.sqrt(fan)
        return {'x': jax.random.normal(ks[0], (B, T, D), dtype=jnp.float32), 'router_w': s(ks[1], (E, D), D), 'router_bias': jnp.zeros((E,), dtype=jnp.float32), 'gate_w': s(ks[2], (E, H, D), D), 'up_w': s(ks[3], (E, H, D), D), 'down_w': s(ks[4], (E, D, H), H), 'sgate_w': s(ks[5], (HS, D), D), 'sup_w': s(ks[6], (HS, D), D), 'sdown_w': s(ks[7], (D, HS), HS)}
    _L1_ffn_in = _L1_ffn_setup()
    _d = {'L0_attn_x': _L0_attn_in['x'], 'L0_attn_Wq': _L0_attn_in['Wq'], 'L0_attn_Wkv_down': _L0_attn_in['Wkv_down'], 'L0_attn_Wk_up': _L0_attn_in['Wk_up'], 'L0_attn_Wv_up': _L0_attn_in['Wv_up'], 'L0_attn_Wo': _L0_attn_in['Wo'], 'L0_ffn_Wr': _L0_ffn_in['Wr'], 'L0_ffn_br': _L0_ffn_in['br'], 'L0_ffn_W1': _L0_ffn_in['W1'], 'L0_ffn_b1': _L0_ffn_in['b1'], 'L0_ffn_W2': _L0_ffn_in['W2'], 'L0_ffn_b2': _L0_ffn_in['b2'], 'L0_ffn_W3': _L0_ffn_in['W3'], 'L0_ffn_b3': _L0_ffn_in['b3'], 'L1_attn_Wqkv': _L1_attn_in['Wqkv'], 'L1_attn_Wo': _L1_attn_in['Wo'], 'L1_ffn_router_w': _L1_ffn_in['router_w'], 'L1_ffn_router_bias': _L1_ffn_in['router_bias'], 'L1_ffn_gate_w': _L1_ffn_in['gate_w'], 'L1_ffn_up_w': _L1_ffn_in['up_w'], 'L1_ffn_down_w': _L1_ffn_in['down_w'], 'L1_ffn_sgate_w': _L1_ffn_in['sgate_w'], 'L1_ffn_sup_w': _L1_ffn_in['sup_w'], 'L1_ffn_sdown_w': _L1_ffn_in['sdown_w']}
    _x0 = _d['L0_attn_x']
    _d['L0_attn_x'] = jax.random.normal(jax.random.fold_in(jax.random.key(seed), 1), (1, 2048, 128), dtype=_x0.dtype)
    del _x0
    return _d

def reference(L0_attn_x, L0_attn_Wq, L0_attn_Wkv_down, L0_attn_Wk_up, L0_attn_Wv_up, L0_attn_Wo, L0_ffn_Wr, L0_ffn_br, L0_ffn_W1, L0_ffn_b1, L0_ffn_W2, L0_ffn_b2, L0_ffn_W3, L0_ffn_b3, L1_attn_Wqkv, L1_attn_Wo, L1_ffn_router_w, L1_ffn_router_bias, L1_ffn_gate_w, L1_ffn_up_w, L1_ffn_down_w, L1_ffn_sgate_w, L1_ffn_sup_w, L1_ffn_sdown_w):

    def _L0_attn_ref(x, Wq, Wkv_down, Wk_up, Wv_up, Wo):
        import jax, jax.numpy as jnp
        import numpy as np
        B, T = (4, 256)
        D_MODEL = 128
        N_HEADS = 8
        HEAD_DIM = 32
        KV_LRANK = 64

        def _orthogonalize_per_head(w):
            chunks = w.reshape(N_HEADS, HEAD_DIM, D_MODEL)

            def ns(m):
                A = m @ m.T
                Bm = 1.5 * jnp.eye(HEAD_DIM, dtype=m.dtype) - 0.5 * A
                return Bm @ m
            return jax.vmap(ns)(chunks).reshape(w.shape)
        b, t, _ = x.shape
        q = (x @ Wq.T).reshape(b, t, N_HEADS, HEAD_DIM)
        kv_latent = x @ Wkv_down.T
        k = (kv_latent @ Wk_up.T).reshape(b, t, N_HEADS, HEAD_DIM)
        v = (kv_latent @ Wv_up.T).reshape(b, t, N_HEADS, HEAD_DIM)
        scale = HEAD_DIM ** (-0.5)
        scores = jnp.einsum('bqhd,bkhd->bhqk', q, k) * scale
        attn = jax.nn.softmax(scores, axis=-1)
        out = jnp.einsum('bhqk,bkhd->bqhd', attn, v)
        out = out.reshape(b, t, N_HEADS * HEAD_DIM)
        return out @ Wo.T

    def _L0_ffn_ref(hidden_states, Wr, br, W1, b1, W2, b2, W3, b3):
        import jax, jax.numpy as jnp
        import numpy as np
        B, S, D, E = (4, 256, 128, 8)
        b, s, d = hidden_states.shape
        num_experts = Wr.shape[1]
        x = hidden_states.reshape(-1, d)
        router_logits = x @ Wr + br
        expert_mask = jax.nn.one_hot(jnp.argmax(router_logits, axis=-1), num_experts, dtype=x.dtype)
        out = jnp.zeros_like(x)
        for e in range(num_experts):
            h = jax.nn.gelu(x @ W1[e] + b1[e], approximate=False)
            h = jax.nn.gelu(h @ W2[e] + b2[e], approximate=False)
            y = h @ W3[e] + b3[e]
            out = out + expert_mask[:, e:e + 1] * y
        return out.reshape(b, s, d)

    def _L1_attn_ref(x, Wqkv, Wo):
        import jax, jax.numpy as jnp
        import numpy as np
        B, L, D = (2, 256, 128)
        H = 16
        DH = D // H

        def rope_tables(seq_len, dim):
            inv_freq = 1.0 / 10000.0 ** (jnp.arange(0, dim, 2, dtype=jnp.float32) / dim)
            t = jnp.arange(seq_len, dtype=jnp.float32)
            freqs = jnp.outer(t, inv_freq)
            emb = jnp.concatenate([freqs, freqs], -1)
            return (jnp.cos(emb), jnp.sin(emb))

        def rotate_half(x):
            x1, x2 = (x[..., :x.shape[-1] // 2], x[..., x.shape[-1] // 2:])
            return jnp.concatenate([-x2, x1], axis=-1)
        b, l, d = x.shape
        qkv = (x @ Wqkv).reshape(b, l, 3, H, DH)
        q, k, v = (qkv[:, :, 0], qkv[:, :, 1], qkv[:, :, 2])
        cos, sin = rope_tables(l, DH)
        cos = cos[:, None, :]
        sin = sin[:, None, :]
        q = q * cos + rotate_half(q) * sin
        k = k * cos + rotate_half(k) * sin
        scale = DH ** (-0.5)
        scores = jnp.einsum('bqhd,bkhd->bhqk', q, k) * scale
        attn = jax.nn.softmax(scores, axis=-1)
        out = jnp.einsum('bhqk,bkhd->bqhd', attn, v)
        out = out.reshape(b, l, d)
        return out @ Wo

    def _L1_ffn_ref(x, router_w, router_bias, gate_w, up_w, down_w, sgate_w, sup_w, sdown_w):
        import jax, jax.numpy as jnp
        import numpy as np
        TOPK = 4
        B, T, D = x.shape
        flat = x.reshape(B * T, D)
        logits = flat.astype(jnp.float32) @ router_w.T + router_bias
        scores = jax.nn.softmax(logits, axis=-1)
        topk_scores, topk_idx = jax.lax.top_k(scores, TOPK)
        topk_scores = topk_scores / jnp.clip(topk_scores.sum(axis=-1, keepdims=True), 1e-12, None)
        h = jax.nn.silu(jnp.einsum('nd,ehd->neh', flat, gate_w)) * jnp.einsum('nd,ehd->neh', flat, up_w)
        expert_out = jnp.einsum('neh,edh->ned', h, down_w)
        sel = jnp.take_along_axis(expert_out, topk_idx[:, :, None], axis=1)
        out = (sel * topk_scores.astype(flat.dtype)[:, :, None]).sum(axis=1)
        out = out + jax.nn.silu(flat @ sgate_w.T) * (flat @ sup_w.T) @ sdown_w.T
        return out.reshape(B, T, D)
    x = L0_attn_x
    x = x + 0.5 * _L0_ffn_ref(_layernorm(x, axis=-1), L0_ffn_Wr, L0_ffn_br, L0_ffn_W1, L0_ffn_b1, L0_ffn_W2, L0_ffn_b2, L0_ffn_W3, L0_ffn_b3)
    x = x + _L0_attn_ref(_layernorm(x, axis=-1), L0_attn_Wq, L0_attn_Wkv_down, L0_attn_Wk_up, L0_attn_Wv_up, L0_attn_Wo)
    x = x + 0.5 * _L0_ffn_ref(_layernorm(x, axis=-1), L0_ffn_Wr, L0_ffn_br, L0_ffn_W1, L0_ffn_b1, L0_ffn_W2, L0_ffn_b2, L0_ffn_W3, L0_ffn_b3)
    x = x + 0.5 * _L1_ffn_ref(_layernorm(x, axis=-1), L1_ffn_router_w, L1_ffn_router_bias, L1_ffn_gate_w, L1_ffn_up_w, L1_ffn_down_w, L1_ffn_sgate_w, L1_ffn_sup_w, L1_ffn_sdown_w)
    x = x + _L1_attn_ref(_layernorm(x, axis=-1), L1_attn_Wqkv, L1_attn_Wo)
    x = x + 0.5 * _L1_ffn_ref(_layernorm(x, axis=-1), L1_ffn_router_w, L1_ffn_router_bias, L1_ffn_gate_w, L1_ffn_up_w, L1_ffn_down_w, L1_ffn_sgate_w, L1_ffn_sup_w, L1_ffn_sdown_w)
    return x

_drawn_inputs = setup_inputs


def setup_inputs(seed=0):
    import zlib

    import numpy as np

    out = dict(_drawn_inputs(seed))
    spreads = {'L0_ffn_br': (0.0, 0.1),
     'L0_ffn_b1': (0.0, 0.603),
     'L0_ffn_b2': (0.0, 0.1),
     'L0_ffn_b3': (0.0, 0.1),
     'L1_ffn_router_bias': (0.0, 0.1)}
    factors = {'L0_attn_Wq': 3.476,
     'L0_attn_Wkv_down': 3.482,
     'L0_attn_Wk_up': 3.413,
     'L0_ffn_W1': 3.177,
     'L0_ffn_W2': 3.075}
    for name, (base, spread) in spreads.items():
        noise = np.random.default_rng([zlib.crc32(name.encode()), seed]).standard_normal(out[name].shape)
        drawn = base * np.exp(spread * noise) if base else spread * noise
        out[name] = jnp.asarray(drawn.astype(out[name].dtype))
    for name, factor in factors.items():
        out[name] = (out[name] * factor).astype(out[name].dtype)
    return out
```

```python
import numpy as np
import concourse.bass as bass
from concourse import mybir
from contextlib import ExitStack

F32 = mybir.dt.float32
BF16 = mybir.dt.bfloat16
I32 = mybir.dt.int32
U32 = mybir.dt.uint32
ALU = mybir.AluOpType
ACT = mybir.ActivationFunctionType
AX = mybir.AxisListType

P = 128
N = 2048
D = 128
NT = N // P
BANK = 512
NC4 = N // BANK
EPS = 1e-5


class Scope:

    used = []

    def __init__(self, nc, ctx, prefix):
        self.nc, self.ctx, self.prefix = nc, ctx, prefix

    def sb(self, name, shape, dt=F32):
        return self.ctx.enter_context(self.nc.sbuf_tensor(f"{self.prefix}_{name}", shape, dt))

    def ps(self, name, shape, dt=F32):
        return self.ctx.enter_context(self.nc.psum_tensor(f"{self.prefix}_{name}", shape, dt))

    def sem(self, name):
        s = self.nc.alloc_semaphore(f"{self.prefix}_{name}")
        Scope.used.append(s)
        return s


def clear_semaphores(nc):
    nc.clear_and_free_semaphores(Scope.used)
    nc.all_engine_barrier()
    Scope.used = []


def layernorm_phase(nc, prefix, x_sb, xn, xnT, ident):
    with ExitStack() as ctx:
        sc = Scope(nc, ctx, prefix)
        stats = sc.sb("stats", [P, NT, 6])
        meanvar = sc.sb("meanvar", [P, NT, 2])
        std = sc.sb("std", [P, NT])
        rstd = sc.sb("rstd", [P, NT])
        eps = sc.sb("eps", [P, 1])
        tp = sc.ps("tp", [P, NC4, BANK])
        stats_done = sc.sem("stats_done")
        var_done = sc.sem("var_done")
        std_done = sc.sem("std_done")
        rstd_done = sc.sem("rstd_done")
        xn_done = sc.sem("xn_done")
        tp_done = sc.sem("tp_done")
        eps_set = sc.sem("eps_set")
        copied = sc.sem("copied")
        block = ctx.enter_context(nc.Block())

        @block.vector
        def _(dve):
            dve.memset(eps[:, :], EPS).then_inc(eps_set, 1)
            for t in range(NT):
                dve.bn_stats(stats[:, t, :], x_sb[:, t, :]).then_inc(stats_done, 1)
            for t in range(NT):
                dve.wait_ge(stats_done, t + 1)
                dve.bn_aggr(meanvar[:, t, :], stats[:, t, :]).then_inc(var_done, 1)
            dve.wait_ge(std_done, 1)
            dve.reciprocal(rstd[:, :], std[:, :]).then_inc(rstd_done, 1)
            dve.wait_ge(rstd_done, 1)
            for t in range(NT):
                dve.tensor_scalar(xn[:, t, :], x_sb[:, t, :], meanvar[:, t, 0:1], rstd[:, t:t + 1],
                                  ALU.subtract, ALU.mult).then_inc(xn_done, 1)

        @block.scalar
        def _(act):
            act.wait_ge(eps_set, 1)
            act.wait_ge(var_done, NT)
            act.activation(std[:, :], meanvar[:, :, 1], ACT.Sqrt, bias=eps[:, 0:1]).then_inc(std_done, 1)
            for c in range(NC4):
                act.wait_ge(tp_done, 4 * (c + 1))
                act.copy(xnT[:, c * BANK:(c + 1) * BANK], tp[:, c, :]).then_inc(copied, 1)
            act.wait_ge(copied, NC4)

        @block.tensor
        def _(pe):
            for t in range(NT):
                pe.wait_ge(xn_done, t + 1)
                pe.transpose(tp[:, t // 4, (t % 4) * P:(t % 4 + 1) * P], xn[:, t, :], ident[:, :]).then_inc(tp_done, 1)


class AttnShape:

    def __init__(self, heads, hd, units):
        self.H, self.HD = heads, hd
        self.R = heads * hd
        self.RH = self.R // P
        self.U = units
        self.G = NC4 // units
        self.W = P // self.G
        self.STEPS = units * NT
        self.CH = self.STEPS * self.G
        self.MPS = 32 // self.STEPS
        self.terms = [(0, 0), (0, 1), (1, 0), (1, 1), (0, 2), (2, 0)]
        self.per = min(P // hd, 6)
        self.stacks = 2 if hd * 6 > 96 else 1
        self.K_MAX = max(96, self.per * hd)
        self.ROW_MAX = 96


def scores_phase(nc, prefix, sh, parts_q, parts_k, max_dram, v_all, attn_tok, ident, ident_bf, scale):
    H, HD, G, W, U, STEPS, CH = sh.H, sh.HD, sh.G, sh.W, sh.U, sh.STEPS, sh.CH
    MCH, SLOTS, SBANKS, SHIFT = 32, 8, 3, 3
    TURNS = MCH + 1 + U
    AHEAD = 12
    LEAD = MCH + AHEAD + 1
    with ExitStack() as ctx:
        sc = Scope(nc, ctx, prefix)
        mq = [sc.sb(f"mq{i}", [P, N], BF16) for i in range(2)]
        mk = [sc.sb(f"mk{i}", [P, N], BF16) for i in range(2)]
        sq = [[sc.sb(f"sq{i}_{j}", [P, N], BF16) for j in range(sh.stacks)] for i in range(2)]
        sk = [[sc.sb(f"sk{i}_{j}", [P, N], BF16) for j in range(sh.stacks)] for i in range(2)]
        vh = [sc.sb(f"vh{i}", [P, NT, W]) for i in range(2)]
        probs = sc.sb("probs", [P, SLOTS, BANK])
        half_max = sc.sb("half_max", [P, 2, NT, 2])
        row_max = sc.sb("row_max", [P, NT])
        max_parts = sc.sb("max_parts", [P, 2, NT], BF16)
        max_rows = sc.sb("max_rows", [2 * NT, P], BF16)
        o_sb = [sc.sb(f"o_sb{i}", [P, BANK]) for i in range(2)]
        rsum = sc.sb("rsum", [P, G, 4])
        ps_m = sc.ps("ps_m", [P, 2, 2 * BANK])
        ps_s = sc.ps("ps_s", [P, SBANKS, BANK])
        ps_o = sc.ps("ps_o", [P, BANK])

        cleared = sc.sem("cleared")
        mstack_in = [sc.sem(f"mstack_in{i}") for i in range(2)]
        sstack_in = [sc.sem(f"sstack_in{i}") for i in range(2)]
        maxrow_out = sc.sem("maxrow_out")
        maxrow_in = [sc.sem(f"maxrow_in{i}") for i in range(2)]
        v_in = sc.sem("v_in")
        m_done = sc.sem("m_done")
        m_used = sc.sem("m_used")
        s_done = sc.sem("s_done")
        exp_done = sc.sem("exp_done")
        pv_done = sc.sem("pv_done")
        o_copied = sc.sem("o_copied")
        parts_done = sc.sem("parts_done")
        split_step = sc.sem("split_step")
        zeroed = sc.sem("zeroed")
        norm_step = sc.sem("norm_step")
        block = ctx.enter_context(nc.Block())
        FREE_STEPS = SLOTS // G

        def round_turns(with_next, with_second):
            out = []
            for r in range(STEPS):
                if U == 2 and r == NT + 2 - SHIFT:
                    out.append((r, "x", 0))
                if r == STEPS - 1:
                    out.append((r, "x", U - 1))
                for c in range(r * sh.MPS, (r + 1) * sh.MPS):
                    if c < MCH - AHEAD:
                        if with_next:
                            out.append((r, "m", (1, AHEAD + c)))
                    else:
                        if with_second:
                            out.append((r, "m", (2, c - (MCH - AHEAD))))
                        if with_next and c == MCH - AHEAD + 1:
                            out.append((r, "t", None))
            return out

        rounds = {"loop": round_turns(True, True), "second last": round_turns(True, False),
                  "last": round_turns(False, False)}
        assert len(rounds["loop"]) == TURNS

        def turn_base(h):
            if type(h) is int and h == H - 1:
                return LEAD + (H - 2) * TURNS + len(rounds["second last"])
            return LEAD + h * TURNS

        def slot(h, par, idx):
            return (turn_base(h if type(h) is int else par) + idx) % 2

        def t_turn(h):
            if type(h) is int and h == 0:
                return MCH + 2
            where = [k for _, k, _ in rounds["loop"] if k != "skip"]
            idx = where.index("t")
            if type(h) is int and h == H - 1:
                idx = [k for _, k, _ in rounds["second last"]].index("t")
            return turn_base(h - 1) + idx

        def run_rounds(eng, one):
            with eng.Fori(0, H // 2 - 1) as i:
                for par in range(2):
                    one(i * 2 + par, par, "loop", lambda ahead, par=par: i + (par + ahead) // 2 + 1)
            for h, kind in ((H - 2, "second last"), (H - 1, "last")):
                one(h, h % 2, kind, lambda ahead, h=h: (h + ahead) // 2 + 1)

        @block.sync
        def _(sp):
            def load(stack_q, stack_k, terms, h, sem):
                for r, (a, b) in enumerate(terms):
                    rows = slice(r * HD, (r + 1) * HD)
                    sp.dma_start(stack_q[rows, :], parts_q[a, bass.ds(h * HD, HD), :]).then_inc(sem, 16)
                    sp.dma_start(stack_k[rows, :], parts_k[b, bass.ds(h * HD, HD), :]).then_inc(sem, 16)

            def load_max_stack(h, par):
                load(mq[par], mk[par], sh.terms[:sh.per], h, mstack_in[par])

            def load_score_stacks(h, par):
                for j in range(sh.stacks):
                    load(sq[par][j], sk[par][j], sh.terms[j * sh.per:(j + 1) * sh.per], h, sstack_in[par])

            def load_max_rows(h, par):
                sp.wait_ge(m_used, 2 + t_turn(h) + 1)
                sp.dma_start(max_dram, max_rows[:, :]).then_inc(maxrow_out, 16)
                sp.wait_ge(maxrow_out, (h + 1) * 16)
                sp.dma_start(sq[par][-1][sh.ROW_MAX:sh.ROW_MAX + 2, :],
                             max_dram.rearrange("(a t) n -> a (t n)", a=2)).then_inc(maxrow_in[par], 16)

            sp.wait_ge(cleared, 1)
            load_max_stack(0, 0)
            load_max_stack(1, 1)
            load_score_stacks(0, 0)
            load_max_rows(0, 0)

            def one(h, par, kind, loads):
                if kind != "last":
                    sp.wait_ge(s_done, h * CH + 1)
                    load_score_stacks(h + 1, 1 - par)
                if kind == "loop":
                    sp.wait_ge(m_done, turn_base(h) + 1)
                    load_max_stack(h + 2, par)
                if kind != "last":
                    load_max_rows(h + 1, 1 - par)

            run_rounds(sp, one)

        @block.gpsimd
        def _(pool):
            for i in range(2):
                pool.memset(vh[i][:, :, :], 0.0)
                for t in [mq[i], mk[i]] + sq[i] + sk[i]:
                    pool.memset(t[:, :].bitcast(U32), 0)
            pool.memset(o_sb[0][:, 0:1], 0.0).then_inc(zeroed, 1)
            pool.wait_ge(zeroed, 1)
            for i in range(2):
                pool.memset(vh[i][:, :, HD:HD + 1], 1.0).then_inc(zeroed, 1)
                pool.wait_ge(zeroed, 2 + 2 * i)
                pool.memset(sk[i][-1][sh.ROW_MAX:sh.ROW_MAX + 2, :], -1.0).then_inc(zeroed, 1)
                pool.wait_ge(zeroed, 3 + 2 * i)
            pool.sem_inc(cleared, 1)

            def copy_v(h, par):
                pool.tensor_copy(vh[par][:, :, 0:HD], v_all[:, :, bass.ds(h * HD, HD)]).then_inc(v_in, 1)

            copy_v(0, 0)
            copy_v(1, 1)

            def one(h, par, kind, loads):
                if kind == "loop":
                    pool.wait_ge(pv_done, FREE_STEPS + (h + 1) * STEPS)
                    copy_v(h + 2, par)

            run_rounds(pool, one)

        @block.tensor
        def _(pe):
            def turn(number, slot, kind, what, h, par, loads):
                pe.wait_ge(m_used, number + 1)
                if kind == "m":
                    ahead, c = what
                    of = (par + ahead) % 2
                    if c == 0:
                        pe.wait_ge(mstack_in[of], loads(ahead) * (32 * sh.per))
                    t, half = c // 2, c % 2
                    for b in range(2):
                        col = (2 * half + b) * BANK
                        last = pe.matmul(ps_m[:, slot, b * BANK:(b + 1) * BANK],
                                         mq[of][0:sh.K_MAX, t * P:(t + 1) * P],
                                         mk[of][0:sh.K_MAX, col:col + BANK], start=True, stop=True)
                    last.then_inc(m_done, 1)
                elif kind == "t":
                    pe.wait_ge(parts_done, h + 2)
                    pe.transpose(ps_m[0:2 * NT, slot, 0:P // 2].bitcast(BF16),
                                 max_parts[:, :, :].rearrange("p a t -> p (a t)"), ident_bf[:, :]).then_inc(m_done, 1)
                else:
                    pe.wait_ge(o_copied, h * U + what + 2)
                    src = o_sb[what if U == 2 else par]
                    for c in range(4):
                        last = pe.transpose(ps_m[:, slot, c * P:(c + 1) * P], src[:, c * P:(c + 1) * P], ident[:, :])
                    last.then_inc(m_done, 1)

            def score_chunk(h, par, q):
                s, g = q // G, q % G
                kt, col = s % NT, (s // NT * G + g) * BANK
                before = q - SBANKS if q >= SBANKS else max(c for c in range(CH) if c % SBANKS == q) - CH
                pe.wait_ge(exp_done, h * CH + (SBANKS + before + 1))
                for j in range(sh.stacks):
                    rows = P if j < sh.stacks - 1 else sh.ROW_MAX + 2
                    last = pe.matmul(ps_s[:, q % SBANKS, :], sk[par][j][0:rows, kt * P:(kt + 1) * P],
                                     sq[par][j][0:rows, col:col + BANK], start=(j == 0), stop=(j == sh.stacks - 1))
                last.then_inc(s_done, 1)

            def probs_v(h, par, s):
                kt = s % NT
                pe.wait_ge(exp_done, h * CH + (SBANKS + G * (s + 1)))
                if kt == 0:
                    pe.wait_ge(o_copied, h * U + (s // NT + 1))
                if s == 0:
                    pe.wait_ge(v_in, h + 1)
                for g in range(G):
                    last = pe.matmul(ps_o[g * W:(g + 1) * W, :], vh[par][:, kt, :], probs[:, (s * G + g) % SLOTS, :],
                                     start=(kt == 0), stop=(kt == NT - 1))
                last.then_inc(pv_done, 1)

            def step(h, par, s, between, before, loads_of):
                if s == 0:
                    pe.wait_ge(sstack_in[par], loads_of * (32 * 6))
                    pe.wait_ge(maxrow_in[par], loads_of * 16)
                between = list(between)
                for g in range(G):
                    score_chunk(h, par, s * G + g)
                    if between:
                        between.pop(0)()
                while between:
                    between.pop(0)()
                if before:
                    probs_v(*before)

            pe.wait_ge(cleared, 1)
            pe.sem_inc(pv_done, FREE_STEPS)
            for c in range(MCH):
                turn(c, c % 2, "m", (0, c), 0, 0, lambda ahead: 1)
            n = MCH
            for c in range(AHEAD):
                turn(n, n % 2, "m", (1, c), 0, 0, lambda ahead: 1)
                n += 1
                if c == 1:
                    turn(n, n % 2, "t", None, -1, 0, None)
                    n += 1
            for s in range(SHIFT):
                step(0, 0, s, [], (0, 0, s - 1) if s else None, 1)

            def one(h, par, kind, loads):
                mine = rounds[kind]
                for r in range(STEPS):
                    between = [lambda i=i, k=k, w=w: turn(turn_base(h) + i, slot(h, par, i), k, w, h, par, loads)
                               for i, (at, k, w) in enumerate(mine) if at == r]
                    s = r + SHIFT
                    if s < STEPS:
                        step(h, par, s, between, (h, par, s - 1), None)
                    elif kind != "last":
                        s -= STEPS
                        before = (h, par, STEPS - 1) if s == 0 else (h + 1, 1 - par, s - 1)
                        step(h + 1, 1 - par, s, between, before, loads(1))
                    else:
                        if s == STEPS:
                            probs_v(h, par, STEPS - 1)
                        for b in between:
                            b()

            run_rounds(pe, one)

        @block.scalar
        def _(act):
            act.sem_inc(exp_done, SBANKS)
            act.sem_inc(o_copied, 1)

            def exps(h, s):
                for q in range(s * G, (s + 1) * G):
                    act.wait_ge(s_done, h * CH + (q + 1))
                    if q == s * G:
                        act.wait_ge(pv_done, h * STEPS + (s + 1))
                    act.activation(probs[:, q % SLOTS, :], ps_s[:, q % SBANKS, :], ACT.Exp,
                                   scale=scale).then_inc(exp_done, 1)

            def copy_out(h, par, unit):
                act.wait_ge(pv_done, h * STEPS + (FREE_STEPS + (unit + 1) * NT))
                act.copy(o_sb[unit if U == 2 else par][:, :], ps_o[:, :]).then_inc(o_copied, 1)

            def one(h, par, kind, loads):
                for s in range(1, STEPS):
                    exps(h, s)
                    if s == NT:
                        copy_out(h, par, 0)
                if kind != "last":
                    exps(h + 1, 0)
                copy_out(h, par, U - 1)

            exps(0, 0)
            run_rounds(act, one)

        @block.vector
        def _(dve):
            dve.sem_inc(m_used, 2)

            def read_max(number, slot, of, c):
                dve.wait_ge(m_done, number + 1)
                dve.reduce_max(half_max[:, of, c // 2, c % 2:c % 2 + 1], ps_m[:, slot, :], AX.X).then_inc(m_used, 1)

            def split_max(number, of, h):
                dve.wait_ge(m_used, number + 3)
                dve.tensor_tensor(row_max[:, :], half_max[:, of, :, 0], half_max[:, of, :, 1],
                                  ALU.max).then_inc(split_step, 1)
                dve.wait_ge(split_step, h * 2 + 1)
                dve.tensor_copy(max_parts[:, 0, :], row_max[:, :]).then_inc(split_step, 1)
                dve.wait_ge(split_step, h * 2 + 2)
                dve.tensor_tensor(max_parts[:, 1, :], row_max[:, :], max_parts[:, 0, :],
                                  ALU.subtract).then_inc(parts_done, 1)

            def read_rows(number, slot, h):
                dve.wait_ge(m_done, number + 1)
                if not (type(h) is int and h == 0):
                    dve.wait_ge(maxrow_out, h * 16)
                dve.tensor_copy(max_rows[:, :], ps_m[0:2 * NT, slot, 0:P // 2].bitcast(BF16)).then_inc(m_used, 1)

            def read_out(number, slot, unit, h):
                dve.wait_ge(m_done, number + 1)
                dve.wait_ge(m_used, number + 2)
                src = ps_m[:, slot, 0:BANK].rearrange("p (c g w) -> p g c w", c=4, g=G)
                dve.reciprocal(rsum[:, :, :], src[:, :, :, HD]).then_inc(norm_step, 1)
                dve.wait_ge(norm_step, h * U + (unit + 1))
                t0 = unit * G * 4
                for g in range(G):
                    dst = attn_tok[:, t0 + 4 * g:t0 + 4 * g + 4, bass.ds(h * HD, HD)]
                    last = dve.tensor_tensor(dst, src[:, g, :, 0:HD],
                                             rsum[:, g, :].unsqueeze(2).to_broadcast([P, 4, HD]), ALU.mult)
                last.then_inc(m_used, 1)

            for c in range(MCH):
                read_max(c, c % 2, 0, c)
            split_max(MCH - 1, 0, 0)
            n = MCH
            for c in range(AHEAD):
                read_max(n, n % 2, 1, c)
                n += 1
                if c == 1:
                    read_rows(n, n % 2, 0)
                    n += 1

            def one(h, par, kind, loads):
                base = turn_base(h)
                for idx, (_, k, what) in enumerate(rounds[kind]):
                    if k == "m":
                        ahead, c = what
                        read_max(base + idx, slot(h, par, idx), (par + ahead) % 2, c)
                        if c == MCH - 1:
                            split_max(base + idx, (par + ahead) % 2, h + ahead)
                    elif k == "t":
                        read_rows(base + idx, slot(h, par, idx), h + 1)
                    else:
                        read_out(base + idx, slot(h, par, idx), what, h)

            run_rounds(dve, one)
            dve.wait_ge(m_used, turn_base(H - 1) + len(rounds["last"]) + 2)

def qkv_latent_phase(nc, prefix, sh, xnT, w, parts_q, parts_k, v_all):
    with ExitStack() as ctx:
        sc = Scope(nc, ctx, prefix)
        RANK = w["kv_down"].shape[1]
        RING, VRING = 4, 2
        latT = sc.sb("latT", [RANK, N])
        part = [sc.sb(f"part{i}", [P, 3, BANK], BF16) for i in range(RING)]
        rest = [sc.sb(f"rest{i}", [P, BANK]) for i in range(RING)]
        ps = sc.ps("ps", [P, RING, BANK])
        ps_lat = sc.ps("ps_lat", [RANK, 2, BANK])
        ps_v = sc.ps("ps_v", [P, VRING, BANK])
        lat_done, lat_copied = sc.sem("lat_done"), sc.sem("lat_copied")
        proj_done = sc.sem("proj_done")
        v_done, v_copied = sc.sem("v_done"), sc.sem("v_copied")
        high_done, mid_done = sc.sem("high_done"), sc.sem("mid_done")
        rest_done, low_done = sc.sem("rest_done"), sc.sem("low_done")
        part_out = [sc.sem(f"part_out{i}") for i in range(RING)]
        units = [(which, half, c) for which in (1, 0) for half in range(sh.RH) for c in range(NC4)]
        n_v = NT * sh.R // BANK
        block = ctx.enter_context(nc.Block())

        @block.tensor
        def _(pe):
            for c in range(NC4):
                if c >= 2:
                    pe.wait_ge(lat_copied, c - 1)
                pe.matmul(ps_lat[:, c % 2, :], w["kv_down"][:, :], xnT[:, c * BANK:(c + 1) * BANK],
                          start=True, stop=True).then_inc(lat_done, 1)
            for u, (which, half, c) in enumerate(units):
                if u >= RING:
                    pe.wait_ge(rest_done, u - RING + 1)
                cols = slice(half * P, (half + 1) * P)
                if which == 0:
                    last = pe.matmul(ps[:, u % RING, :], w["q"][:, cols], xnT[:, c * BANK:(c + 1) * BANK],
                                     start=True, stop=True)
                else:
                    pe.wait_ge(lat_copied, c + 1)
                    last = pe.matmul(ps[:, u % RING, :], w["k_up"][:, cols], latT[:, c * BANK:(c + 1) * BANK],
                                     start=True, stop=True)
                last.then_inc(proj_done, 1)
            for b in range(n_v):
                if b >= VRING:
                    pe.wait_ge(v_copied, b - VRING + 1)
                for i in range(2):
                    t = 2 * b + i
                    last = pe.matmul(ps_v[:, b % VRING, i * sh.R:(i + 1) * sh.R], latT[:, t * P:(t + 1) * P],
                                     w["v_up"][:, :], start=True, stop=True)
                last.then_inc(v_done, 1)

        @block.scalar
        def _(act):
            for c in range(NC4):
                act.wait_ge(lat_done, c + 1)
                act.copy(latT[:, c * BANK:(c + 1) * BANK], ps_lat[:, c % 2, :]).then_inc(lat_copied, 1)
            for u in range(len(units) + 1):
                if u < len(units):
                    act.wait_ge(proj_done, u + 1)
                    if u >= RING:
                        act.wait_ge(part_out[u % RING], 16 * (u // RING))
                    act.copy(part[u % RING][:, 0, :], ps[:, u % RING, :]).then_inc(high_done, 1)
                if u:
                    act.wait_ge(rest_done, u)
                    act.copy(part[(u - 1) % RING][:, 1, :], rest[(u - 1) % RING][:, :]).then_inc(mid_done, 1)
            for b in range(n_v):
                act.wait_ge(v_done, b + 1)
                act.copy(v_all[:, 2 * b:2 * b + 2, :].rearrange("p t r -> p (t r)"), ps_v[:, b % VRING, :])\
                   .then_inc(v_copied, 1)
            act.wait_ge(v_copied, n_v)

        @block.vector
        def _(dve):
            for u in range(len(units) + 1):
                if u < len(units):
                    dve.wait_ge(high_done, u + 1)
                    if u >= RING:
                        dve.wait_ge(low_done, u - RING + 1)
                    i = u % RING
                    dve.tensor_tensor(rest[i][:, :], ps[:, i, :], part[i][:, 0, :], ALU.subtract).then_inc(rest_done, 1)
                if u:
                    dve.wait_ge(mid_done, u)
                    i = (u - 1) % RING
                    dve.tensor_tensor(part[i][:, 2, :], rest[i][:, :], part[i][:, 1, :],
                                      ALU.subtract).then_inc(low_done, 1)

        @block.sync
        def _(sp):
            for u, (which, half, c) in enumerate(units):
                sp.wait_ge(low_done, u + 1)
                dst = (parts_q, parts_k)[which]
                sp.dma_start(dst[:, half * P:(half + 1) * P, c * BANK:(c + 1) * BANK].rearrange("a r n -> r a n"),
                             part[u % RING][:, :, :]).then_inc(part_out[u % RING], 16)
            for i in range(RING):
                sp.wait_ge(part_out[i], 16 * (len(units) // RING))


def qkv_rope_phase(nc, prefix, sh, xnT, w, cos_dram, sin_dram, parts_q, parts_k, v_all):
    with ExitStack() as ctx:
        sc = Scope(nc, ctx, prefix)
        RING, PRING = 3, 2
        cos = sc.sb("cos", [P, N])
        sin = sc.sb("sin", [P, N])
        part = [sc.sb(f"part{i}", [P, 3, BANK], BF16) for i in range(RING)]
        with_cos = [sc.sb(f"with_cos{i}", [P, BANK]) for i in range(RING)]
        with_sin = [sc.sb(f"with_sin{i}", [P, BANK]) for i in range(RING)]
        rotated = [sc.sb(f"rotated{i}", [P, BANK]) for i in range(RING)]
        rest = [sc.sb(f"rest{i}", [P, BANK]) for i in range(RING)]
        ps = sc.ps("ps", [P, PRING, 2, BANK])
        ps_v = sc.ps("ps_v", [P, NC4, BANK])
        table_in = sc.sem("table_in")
        proj_done = sc.sem("proj_done")
        v_done, v_copied = sc.sem("v_done"), sc.sem("v_copied")
        table_used = sc.sem("table_used")
        rot_done = sc.sem("rot_done")
        high_done, mid_done = sc.sem("high_done"), sc.sem("mid_done")
        rest_done, low_done = sc.sem("rest_done"), sc.sem("low_done")
        part_out = [sc.sem(f"part_out{i}") for i in range(RING)]
        units = [(which, c) for c in range(NC4) for which in range(2)]
        U = len(units)
        block = ctx.enter_context(nc.Block())

        @block.tensor
        def _(pe):
            for u, (which, c) in enumerate(units):
                if u >= PRING:
                    pe.wait_ge(table_used, u - PRING + 1)
                for i in range(2):
                    last = pe.matmul(ps[:, u % PRING, i, :], w["qkv"][:, which, i, :], xnT[:, c * BANK:(c + 1) * BANK],
                                     start=True, stop=True)
                last.then_inc(proj_done, 1)
            for t in range(NT):
                last = pe.matmul(ps_v[:, t // 4, (t % 4) * P:(t % 4 + 1) * P], xnT[:, t * P:(t + 1) * P], w["v"][:, :],
                                 start=True, stop=True)
                last.then_inc(v_done, 1)

        @block.vector
        def _(dve):
            dve.wait_ge(table_in, 32)
            for u in range(U + 2):
                if u < U:
                    which, c = units[u]
                    i, cols = u % RING, slice(c * BANK, (c + 1) * BANK)
                    dve.wait_ge(proj_done, u + 1)
                    if u >= RING:
                        dve.wait_ge(low_done, u - RING + 1)
                    dve.tensor_tensor(with_cos[i][:, :], ps[:, u % PRING, 0, :], cos[:, cols], ALU.mult)
                    dve.tensor_tensor(with_sin[i][:, :], ps[:, u % PRING, 1, :], sin[:, cols], ALU.mult)\
                       .then_inc(table_used, 1)
                if 1 <= u <= U:
                    i = (u - 1) % RING
                    dve.wait_ge(high_done, u)
                    dve.tensor_tensor(rest[i][:, :], rotated[i][:, :], part[i][:, 0, :], ALU.subtract)\
                       .then_inc(rest_done, 1)
                if u < U:
                    dve.wait_ge(table_used, u + 1)
                    i = u % RING
                    dve.tensor_tensor(rotated[i][:, :], with_cos[i][:, :], with_sin[i][:, :], ALU.add)\
                       .then_inc(rot_done, 1)
                if u >= 2:
                    i = (u - 2) % RING
                    dve.wait_ge(mid_done, u - 1)
                    dve.tensor_tensor(part[i][:, 2, :], rest[i][:, :], part[i][:, 1, :], ALU.subtract)\
                       .then_inc(low_done, 1)

        @block.scalar
        def _(act):
            for u in range(U + 1):
                if u < U:
                    i = u % RING
                    act.wait_ge(rot_done, u + 1)
                    if u >= RING:
                        act.wait_ge(part_out[i], 16 * (u // RING))
                    act.copy(part[i][:, 0, :], rotated[i][:, :]).then_inc(high_done, 1)
                if u:
                    i = (u - 1) % RING
                    act.wait_ge(rest_done, u)
                    act.copy(part[i][:, 1, :], rest[i][:, :]).then_inc(mid_done, 1)
            for c in range(NC4):
                act.wait_ge(v_done, 4 * (c + 1))
                act.copy(v_all[:, 4 * c:4 * c + 4, :].rearrange("p t r -> p (t r)"), ps_v[:, c, :]).then_inc(v_copied, 1)
            act.wait_ge(v_copied, NC4)

        @block.sync
        def _(sp):
            sp.dma_start(cos[:, :], cos_dram).then_inc(table_in, 16)
            sp.dma_start(sin[:, :], sin_dram).then_inc(table_in, 16)
            for u, (which, c) in enumerate(units):
                sp.wait_ge(low_done, u + 1)
                dst = (parts_q, parts_k)[which]
                sp.dma_start(dst[:, :, c * BANK:(c + 1) * BANK].rearrange("a r n -> r a n"),
                             part[u % RING][:, :, :]).then_inc(part_out[u % RING], 16)
            for i in range(RING):
                sp.wait_ge(part_out[i], 16 * len([u for u in range(U) if u % RING == i]))


def attn_out_phase(nc, prefix, sh, attn_tok, w_o, x_sb, ident):
    with ExitStack() as ctx:
        sc = Scope(nc, ctx, prefix)
        RH = sh.RH
        attT = [sc.sb(f"attT{i}", [P, RH, BANK]) for i in range(2)]
        ps_t = sc.ps("ps_t", [P, 2, RH, BANK])
        ps_y = sc.ps("ps_y", [P, 2, BANK])
        tp_done, t_copied, y_done, x_done = sc.sem("tp_done"), sc.sem("t_copied"), sc.sem("y_done"), sc.sem("x_done")
        block = ctx.enter_context(nc.Block())

        @block.tensor
        def _(pe):
            for c in range(NC4 + 1):
                if c < NC4:
                    if c >= 2:
                        pe.wait_ge(t_copied, c - 1)
                    for i in range(4):
                        for r in range(RH):
                            last = pe.transpose(ps_t[:, c % 2, r, i * P:(i + 1) * P],
                                                attn_tok[:, 4 * c + i, r * P:(r + 1) * P], ident[:, :])
                    last.then_inc(tp_done, 1)
                if c:
                    pe.wait_ge(t_copied, c)
                    if c >= 3:
                        pe.wait_ge(x_done, c - 2)
                    for i in range(4):
                        for r in range(RH):
                            last = pe.matmul(ps_y[:, (c - 1) % 2, i * P:(i + 1) * P],
                                             attT[(c - 1) % 2][:, r, i * P:(i + 1) * P], w_o[:, r, :],
                                             start=(r == 0), stop=(r == RH - 1))
                    last.then_inc(y_done, 1)

        @block.scalar
        def _(act):
            for c in range(NC4):
                act.wait_ge(tp_done, c + 1)
                if c >= 2:
                    act.wait_ge(y_done, c - 1)
                act.copy(attT[c % 2][:, :, :], ps_t[:, c % 2, :, :]).then_inc(t_copied, 1)

        @block.vector
        def _(dve):
            for c in range(NC4):
                dve.wait_ge(y_done, c + 1)
                xs = x_sb[:, 4 * c:4 * c + 4, :].rearrange("p t d -> p (t d)")
                dve.tensor_tensor(xs, xs, ps_y[:, c % 2, :], ALU.add).then_inc(x_done, 1)
            dve.wait_ge(x_done, NC4)


class MoeShape:

    def __init__(self, experts, top, hidden):
        self.E, self.K, self.F = experts, top, hidden
        most = (N * top + experts * (P - 1)) // P
        self.TILES = -(-most // 4) * 4


def routing_phase(nc, prefix, ms, xnT, w_r, bias_dram, softmax, place, weight, expert_row, ident, before, ones_bf):
    E, K, TILES = ms.E, ms.K, ms.TILES
    with ExitStack() as ctx:
        sc = Scope(nc, ctx, prefix)
        bias = sc.sb("bias", [P, E])
        logits = sc.sb("logits", [P, NT, E])
        score = sc.sb("score", [P, NT, E])
        best = sc.sb("best", [P, NT, 8])
        best_at = sc.sb("best_at", [P, NT, 8], U32)
        at_f = sc.sb("at_f", [P, NT, K])
        iota_e = sc.sb("iota_e", [P, NT, E])
        iota_p = sc.sb("iota_p", [P, 1])
        onehot = sc.sb("onehot", [P, K, NT, E])
        taken = sc.sb("taken", [P, NT, E], BF16)
        stat = sc.sb("stat", [P, NT])
        inv = sc.sb("inv", [P, NT])
        first = sc.sb("first", [P, E, NT])
        upto = sc.sb("upto", [P, E, NT])
        count = sc.sb("count", [P, E, NT])
        ones_e = sc.sb("ones_e", [P, E])
        count_i = sc.sb("count_i", [P, E], I32)
        tiles_i = sc.sb("tiles_i", [P, E], I32)
        tiles_f = sc.sb("tiles_f", [P, E])
        tile_end = sc.sb("tile_end", [P, E])
        start = sc.sb("start", [P, E])
        rank = sc.sb("rank", [P, NT, E])
        picked = sc.sb("picked", [P, K, NT, E])
        place_f = sc.sb("place_f", [P, K, NT])
        le = sc.sb("le", [P, E])
        of_tile = sc.sb("of_tile", [P, 1])
        ps_l = sc.ps("ps_l", [P, NT, E])
        ps_b = sc.ps("ps_b", [P, NT, E])
        ps_c = sc.ps("ps_c", [P, NT, E])
        ps_e = sc.ps("ps_e", [1, P])
        bias_in, consts = sc.sem("bias_in"), sc.sem("consts")
        logits_done = sc.sem("logits_done")
        exp_done, shifted = sc.sem("exp_done"), sc.sem("shifted")
        taken_done, counted = sc.sem("taken_done"), sc.sem("counted")
        tile_done, row_done = sc.sem("tile_done"), sc.sem("row_done")
        chain = sc.sem("chain")
        block = ctx.enter_context(nc.Block())
        per_token = lambda a: a.unsqueeze(2).to_broadcast([P, NT, E])

        @block.sync
        def _(sp):
            sp.dma_start(bias[:, :], bias_dram.partition_broadcast(P)).then_inc(bias_in, 16)
            sp.wait_ge(bias_in, 16)

        @block.gpsimd
        def _(pool):
            pool.iota(iota_e[:, :, :], pattern=[[0, NT], [1, E]], base=0, channel_multiplier=0,
                      allow_small_or_imprecise_dtypes=True)
            pool.iota(iota_p[:, :], pattern=[[0, 1]], base=0, channel_multiplier=1,
                      allow_small_or_imprecise_dtypes=True)
            pool.memset(ones_e[:, :], 1.0)
            pool.memset(first[:, :, :], 1.0).then_inc(consts, 1)
            pool.wait_ge(consts, 1)
            pool.memset(first[:, :, 0:1], 0.0).then_inc(consts, 1)

        @block.tensor
        def _(pe):
            for t in range(NT):
                last = pe.matmul(ps_l[:, t, :], xnT[:, t * P:(t + 1) * P], w_r[:, :], start=True, stop=True)
            last.then_inc(logits_done, 1)
            pe.wait_ge(taken_done, 1)
            pe.matmul(ps_b[:, :, :].rearrange("p t e -> p (t e)"), before[:, :], taken[:, :, :].rearrange("p t e -> p (t e)"),
                      start=True, stop=True)
            pe.matmul(ps_c[:, :, :].rearrange("p t e -> p (t e)"), ones_bf[:, :], taken[:, :, :].rearrange("p t e -> p (t e)"),
                      start=True, stop=True).then_inc(counted, 1)
            pe.wait_ge(tile_done, 1)
            pe.matmul(ps_e[:, :], of_tile[:, :], ident[:, :], start=True, stop=True).then_inc(row_done, 1)

        if softmax:
            @block.scalar
            def _(act):
                act.wait_ge(shifted, 1)
                act.activation(score[:, :, :], logits[:, :, :], ACT.Exp).then_inc(exp_done, 1)

        @block.vector
        def _(dve):
            steps = [0]

            def then(ins):
                steps[0] += 1
                ins.then_inc(chain, 1)
                dve.wait_ge(chain, steps[0])

            dve.wait_ge(bias_in, 16)
            dve.wait_ge(consts, 2)
            dve.wait_ge(logits_done, 1)
            then(dve.tensor_tensor(logits[:, :, :], ps_l[:, :, :], bias[:, :].unsqueeze(1).to_broadcast([P, NT, E]), ALU.add))
            ranked = logits
            if softmax:
                then(dve.tensor_reduce(stat[:, :], logits[:, :, :], AX.X, ALU.max))
                dve.tensor_tensor(logits[:, :, :], logits[:, :, :], per_token(stat[:, :]), ALU.subtract).then_inc(shifted, 1)
                dve.wait_ge(exp_done, 1)
                then(dve.tensor_reduce(stat[:, :], score[:, :, :], AX.X, ALU.add))
                then(dve.reciprocal(inv[:, :], stat[:, :]))
                then(dve.tensor_tensor(score[:, :, :], score[:, :, :], per_token(inv[:, :]), ALU.mult))
                ranked = score
            for t in range(NT):
                last = dve.max(best[:, t, :], ranked[:, t, :])
            then(last)
            for t in range(NT):
                last = dve.max_index(best_at[:, t, :], best[:, t, :], ranked[:, t, :])
            then(last)
            if softmax:
                then(dve.tensor_reduce(stat[:, :], best[:, :, 0:K], AX.X, ALU.add))
                then(dve.tensor_scalar(stat[:, :], stat[:, :], 1e-12, None, ALU.max))
                then(dve.reciprocal(inv[:, :], stat[:, :]))
                then(dve.tensor_scalar(inv[:, :], inv[:, :], 0.5, None, ALU.mult))
                dve.tensor_tensor(weight[:, :, :], best[:, :, 0:K], inv[:, :].unsqueeze(2).to_broadcast([P, NT, K]), ALU.mult)
            then(dve.tensor_copy(at_f[:, :, :], best_at[:, :, 0:K]))
            for k in range(K):
                last = dve.tensor_tensor(onehot[:, k, :, :], iota_e[:, :, :], per_token(at_f[:, :, k]), ALU.is_equal)
            then(last)
            total = onehot[:, 0, :, :]
            if K == 1:
                dve.tensor_copy(taken[:, :, :], total).then_inc(taken_done, 1)
            else:
                then(dve.tensor_tensor(picked[:, 0, :, :], onehot[:, 0, :, :], onehot[:, 1, :, :], ALU.add))
                then(dve.tensor_tensor(picked[:, 1, :, :], onehot[:, 2, :, :], onehot[:, 3, :, :], ALU.add))
                dve.tensor_tensor(taken[:, :, :], picked[:, 0, :, :], picked[:, 1, :, :], ALU.add).then_inc(taken_done, 1)
            dve.wait_ge(counted, 1)
            then(dve.tensor_copy(count[:, :, :].rearrange("p e t -> p t e"), ps_c[:, :, :]))
            then(dve.tensor_tensor_scan(upto[:, :, :].rearrange("p e t -> p (e t)"), first[:, :, :].rearrange("p e t -> p (e t)"),
                                        count[:, :, :].rearrange("p e t -> p (e t)"), 0.0, ALU.mult, ALU.add))
            then(dve.tensor_scalar(count_i[:, :], upto[:, :, NT - 1], float(P - 1), None, ALU.add))
            then(dve.tensor_scalar(tiles_i[:, :], count_i[:, :], P.bit_length() - 1, None, ALU.logical_shift_right))
            then(dve.tensor_copy(tiles_f[:, :], tiles_i[:, :]))
            then(dve.tensor_tensor_scan(tile_end[:, :], ones_e[:, :], tiles_f[:, :], 0.0, ALU.mult, ALU.add))
            then(dve.tensor_scalar(le[:, :], tile_end[:, :], iota_p[:, 0:1], None, ALU.is_le))
            then(dve.tensor_reduce(of_tile[:, :], le[:, :], AX.X, ALU.add))
            dve.tensor_scalar(of_tile[:, :], of_tile[:, :], float(E - 1), None, ALU.min).then_inc(tile_done, 1)
            then(dve.tensor_tensor(start[:, :], tile_end[:, :], tiles_f[:, :], ALU.subtract))
            then(dve.tensor_scalar(start[:, :], start[:, :], float(P), None, ALU.mult))
            then(dve.tensor_tensor(rank[:, :, :], upto[:, :, :].rearrange("p e t -> p t e"),
                                   count[:, :, :].rearrange("p e t -> p t e"), ALU.subtract))
            then(dve.tensor_tensor(rank[:, :, :], rank[:, :, :], start[:, :].unsqueeze(1).to_broadcast([P, NT, E]), ALU.add))
            then(dve.tensor_tensor(rank[:, :, :], rank[:, :, :], ps_b[:, :, :], ALU.add))
            for k in range(K):
                last = dve.tensor_tensor(picked[:, k, :, :], onehot[:, k, :, :], rank[:, :, :], ALU.mult)
            then(last)
            then(dve.tensor_reduce(place_f[:, :, :], picked[:, :, :, :], AX.X, ALU.add))
            then(dve.tensor_copy(place[:, :, :], place_f[:, :, :]))
            dve.wait_ge(row_done, 1)
            then(dve.tensor_copy(expert_row[:, :], ps_e[0:1, 0:TILES]))



def dispatch_phase(nc, prefix, ms, xn, xnT, place, x_dram, shared, x_sb):
    K = ms.K
    with ExitStack() as ctx:
        sc = Scope(nc, ctx, prefix)
        rows_out = sc.sem("rows_out")
        block_sems = {}
        if shared:
            FS = 4
            act_gate = [sc.sb(f"act_gate{i}", [P, BANK]) for i in range(2)]
            hidden = [sc.sb(f"hidden{i}", [P, FS, BANK]) for i in range(2)]
            ps_g = sc.ps("ps_g", [P, 2, BANK])
            ps_u = sc.ps("ps_u", [P, 2, BANK])
            ps_y = sc.ps("ps_y", [P, 2, BANK])
            gu_done = sc.sem("gu_done")
            silu_done = sc.sem("silu_done")
            hid_done = sc.sem("hid_done")
            y_done, x_done = sc.sem("y_done"), sc.sem("x_done")
        block = ctx.enter_context(nc.Block())

        @block.gpsimd
        def _(pool):
            for t in range(NT):
                for k in range(K):
                    pool.indirect_dma_start(x_dram, bass.IndirectOffsetOnAxis(ap=place[:, k, t:t + 1], axis=0),
                                            xn[:, t, :], None).then_inc(rows_out, 16)
            pool.wait_ge(rows_out, 16 * NT * K)

        if not shared:
            return

        @block.tensor
        def _(pe):
            def down(c):
                pe.wait_ge(hid_done, FS * (c + 1))
                if c >= 2:
                    pe.wait_ge(x_done, c - 1)
                for i in range(4):
                    for f in range(FS):
                        last = pe.matmul(ps_y[:, c % 2, i * P:(i + 1) * P], hidden[c % 2][:, f, i * P:(i + 1) * P],
                                         shared["down"][:, f, :], start=(f == 0), stop=(f == FS - 1))
                last.then_inc(y_done, 1)

            for c in range(NC4):
                for f in range(FS):
                    n = c * FS + f
                    if n >= 2:
                        pe.wait_ge(hid_done, n - 1)
                    cols = slice(c * BANK, (c + 1) * BANK)
                    pe.matmul(ps_g[:, n % 2, :], shared["gate"][:, f * P:(f + 1) * P], xnT[:, cols], start=True, stop=True)
                    pe.matmul(ps_u[:, n % 2, :], shared["up"][:, f * P:(f + 1) * P], xnT[:, cols],
                              start=True, stop=True).then_inc(gu_done, 1)
                    if f == 1 and c:
                        down(c - 1)
            down(NC4 - 1)

        @block.scalar
        def _(act):
            for n in range(NC4 * FS):
                act.wait_ge(gu_done, n + 1)
                if n >= 2:
                    act.wait_ge(hid_done, n - 1)
                act.activation(act_gate[n % 2][:, :], ps_g[:, n % 2, :], ACT.Silu).then_inc(silu_done, 1)

        @block.vector
        def _(dve):
            def add(c):
                dve.wait_ge(y_done, c + 1)
                xs = x_sb[:, 4 * c:4 * c + 4, :].rearrange("p t d -> p (t d)")
                dve.scalar_tensor_tensor(xs, ps_y[:, c % 2, :], 0.5, xs, ALU.mult, ALU.add).then_inc(x_done, 1)

            for n in range(NC4 * FS):
                c, f = n // FS, n % FS
                dve.wait_ge(silu_done, n + 1)
                if c >= 2 and f == 0:
                    dve.wait_ge(y_done, c - 1)
                dve.tensor_tensor(hidden[c % 2][:, f, :], ps_u[:, n % 2, :], act_gate[n % 2][:, :], ALU.mult)\
                   .then_inc(hid_done, 1)
                if f == 2 and c:
                    add(c - 1)
            add(NC4 - 1)
            dve.wait_ge(x_done, NC4)


def combine_phase(nc, prefix, ms, place, weight, y_dram, x_sb):
    K, RING = ms.K, 16
    with ExitStack() as ctx:
        sc = Scope(nc, ctx, prefix)
        got = sc.sb("got", [P, RING, D])
        row_in = [sc.sem(f"row_in{i}") for i in range(RING)]
        added = sc.sem("added")
        block = ctx.enter_context(nc.Block())

        @block.gpsimd
        def _(pool):
            for n in range(NT * K):
                t, k = n // K, n % K
                if n >= RING:
                    pool.wait_ge(added, n - RING + 1)
                pool.indirect_dma_start(got[:, n % RING, :], None, y_dram,
                                        bass.IndirectOffsetOnAxis(ap=place[:, k, t:t + 1], axis=0))\
                    .then_inc(row_in[n % RING], 16)

        @block.vector
        def _(dve):
            for n in range(NT * K):
                t, k = n // K, n % K
                dve.wait_ge(row_in[n % RING], 16 * (n // RING + 1))
                if k:
                    dve.wait_ge(added, n)
                w = weight[:, t, k:k + 1] if K > 1 else 0.5
                dve.scalar_tensor_tensor(x_sb[:, t, :], got[:, n % RING, :], w, x_sb[:, t, :], ALU.mult, ALU.add)\
                   .then_inc(added, 1)
            dve.wait_ge(added, NT * K)


def load_experts(eng, nc, expert_row, first, count):
    _, values = nc.values_load_multi_w_load_instructions(
        expert_row[0:1, bass.ds(first, count)], [eng.engine],
        skip_runtime_bounds_check_because="routing clamps every tile's expert to 0 .. E - 1")
    return values


def swiglu_experts_phase(nc, prefix, ms, w, expert_row, x_dram, y_dram, ident):
    GROUPS = ms.TILES // 4
    SIZE = 3 * P
    with ExitStack() as ctx:
        sc = Scope(nc, ctx, prefix)
        x_in = [sc.sb(f"x_in{i}", [P, 4, D]) for i in range(2)]
        xT = [sc.sb(f"xT{i}", [P, BANK]) for i in range(2)]
        wt = [sc.sb(f"wt{i}", [P, 4, SIZE]) for i in range(4)]
        act_gate = [sc.sb(f"act_gate{i}", [P, BANK]) for i in range(2)]
        hidden = [sc.sb(f"hidden{i}", [P, BANK]) for i in range(2)]
        y = [sc.sb(f"y{i}", [P, 4, D]) for i in range(2)]
        ps_t = sc.ps("ps_t", [P, 2, BANK])
        ps_g = sc.ps("ps_g", [P, 2, BANK])
        ps_u = sc.ps("ps_u", [P, 2, BANK])
        ps_y = sc.ps("ps_y", [P, 2, BANK])
        loaded = [sc.sem(f"loaded{i}") for i in range(2)]
        stored = [sc.sem(f"stored{i}") for i in range(2)]
        t_done = sc.sem("t_done")
        gu_done = sc.sem("gu_done")
        y_done = sc.sem("y_done")
        xT_done = sc.sem("xT_done")
        silu_done = sc.sem("silu_done")
        y_copied = sc.sem("y_copied")
        staged = sc.sem("staged")
        hid_done = sc.sem("hid_done")
        block = ctx.enter_context(nc.Block())
        x_g = x_dram.rearrange("(g i p) d -> g p i d", i=4, p=P)
        y_g = y_dram.rearrange("(g i p) d -> g p i d", i=4, p=P)

        def run_bodies(eng, one, after=0):
            for g in range(4):
                one(g, g, g // 2)
            with eng.Fori(1, GROUPS // 4 - 1) as i:
                for m in range(4):
                    one(i * 4 + m, m, i * 2 + m // 2)
            for g in range(GROUPS - 4, GROUPS + after):
                one(g, g % 4, g // 2)

        def there(g, ahead):
            return type(g) is not int or 0 <= g + ahead < GROUPS

        @block.sync
        def _(sp):
            def load(g, par):
                sp.dma_start(x_in[par][:, :, :], x_g[bass.ds(g, 1), :, :, :].rearrange("o p i d -> (o p) i d"))\
                  .then_inc(loaded[par], 16)

            def store(g, par):
                sp.wait_ge(y_copied, g + 3)
                sp.dma_start(y_g[bass.ds(g, 1), :, :, :].rearrange("o p i d -> (o p) i d"), y[par][:, :, :])\
                  .then_inc(stored[par], 16)

            load(0, 0)
            load(1, 1)

            def one(g, m, half):
                if there(g, 2):
                    sp.wait_ge(t_done, g + 1)
                    load(g + 2, m % 2)
                if there(g, -3):
                    store(g - 3, (m + 1) % 2)

            run_bodies(sp, one, after=3)
            for par in range(2):
                sp.wait_ge(stored[par], 16 * (GROUPS // 2))

        @block.tensor
        def _(pe):
            def transposes(g, par, uses):
                pe.wait_ge(loaded[par], uses * 16 + 16)
                pe.wait_ge(xT_done, g + 1)
                for i in range(4):
                    last = pe.transpose(ps_t[:, par, i * P:(i + 1) * P], x_in[par][:, i, :], ident[:, :])
                last.then_inc(t_done, 1)

            def gate_up(g, m):
                par = m % 2
                pe.wait_ge(xT_done, g + 3)
                pe.wait_ge(staged, g + 1)
                pe.wait_ge(hid_done, g + 1)
                for i in range(4):
                    cols = slice(i * P, (i + 1) * P)
                    pe.matmul(ps_g[:, par, cols], wt[m][:, i, 0:P], xT[par][:, cols], start=True, stop=True)
                    last = pe.matmul(ps_u[:, par, cols], wt[m][:, i, P:2 * P], xT[par][:, cols], start=True, stop=True)
                last.then_inc(gu_done, 1)

            def down(g, m):
                par = m % 2
                pe.wait_ge(hid_done, g + 3)
                pe.wait_ge(y_copied, g + 1)
                for i in range(4):
                    cols = slice(i * P, (i + 1) * P)
                    last = pe.matmul(ps_y[:, par, cols], hidden[par][:, cols], wt[m][:, i, 2 * P:SIZE], start=True, stop=True)
                last.then_inc(y_done, 1)

            pe.sem_inc(gu_done, 2)
            pe.sem_inc(y_done, 2)
            transposes(0, 0, 0)
            transposes(1, 1, 0)
            gate_up(0, 0)

            def one(g, m, half):
                if there(g, 2):
                    transposes(g + 2, m % 2, half + 1)
                if there(g, 1):
                    gate_up(g + 1, (m + 1) % 4)
                down(g, m)

            run_bodies(pe, one)

        @block.scalar
        def _(act):
            act.sem_inc(xT_done, 2)
            act.sem_inc(y_copied, 2)

            def copy_xT(g, par):
                act.wait_ge(t_done, g + 1)
                act.wait_ge(gu_done, g + 1)
                act.copy(xT[par][:, :], ps_t[:, par, :]).then_inc(xT_done, 1)

            def silu(g, par):
                act.wait_ge(gu_done, g + 3)
                act.wait_ge(hid_done, g + 1)
                act.activation(act_gate[par][:, :], ps_g[:, par, :], ACT.Silu).then_inc(silu_done, 1)

            def copy_y(g, par, uses):
                act.wait_ge(y_done, g + 3)
                if not (type(uses) is int and uses == 0):
                    act.wait_ge(stored[par], uses * 16)
                act.copy(y[par][:, :, :].rearrange("p i d -> p (i d)"), ps_y[:, par, :]).then_inc(y_copied, 1)

            copy_xT(0, 0)
            copy_xT(1, 1)
            silu(0, 0)

            def one(g, m, half):
                if there(g, -1):
                    copy_y(g - 1, (m + 1) % 2, half - (m + 1) % 2)
                if there(g, 2):
                    copy_xT(g + 2, m % 2)
                if there(g, 1):
                    silu(g + 1, (m + 1) % 2)

            run_bodies(act, one, after=1)

        @block.vector
        def _(dve):
            dve.sem_inc(hid_done, 2)

            def stage(g, m, experts):
                if not (type(g) is int and g < 4):
                    dve.wait_ge(y_done, g - 1)
                for i, e in enumerate(experts):
                    last = dve.tensor_copy(wt[m][:, i, :], w["experts"][:, bass.ds(e * SIZE, SIZE)])
                last.then_inc(staged, 1)

            def product(g, par):
                dve.wait_ge(silu_done, g + 1)
                dve.wait_ge(y_done, g + 1)
                dve.tensor_tensor(hidden[par][:, :], ps_u[:, par, :], act_gate[par][:, :], ALU.mult)\
                   .then_inc(hid_done, 1)

            def one(g, m, experts):
                product(g, m % 2)
                if experts:
                    stage(g + 3, (m + 3) % 4, experts)

            e = load_experts(dve, nc, expert_row, 0, 28)
            for g in range(3):
                stage(g, g, e[4 * g:4 * g + 4])
            for g in range(4):
                one(g, g, e[4 * g + 12:4 * g + 16])
            with dve.Fori(1, GROUPS // 4 - 1) as i:
                e = load_experts(dve, nc, expert_row, i * 16 + 12, 16)
                for m in range(4):
                    one(i * 4 + m, m, e[4 * m:4 * m + 4])
            e = load_experts(dve, nc, expert_row, 4 * (GROUPS - 1), 4)
            for g in range(GROUPS - 4, GROUPS):
                one(g, g % 4, e if g == GROUPS - 4 else None)


def gelu_experts_phase(nc, prefix, ms, w, expert_row, x_dram, y_dram, ident):
    TILES, F1, F2 = ms.TILES, 4, 2
    SIZE1 = F1 * P + F1
    SIZE2 = F1 * F2 * P + F2
    with ExitStack() as ctx:
        sc = Scope(nc, ctx, prefix)
        x_in = [sc.sb(f"x_in{i}", [P, D]) for i in range(2)]
        xT = [sc.sb(f"xT{i}", [P, P]) for i in range(2)]
        w1 = [sc.sb(f"w1{i}", [P, SIZE1]) for i in range(2)]
        w2 = [sc.sb(f"w2{i}", [P, SIZE2]) for i in range(2)]
        w3 = [sc.sb(f"w3{i}", [P, F2, D]) for i in range(2)]
        b3 = [sc.sb(f"b3{i}", [1, D]) for i in range(2)]
        h1 = [sc.sb(f"h1{i}", [P, F1, P]) for i in range(2)]
        h2 = [sc.sb(f"h2{i}", [P, F2, P]) for i in range(2)]
        y = [sc.sb(f"y{i}", [P, D]) for i in range(2)]
        ones = sc.sb("ones", [1, P])
        ps_t = sc.ps("ps_t", [P, 2, BANK])
        ps_1 = sc.ps("ps_1", [P, 2, BANK])
        ps_2 = sc.ps("ps_2", [P, 2, BANK])
        ps_y = sc.ps("ps_y", [P, 2, BANK])
        loaded = [sc.sem(f"loaded{i}") for i in range(2)]
        stored = [sc.sem(f"stored{i}") for i in range(2)]
        ones_set = sc.sem("ones_set")
        t_done, h1_done, h2_done, y_done = (sc.sem(n) for n in ("t_done", "h1_done", "h2_done", "y_done"))
        xT_done, g1_done, g2_done = (sc.sem(n) for n in ("xT_done", "g1_done", "g2_done"))
        w1_staged, w2_staged, w3_staged = (sc.sem(n) for n in ("w1_staged", "w2_staged", "w3_staged"))
        y_copied = sc.sem("y_copied")
        block = ctx.enter_context(nc.Block())
        x_t = x_dram.rearrange("(t p) d -> t p d", p=P)
        y_t = y_dram.rearrange("(t p) d -> t p d", p=P)

        def run_bodies(eng, one, after=0):
            for t in range(4):
                one(t, t % 2, t // 2)
            with eng.Fori(2, TILES // 2 - 1) as i:
                for par in range(2):
                    one(i * 2 + par, par, i)
            for t in range(TILES - 2, TILES + after):
                one(t, t % 2, t // 2)

        def there(t, ahead):
            return type(t) is not int or 0 <= t + ahead < TILES

        @block.sync
        def _(sp):
            def load(t, par):
                sp.dma_start(x_in[par][:, :], x_t[bass.ds(t, 1), :, :].rearrange("o p d -> (o p) d")).then_inc(loaded[par], 16)

            def one(t, par, i):
                if there(t, -4):
                    sp.wait_ge(y_copied, t - 1)
                    sp.dma_start(y_t[bass.ds(t - 4, 1), :, :].rearrange("o p d -> (o p) d"), y[par][:, :])\
                      .then_inc(stored[par], 16)
                if there(t, 2):
                    sp.wait_ge(t_done, t + 1)
                    load(t + 2, par)

            load(0, 0)
            load(1, 1)
            run_bodies(sp, one, after=4)
            for par in range(2):
                sp.wait_ge(stored[par], 16 * (TILES // 2))

        @block.tensor
        def _(pe):
            def transpose(t, par, uses):
                pe.wait_ge(loaded[par], uses * 16 + 16)
                pe.wait_ge(xT_done, t + 1)
                pe.transpose(ps_t[:, par, 0:P], x_in[par][:, :], ident[:, :]).then_inc(t_done, 1)

            def first(t, par):
                pe.wait_ge(xT_done, t + 3)
                pe.wait_ge(w1_staged, t + 1)
                pe.wait_ge(g1_done, t * F1 + F1)
                for f in range(F1):
                    pe.matmul(ps_1[:, par, f * P:(f + 1) * P], w1[par][:, f * P:(f + 1) * P], xT[par][:, :],
                              start=True, stop=True).then_inc(h1_done, 1)

            def second(t, par):
                pe.wait_ge(w2_staged, t + 1)
                pe.wait_ge(g2_done, t * F2 + F2)
                for o in range(F2):
                    for f in range(F1):
                        if o == 0:
                            pe.wait_ge(g1_done, t * F1 + (2 * F1 + f + 1))
                        at = f * F2 * P + o * P
                        last = pe.matmul(ps_2[:, par, o * P:(o + 1) * P], w2[par][:, at:at + P], h1[par][:, f, :],
                                         start=(f == 0), stop=(f == F1 - 1))
                    last.then_inc(h2_done, 1)

            def third(t, par):
                pe.wait_ge(w3_staged, t + 1)
                pe.wait_ge(y_copied, t + 1)
                pe.matmul(ps_y[:, par, 0:D], ones[:, :], b3[par][:, :], start=True, stop=False)
                for f in range(F2):
                    pe.wait_ge(g2_done, t * F2 + (2 * F2 + f + 1))
                    last = pe.matmul(ps_y[:, par, 0:D], h2[par][:, f, :], w3[par][:, f, :],
                                     start=False, stop=(f == F2 - 1))
                last.then_inc(y_done, 1)

            def one(t, par, i):
                if there(t, 1):
                    first(t + 1, 1 - par)
                if there(t, 2):
                    transpose(t + 2, par, i + 1)
                if there(t, 0):
                    second(t, par)
                if there(t, -1):
                    third(t - 1, 1 - par)

            pe.sem_inc(h1_done, 2 * F1)
            pe.sem_inc(h2_done, 2 * F2)
            pe.sem_inc(y_done, 2)
            pe.wait_ge(ones_set, 1)
            transpose(0, 0, 0)
            transpose(1, 1, 0)
            first(0, 0)
            run_bodies(pe, one, after=1)

        @block.scalar
        def _(act):
            act.sem_inc(xT_done, 2)
            act.sem_inc(g1_done, 2 * F1)
            act.sem_inc(g2_done, 2 * F2)

            def copy_xT(t, par):
                act.wait_ge(t_done, t + 1)
                act.wait_ge(h1_done, t * F1 + F1)
                act.copy(xT[par][:, :], ps_t[:, par, 0:P]).then_inc(xT_done, 1)

            def gelu1(t, par):
                act.wait_ge(h2_done, t * F2 + F2)
                act.wait_ge(h1_done, t * F1 + 3 * F1)
                for f in range(F1):
                    act.activation(h1[par][:, f, :], ps_1[:, par, f * P:(f + 1) * P], ACT.Gelu,
                                   bias=w1[par][:, F1 * P + f:F1 * P + f + 1]).then_inc(g1_done, 1)

            def gelu2(t, par):
                act.wait_ge(y_done, t + 1)
                act.wait_ge(h2_done, t * F2 + 3 * F2)
                for f in range(F2):
                    at = F1 * F2 * P + f
                    act.activation(h2[par][:, f, :], ps_2[:, par, f * P:(f + 1) * P], ACT.Gelu,
                                   bias=w2[par][:, at:at + 1]).then_inc(g2_done, 1)

            def one(t, par, i):
                if there(t, 1):
                    gelu1(t + 1, 1 - par)
                if there(t, 2):
                    copy_xT(t + 2, par)
                gelu2(t, par)

            copy_xT(0, 0)
            copy_xT(1, 1)
            gelu1(0, 0)
            run_bodies(act, one)

        @block.vector
        def _(dve):
            dve.memset(ones[:, :], 1.0).then_inc(ones_set, 1)
            dve.sem_inc(y_copied, 2)

            def stage1(t, par, e):
                dve.wait_ge(g1_done, t * F1 + F1)
                dve.tensor_copy(w1[par][:, :], w["w1"][:, bass.ds(e * SIZE1, SIZE1)]).then_inc(w1_staged, 1)

            def stage2(t, par, e):
                dve.wait_ge(g2_done, t * F2 + F2)
                dve.tensor_copy(w2[par][:, :], w["w2"][:, bass.ds(e * SIZE2, SIZE2)]).then_inc(w2_staged, 1)

            def stage3(t, par, e):
                dve.wait_ge(y_done, t + 1)
                dve.tensor_copy(b3[par][:, :], w["b3"][:, bass.ds(e * D, D)])
                dve.tensor_copy(w3[par][:, :, :].rearrange("p f d -> p (f d)"),
                                w["w3"][:, bass.ds(e * F2 * D, F2 * D)]).then_inc(w3_staged, 1)

            def copy_y(t, par, uses):
                dve.wait_ge(y_done, t + 3)
                if not (type(uses) is int and uses == 0):
                    dve.wait_ge(stored[par], uses * 16)
                dve.tensor_copy(y[par][:, :], ps_y[:, par, 0:D]).then_inc(y_copied, 1)

            def one(t, par, i, experts):
                if there(t, 2):
                    stage1(t + 2, par, experts[2])
                if there(t, -2):
                    copy_y(t - 2, par, i - 1)
                if there(t, 1):
                    stage2(t + 1, 1 - par, experts[1])
                if there(t, 0):
                    stage3(t, par, experts[0])

            e = load_experts(dve, nc, expert_row, 0, 6)
            stage1(0, 0, e[0])
            stage1(1, 1, e[1])
            stage2(0, 0, e[0])
            for t in range(4):
                one(t, t % 2, t // 2, e[t:t + 3])
            with dve.Fori(2, TILES // 2 - 1) as i:
                e = load_experts(dve, nc, expert_row, i * 2, 4)
                for par in range(2):
                    one(i * 2 + par, par, i, e[par:par + 3])
            e = load_experts(dve, nc, expert_row, TILES - 2, 2)
            for t in range(TILES - 2, TILES + 2):
                one(t, t % 2, t // 2, e[t - (TILES - 2):])
            dve.wait_ge(y_copied, TILES + 2)



L0_ATTN = AttnShape(8, 32, 2)
L1_ATTN = AttnShape(16, 8, 1)
L0_MOE = MoeShape(8, 1, 512)
L1_MOE = MoeShape(32, 4, 128)


def moe_layer(nc, prefix, ms, w, x_sb, ident, before, ones_bf, x_dram, y_dram):
    clear_semaphores(nc)
    with ExitStack() as ctx:
        sc = Scope(nc, ctx, prefix)
        xn = sc.sb("xn", [P, NT, D])
        xnT = sc.sb("xnT", [P, N])
        place = sc.sb("place", [P, ms.K, NT], U32)
        weight = sc.sb("weight", [P, NT, ms.K])
        expert_row = sc.sb("expert_row", [1, ms.TILES], I32)
        softmax = ms.K > 1
        rows = slice(0, ms.TILES * P)
        layernorm_phase(nc, prefix + "n", x_sb, xn, xnT, ident)
        routing_phase(nc, prefix + "r", ms, xnT, w["router"], w["router_bias"], softmax, place, weight, expert_row,
                      ident, before, ones_bf)
        dispatch_phase(nc, prefix + "d", ms, xn, xnT, place, x_dram[rows, :], w.get("shared"), x_sb)
        experts = swiglu_experts_phase if softmax else gelu_experts_phase
        experts(nc, prefix + "e", ms, w, expert_row, x_dram[rows, :], y_dram[rows, :], ident)
        combine_phase(nc, prefix + "c", ms, place, weight, y_dram[rows, :], x_sb)


def load_phase(nc, prefix, pairs):
    with ExitStack() as ctx:
        arrived = Scope(nc, ctx, prefix).sem("arrived")
        block = ctx.enter_context(nc.Block())

        @block.sync
        def _(sp):
            for dst, src in pairs:
                sp.dma_start(dst, src).then_inc(arrived, 16)
            sp.wait_ge(arrived, 16 * len(pairs))


def build(nc, a, out, only=None):
    x_dram = nc.dram_tensor("x_by_expert", [L1_MOE.TILES * P, D], F32, kind="Internal").ap()
    y_dram = nc.dram_tensor("y_by_expert", [L1_MOE.TILES * P, D], F32, kind="Internal").ap()
    max_dram = nc.dram_tensor("max_rows", [2 * NT, P], BF16, kind="Internal").ap()
    parts = {}
    for n, sh in ((0, L0_ATTN), (1, L1_ATTN)):
        parts[n] = [nc.dram_tensor(f"parts_{s}{n}", [3, sh.R, N], BF16, kind="Internal").ap() for s in "qk"]
    do = lambda name: only is None or name in only
    Scope.used = []
    with ExitStack() as ctx:
        sc = Scope(nc, ctx, "all")
        x_sb = sc.sb("x", [P, NT, D])
        ident = sc.sb("ident", [P, P])
        ident_bf = sc.sb("ident_bf", [P, P], BF16)
        before = sc.sb("before", [P, P], BF16)
        ones_bf = sc.sb("ones_bf", [P, P], BF16)

        def constants():
            with ExitStack() as inner:
                s2 = Scope(nc, inner, "const")
                ZERO = 8
                zeros = s2.sb("zeros", [P, ZERO * D])
                arrived, filled, zero_out = s2.sem("arrived"), s2.sem("filled"), s2.sem("zero_out")
                made = s2.sem("made")
                block = inner.enter_context(nc.Block())
                n_zero = L1_MOE.TILES // ZERO

                @block.sync
                def _(sp):
                    sp.dma_start(x_sb[:, :, :], a["x"].rearrange("(t p) d -> p t d", p=P)).then_inc(arrived, 16)
                    sp.wait_ge(filled, 1)
                    for z in range(n_zero):
                        sp.dma_start(x_dram[z * ZERO * P:(z + 1) * ZERO * P, :].rearrange("(p i) d -> p (i d)", p=P),
                                     zeros[:, :]).then_inc(zero_out, 16)
                    sp.wait_ge(arrived, 16)
                    sp.wait_ge(zero_out, 16 * n_zero)

                @block.vector
                def _(dve):
                    dve.memset(zeros[:, :], 0.0).then_inc(filled, 1)

                @block.gpsimd
                def _(pool):
                    pool.memset(ident[:, :], 0.0)
                    pool.memset(ident_bf[:, :], 0.0)
                    pool.memset(ones_bf[:, :], 1.0)
                    pool.memset(before[:, :], 1.0).then_inc(made, 1)
                    pool.wait_ge(made, 1)
                    for m in (ident, ident_bf):
                        pool.affine_select(out=m[:, :], in_=m[:, :], compare_op=ALU.not_equal, fill=1.0, base=0,
                                           pattern=[[-1, P]], channel_multiplier=1)
                    pool.affine_select(out=before[:, :], in_=before[:, :], compare_op=ALU.is_gt, fill=0.0, base=0,
                                       pattern=[[1, P]], channel_multiplier=-1).then_inc(made, 1)
                    pool.wait_ge(made, 2)

        constants()

        def attention(prefix, n, sh, qkv, w_o, scale):
            clear_semaphores(nc)
            with ExitStack() as inner:
                s2 = Scope(nc, inner, prefix)
                v_all = s2.sb("v_all", [P, NT, sh.R])
                with ExitStack() as norm:
                    s3 = Scope(nc, norm, prefix + "n")
                    xn = s3.sb("xn", [P, NT, D])
                    xnT = s3.sb("xnT", [P, N])
                    layernorm_phase(nc, prefix + "l", x_sb, xn, xnT, ident)
                    qkv(prefix + "q", xnT, v_all)
                attn_tok = s2.sb("attn_tok", [P, NT, sh.R])
                scores_phase(nc, prefix + "s", sh, parts[n][0], parts[n][1], max_dram, v_all, attn_tok, ident, ident_bf, scale)
                attn_out_phase(nc, prefix + "o", sh, attn_tok, w_o, x_sb, ident)

        with ExitStack() as layer:
            s1 = Scope(nc, layer, "L0")
            w = {"w1": s1.sb("w1", [P, L0_MOE.E * 516]), "w2": s1.sb("w2", [P, L0_MOE.E * 1026]), "w3": s1.sb("w3", [P, L0_MOE.E * 2 * D]),
                 "b3": s1.sb("b3", [1, L0_MOE.E * D]), "router": s1.sb("router", [P, L0_MOE.E]),
                 "router_bias": a["L0_router_bias"]}
            aw = {"q": s1.sb("wq", [P, L0_ATTN.R]), "kv_down": s1.sb("kv_down", [P, 64]),
                  "k_up": s1.sb("k_up", [64, L0_ATTN.R]), "v_up": s1.sb("v_up", [64, L0_ATTN.R]),
                  "o": s1.sb("wo", [P, 2, D])}
            load_phase(nc, "L0w", [(w["router"][:, :], a["L0_router"]), (w["w1"][:, :], a["L0_w1"]), (w["w2"][:, :], a["L0_w2"]),
                                   (w["w3"][:, :], a["L0_w3"]), (w["b3"][:, :], a["L0_b3"]),
                                   (aw["q"][:, :], a["L0_wq"]), (aw["kv_down"][:, :], a["L0_kv_down"]),
                                   (aw["k_up"][:, :], a["L0_k_up"]), (aw["v_up"][:, :], a["L0_v_up"]),
                                   (aw["o"][:, :, :], a["L0_wo"].rearrange("(r p) d -> p r d", p=P))])
            moe = lambda p: moe_layer(nc, p, L0_MOE, w, x_sb, ident, before, ones_bf, x_dram, y_dram)
            if do("m1"):
                moe("m1")
            if do("a1"):
                attention("a1", 0, L0_ATTN, lambda p, xnT, v: qkv_latent_phase(nc, p, L0_ATTN, xnT, aw, *parts[0], v),
                          aw["o"], 32 ** -0.5)
            if do("m2"):
                moe("m2")
        with ExitStack() as layer:
            s1 = Scope(nc, layer, "L1")
            shared = {"gate": s1.sb("sgate", [P, 4 * P]), "up": s1.sb("sup", [P, 4 * P]), "down": s1.sb("sdown", [P, 4, D])}
            w = {"experts": s1.sb("experts", [P, L1_MOE.E * 3 * P]),
                 "router": s1.sb("router", [P, L1_MOE.E]), "router_bias": a["L1_router_bias"], "shared": shared}
            aw = {"qkv": s1.sb("wqkv", [P, 2, 2, P]), "v": s1.sb("wv", [P, P]), "o": s1.sb("wo", [P, 1, D])}
            load_phase(nc, "L1w", [(w["router"][:, :], a["L1_router"]), (w["experts"][:, :], a["L1_experts"]),
                                   (shared["gate"][:, :], a["L1_sgate"]),
                                   (shared["up"][:, :], a["L1_sup"]),
                                   (shared["down"][:, :, :], a["L1_sdown"].rearrange("(f p) d -> p f d", p=P)),
                                   (aw["qkv"][:, :, :, :].rearrange("p a b c -> p (a b c)"), a["L1_wqk"]),
                                   (aw["v"][:, :], a["L1_wv"]), (aw["o"][:, 0, :], a["L1_wo"])])
            moe = lambda p: moe_layer(nc, p, L1_MOE, w, x_sb, ident, before, ones_bf, x_dram, y_dram)
            if do("m3"):
                moe("m3")
            if do("a2"):
                attention("a2", 1, L1_ATTN,
                          lambda p, xnT, v: qkv_rope_phase(nc, p, L1_ATTN, xnT, aw, a["cos"], a["sin"], *parts[1], v),
                          aw["o"], 8 ** -0.5)
            if do("m4"):
                moe("m4")
        with ExitStack() as last:
            stored = Scope(nc, last, "out").sem("stored")
            block = last.enter_context(nc.Block())

            @block.sync
            def _(sp):
                sp.dma_start(out.rearrange("(t p) d -> p t d", p=P), x_sb[:, :, :]).then_inc(stored, 16)
                sp.wait_ge(stored, 16)


def lay_out(i):
    f = lambda v: np.ascontiguousarray(np.asarray(v))
    i = {k: np.asarray(v) for k, v in i.items()}
    a = {"x": f(i["L0_attn_x"].reshape(N, D))}
    a["L0_router"] = f(i["L0_ffn_Wr"])
    a["L0_router_bias"] = f(i["L0_ffn_br"])
    w1 = i["L0_ffn_W1"].transpose(1, 0, 2)
    w2 = i["L0_ffn_W2"].reshape(8, 4, P, 256).transpose(2, 0, 1, 3).reshape(P, 8, 1024)
    b1 = i["L0_ffn_b1"].reshape(8, 4, P).transpose(2, 0, 1)
    b2 = i["L0_ffn_b2"].reshape(8, 2, P).transpose(2, 0, 1)
    a["L0_w1"] = f(np.concatenate([w1, b1], axis=2).reshape(P, -1))
    a["L0_w2"] = f(np.concatenate([w2, b2], axis=2).reshape(P, -1))
    a["L0_w3"] = f(i["L0_ffn_W3"].reshape(8, 2, P, D).transpose(2, 0, 1, 3).reshape(P, -1))
    a["L0_b3"] = f(i["L0_ffn_b3"].reshape(1, -1))
    a["L0_wq"] = f(i["L0_attn_Wq"].T)
    a["L0_kv_down"] = f(i["L0_attn_Wkv_down"].T)
    a["L0_k_up"] = f(i["L0_attn_Wk_up"].T)
    a["L0_v_up"] = f(i["L0_attn_Wv_up"].T)
    a["L0_wo"] = f(i["L0_attn_Wo"].T)
    a["L1_router"] = f(i["L1_ffn_router_w"].T)
    a["L1_router_bias"] = f(i["L1_ffn_router_bias"])
    gate, up = i["L1_ffn_gate_w"].transpose(2, 0, 1), i["L1_ffn_up_w"].transpose(2, 0, 1)
    down = i["L1_ffn_down_w"].transpose(2, 0, 1)
    a["L1_experts"] = f(np.concatenate([gate, up, down], axis=2).reshape(P, -1))
    a["L1_sgate"] = f(i["L1_ffn_sgate_w"].T)
    a["L1_sup"] = f(i["L1_ffn_sup_w"].T)
    a["L1_sdown"] = f(i["L1_ffn_sdown_w"].T)
    qkv = i["L1_attn_Wqkv"].reshape(P, 3, 16, 2, 4)
    a["L1_wqk"] = f(np.stack([qkv[:, :2], qkv[:, :2, :, ::-1]], axis=2).reshape(P, -1))
    a["L1_wv"] = f(qkv[:, 2].reshape(P, P))
    a["L1_wo"] = f(i["L1_attn_Wo"])
    inv_freq = (1.0 / 10000.0 ** (np.arange(0, 8, 2, dtype=np.float32) / np.float32(8))).astype(np.float32)
    angle = np.outer(np.arange(N, dtype=np.float32), inv_freq).astype(np.float32).T
    a["cos"] = f(np.tile(np.cos(angle), (32, 1)).astype(np.float32))
    a["sin"] = f(np.tile(np.concatenate([-np.sin(angle), np.sin(angle)]), (16, 1)).astype(np.float32))
    return a


def kernel(**inputs):
    import numpy as _np
    import concourse.bacc as _bacc
    from concourse import mybir as _mybir
    from concourse.bass_utils import run_bass_kernel_spmd as _run

    nc = _bacc.Bacc("TRN2", target_bir_lowering=False, num_devices=1)
    arrays = {f"in_{k}": v for k, v in lay_out(inputs).items()}
    aps = {k[3:]: nc.dram_tensor(k, v.shape, _mybir.dt.from_np(v.dtype), kind="ExternalInput").ap()
           for k, v in arrays.items()}
    out = nc.dram_tensor("out_0", (N, D), F32, kind="ExternalOutput").ap()
    build(nc, aps, out)
    r = _run(nc, [arrays], core_ids=[0])
    return r.results[0]["out_0"].reshape(1, N, D)
```

```python
import numpy as np
import concourse.bass as bass
from concourse import mybir
from contextlib import ExitStack

F32 = mybir.dt.float32
BF16 = mybir.dt.bfloat16
FP16 = mybir.dt.float16
I32 = mybir.dt.int32
U32 = mybir.dt.uint32
ALU = mybir.AluOpType
ACT = mybir.ActivationFunctionType
AX = mybir.AxisListType

P = 128
N = 2048
D = 128
NT = N // P
BANK = 512
NC4 = N // BANK
EPS = 1e-5


class Scope:

    used = []

    def __init__(self, nc, ctx, prefix):
        self.nc, self.ctx, self.prefix = nc, ctx, prefix

    def sb(self, name, shape, dt=F32):
        return self.ctx.enter_context(self.nc.sbuf_tensor(f"{self.prefix}_{name}", shape, dt))

    def ps(self, name, shape, dt=F32):
        return self.ctx.enter_context(self.nc.psum_tensor(f"{self.prefix}_{name}", shape, dt))

    def sem(self, name):
        s = self.nc.alloc_semaphore(f"{self.prefix}_{name}")
        Scope.used.append(s)
        return s


def clear_semaphores(nc):
    nc.clear_and_free_semaphores(Scope.used)
    nc.all_engine_barrier()
    Scope.used = []


class Arrivals:

    def __init__(self, nc):
        self.nc, self.sems, self.counts = nc, {}, {}

    def start(self, engine, name, dst, src):
        if name not in self.sems:
            self.sems[name] = self.nc.alloc_semaphore(f"arrived_{name}")
            self.counts[name] = 0
        self.counts[name] += 16
        engine.dma_start(dst, src).then_inc(self.sems[name], 16)

    def wait(self, engine, *names):
        for name in names:
            if name in self.sems:
                engine.wait_ge(self.sems[name], self.counts[name])


def layernorm_phase(nc, prefix, x_sb, xn, xnT, ident, sync_program=None):
    with ExitStack() as ctx:
        sc = Scope(nc, ctx, prefix)
        stats = sc.sb("stats", [P, NT, 6])
        meanvar = sc.sb("meanvar", [P, NT, 2])
        std = sc.sb("std", [P, NT])
        rstd = sc.sb("rstd", [P, NT])
        eps = sc.sb("eps", [P, 1])
        warm = sc.sb("warm", [P, 1])
        tp = sc.ps("tp", [P, NC4, BANK])
        stats_done = sc.sem("stats_done")
        var_done = sc.sem("var_done")
        std_done = sc.sem("std_done")
        rstd_done = sc.sem("rstd_done")
        xn_done = sc.sem("xn_done")
        tp_done = sc.sem("tp_done")
        eps_set = sc.sem("eps_set")
        copied = sc.sem("copied")
        block = ctx.enter_context(nc.Block())

        if sync_program:
            @block.sync
            def _(sp):
                sync_program(sp)

        @block.vector
        def _(dve):
            dve.memset(eps[:, :], EPS).then_inc(eps_set, 1)
            for t in range(NT):
                dve.bn_stats(stats[:, t, :], x_sb[:, t, :]).then_inc(stats_done, 1)
            for t in range(NT):
                dve.wait_ge(stats_done, t + 1)
                dve.bn_aggr(meanvar[:, t, :], stats[:, t, :]).then_inc(var_done, 1)
            dve.wait_ge(std_done, 1)
            dve.reciprocal(rstd[:, :], std[:, :]).then_inc(rstd_done, 1)
            dve.wait_ge(rstd_done, 1)
            for t in range(NT):
                dve.tensor_scalar(xn[:, t, :], x_sb[:, t, :], meanvar[:, t, 0:1], rstd[:, t:t + 1],
                                  ALU.subtract, ALU.mult).then_inc(xn_done, 1)

        @block.scalar
        def _(act):
            act.wait_ge(eps_set, 1)
            act.activation(warm[:, :], eps[:, :], ACT.Sqrt)
            act.wait_ge(var_done, NT)
            act.activation(std[:, :], meanvar[:, :, 1], ACT.Sqrt, bias=eps[:, 0:1]).then_inc(std_done, 1)
            for c in range(NC4):
                act.wait_ge(tp_done, 4 * (c + 1))
                act.copy(xnT[:, c * BANK:(c + 1) * BANK], tp[:, c, :]).then_inc(copied, 1)
            act.wait_ge(copied, NC4)

        @block.tensor
        def _(pe):
            for t in range(NT):
                pe.wait_ge(xn_done, t + 1)
                pe.transpose(tp[:, t // 4, (t % 4) * P:(t % 4 + 1) * P], xn[:, t, :], ident[:, :]).then_inc(tp_done, 1)


class AttnShape:

    def __init__(self, heads, hd, units):
        self.H, self.HD = heads, hd
        self.R = heads * hd
        self.RH = self.R // P
        self.U = units
        self.G = NC4 // units
        self.W = P // self.G
        self.STEPS = units * NT
        self.CH = self.STEPS * self.G
        self.MPS = 32 // self.STEPS
        self.terms = [(0, 0), (0, 1), (1, 0)] + ([(1, 1)] if hd * 4 <= 96 else [])
        self.ROW_MAX = 96
        self.SUM_MAX = 2.0 ** 15


def scales_phase(nc, prefix, sh, q_weights, k_weights, scale, ones, scales):
    weights = q_weights + k_weights
    W = len(weights)
    with ExitStack() as ctx:
        sc = Scope(nc, ctx, prefix)
        square = [sc.sb(f"square{i}", [P, w.shape[1]]) for i, w in enumerate(weights)]
        total = sc.sb("total", [P, W])
        norm = sc.sb("norm", [P, W])
        bound = sc.sb("bound", [P, 2])
        power = sc.sb("power", [P, 2])
        two_over = sc.sb("two_over", [P, 2])
        ps = sc.ps("ps", [P, W])
        step, summed, rooted = sc.sem("step"), sc.sem("summed"), sc.sem("rooted")
        block = ctx.enter_context(nc.Block())

        @block.tensor
        def _(pe):
            pe.wait_ge(step, W + 2)
            pe.matmul(ps[:, :], ones[:, :], total[:, :], start=True, stop=True).then_inc(summed, 1)

        @block.scalar
        def _(act):
            act.wait_ge(summed, 1)
            act.activation(norm[:, :], ps[:, :], ACT.Sqrt).then_inc(rooted, 1)

        @block.vector
        def _(dve):
            count = [0]

            def then(ins):
                count[0] += 1
                ins.then_inc(step, 1)
                dve.wait_ge(step, count[0])

            then(dve.memset(total[:, :], 0.0))
            for i, w in enumerate(weights):
                K = w.shape[0]
                then(dve.tensor_tensor(square[i][0:K, :], w, w, ALU.mult))
                last = dve.tensor_reduce(total[0:K, i:i + 1], square[i][0:K, :], AX.X, ALU.add)
            then(last)
            dve.wait_ge(rooted, 1)
            if len(k_weights) == 2:
                then(dve.tensor_tensor(norm[:, 1:2], norm[:, 1:2], norm[:, 2:3], ALU.mult))
            then(dve.tensor_scalar(bound[:, :], norm[:, 0:2], float(1.01 * D ** 0.5), float(2.0 ** -60), ALU.mult, ALU.max))
            EXPONENT = 0x7F800000
            as_int = lambda t: t[:, :].bitcast(I32)
            dve.tensor_scalar(as_int(power), as_int(bound), EXPONENT, None, ALU.bitwise_and)
            then(dve.tensor_scalar(as_int(two_over), as_int(bound), EXPONENT, EXPONENT, ALU.bitwise_and, ALU.bitwise_xor))
            dve.tensor_scalar(scales[:, 0:2], two_over[:, :], sh.SUM_MAX / 4, None, ALU.mult)
            then(dve.tensor_scalar(power[:, :], power[:, :], 2 / sh.SUM_MAX, None, ALU.mult))
            then(dve.scalar_tensor_tensor(scales[:, 2:3], power[:, 0:1], float(scale), power[:, 1:2], ALU.mult, ALU.mult))


def scores_phase(nc, prefix, sh, parts_q, parts_k, max_dram, v_all, attn_tok, ident, ident_h, exp_scale):
    H, HD, G, W, U, STEPS, CH = sh.H, sh.HD, sh.G, sh.W, sh.U, sh.STEPS, sh.CH
    MCH, SLOTS, SBANKS, SHIFT = 32, 8, 3, 3
    TURNS = MCH + 1 + U
    AHEAD = 12
    LEAD = MCH + AHEAD + 1
    with ExitStack() as ctx:
        sc = Scope(nc, ctx, prefix)
        ROW_MAX = sh.ROW_MAX
        TERM_ROWS = len(sh.terms) * HD
        LOAD = 2 * 16 * len(sh.terms)
        mq = [sc.sb(f"mq{i}", [P, N], FP16) for i in range(2)]
        mk = [sc.sb(f"mk{i}", [P, N], FP16) for i in range(2)]
        sq = [sc.sb(f"sq{i}", [P, N], FP16) for i in range(2)]
        sk = [sc.sb(f"sk{i}", [P, N], FP16) for i in range(2)]
        vh = [sc.sb(f"vh{i}", [P, NT, W]) for i in range(2)]
        probs = sc.sb("probs", [P, SLOTS, BANK])
        half_max = sc.sb("half_max", [P, 2, NT, 2])
        row_max = sc.sb("row_max", [P, NT])
        max_parts = sc.sb("max_parts", [P, 2, NT], FP16)
        max_rows = sc.sb("max_rows", [2 * NT, P], FP16)
        o_sb = [sc.sb(f"o_sb{i}", [P, BANK]) for i in range(2)]
        rsum = sc.sb("rsum", [P, G, 4])
        ps_m = sc.ps("ps_m", [P, 2, 2 * BANK])
        ps_s = sc.ps("ps_s", [P, SBANKS, BANK])
        ps_o = sc.ps("ps_o", [P, BANK])

        mcleared = sc.sem("mcleared")
        scleared = sc.sem("scleared")
        ones_set = sc.sem("ones_set")
        mstack_in = [sc.sem(f"mstack_in{i}") for i in range(2)]
        sstack_in = [sc.sem(f"sstack_in{i}") for i in range(2)]
        maxrow_out = sc.sem("maxrow_out")
        maxrow_in = [sc.sem(f"maxrow_in{i}") for i in range(2)]
        v_in = sc.sem("v_in")
        m_done = sc.sem("m_done")
        m_used = sc.sem("m_used")
        s_done = sc.sem("s_done")
        exp_done = sc.sem("exp_done")
        pv_done = sc.sem("pv_done")
        o_copied = sc.sem("o_copied")
        parts_done = sc.sem("parts_done")
        split_step = sc.sem("split_step")
        own_step = sc.sem("own_step")
        norm_step = sc.sem("norm_step")
        block = ctx.enter_context(nc.Block())
        FREE_STEPS = SLOTS // G

        def round_turns(with_next, with_second):
            out = []
            for r in range(STEPS):
                if U == 2 and r == NT + 2 - SHIFT:
                    out.append((r, "x", 0))
                if r == STEPS - 1:
                    out.append((r, "x", U - 1))
                for c in range(r * sh.MPS, (r + 1) * sh.MPS):
                    if c < MCH - AHEAD:
                        if with_next:
                            out.append((r, "m", (1, AHEAD + c)))
                    else:
                        if with_second:
                            out.append((r, "m", (2, c - (MCH - AHEAD))))
                        if with_next and c == MCH - AHEAD + 1:
                            out.append((r, "t", None))
            return out

        rounds = {"loop": round_turns(True, True), "second last": round_turns(True, False),
                  "last": round_turns(False, False)}
        assert len(rounds["loop"]) == TURNS

        def turn_base(h):
            if type(h) is int and h == H - 1:
                return LEAD + (H - 2) * TURNS + len(rounds["second last"])
            return LEAD + h * TURNS

        def slot(h, par, idx):
            return (turn_base(h if type(h) is int else par) + idx) % 2

        def t_turn(h):
            if type(h) is int and h == 0:
                return MCH + 2
            where = [k for _, k, _ in rounds["loop"] if k != "skip"]
            idx = where.index("t")
            if type(h) is int and h == H - 1:
                idx = [k for _, k, _ in rounds["second last"]].index("t")
            return turn_base(h - 1) + idx

        def run_rounds(eng, one):
            with eng.Fori(0, H // 2 - 1) as i:
                for par in range(2):
                    one(i * 2 + par, par, "loop", lambda ahead, par=par: i + (par + ahead) // 2 + 1)
            for h, kind in ((H - 2, "second last"), (H - 1, "last")):
                one(h, h % 2, kind, lambda ahead, h=h: (h + ahead) // 2 + 1)

        @block.sync
        def _(sp):
            def load(stack_q, stack_k, h, sem):
                for r, (a, b) in enumerate(sh.terms):
                    rows = slice(r * HD, (r + 1) * HD)
                    sp.dma_start(stack_q[rows, :], parts_q[a, bass.ds(h * HD, HD), :]).then_inc(sem, 16)
                    sp.dma_start(stack_k[rows, :], parts_k[b, bass.ds(h * HD, HD), :]).then_inc(sem, 16)

            def load_max_stack(h, par):
                load(mq[par], mk[par], h, mstack_in[par])

            def load_score_stack(h, par):
                load(sq[par], sk[par], h, sstack_in[par])

            def load_max_rows(h, par):
                sp.wait_ge(m_used, 2 + t_turn(h) + 1)
                sp.dma_start(max_dram, max_rows[:, :]).then_inc(maxrow_out, 16)
                sp.wait_ge(maxrow_out, (h + 1) * 16)
                sp.dma_start(sq[par][ROW_MAX:ROW_MAX + 2, :],
                             max_dram.rearrange("(a t) n -> a (t n)", a=2)).then_inc(maxrow_in[par], 16)

            if TERM_ROWS < ROW_MAX:
                sp.wait_ge(mcleared, 1)
            load_max_stack(0, 0)
            if TERM_ROWS < ROW_MAX:
                sp.wait_ge(scleared, 1)
            load_score_stack(0, 0)
            if TERM_ROWS < ROW_MAX:
                sp.wait_ge(mcleared, 2)
            load_max_stack(1, 1)
            if TERM_ROWS < ROW_MAX:
                sp.wait_ge(scleared, 2)
            load_max_rows(0, 0)

            def one(h, par, kind, loads):
                if kind != "last":
                    sp.wait_ge(s_done, h * CH + 1)
                    load_score_stack(h + 1, 1 - par)
                if kind == "loop":
                    sp.wait_ge(m_done, turn_base(h) + 1)
                    load_max_stack(h + 2, par)
                if kind != "last":
                    load_max_rows(h + 1, 1 - par)

            run_rounds(sp, one)

        @block.gpsimd
        def _(pool):
            for i in range(2):
                pool.memset(sk[i][ROW_MAX:ROW_MAX + 2, :], -sh.SUM_MAX).then_inc(own_step, 1)
                pool.wait_ge(own_step, 2 * i + 1)
                pool.memset(vh[i][:, :, HD:], 0.0).then_inc(own_step, 1)
                pool.wait_ge(own_step, 2 * i + 2)
                pool.memset(vh[i][:, :, HD:HD + 1], 1.0).then_inc(ones_set, 1)
                pool.wait_ge(ones_set, i + 1)

            def copy_v(h, par):
                pool.tensor_copy(vh[par][:, :, 0:HD], v_all[:, :, bass.ds(h * HD, HD)]).then_inc(v_in, 1)

            copy_v(0, 0)
            copy_v(1, 1)

            def one(h, par, kind, loads):
                if kind == "loop":
                    pool.wait_ge(pv_done, FREE_STEPS + (h + 1) * STEPS)
                    copy_v(h + 2, par)

            run_rounds(pool, one)

        @block.tensor
        def _(pe):
            def turn(number, slot, kind, what, h, par, loads):
                pe.wait_ge(m_used, number + 1)
                if kind == "m":
                    ahead, c = what
                    of = (par + ahead) % 2
                    if c == 0:
                        pe.wait_ge(mstack_in[of], loads(ahead) * LOAD)
                    t, half = c // 2, c % 2
                    for b in range(2):
                        col = (2 * half + b) * BANK
                        last = pe.matmul(ps_m[:, slot, b * BANK:(b + 1) * BANK],
                                         mq[of][0:ROW_MAX, t * P:(t + 1) * P],
                                         mk[of][0:ROW_MAX, col:col + BANK], start=True, stop=True)
                    last.then_inc(m_done, 1)
                elif kind == "t":
                    pe.wait_ge(parts_done, h + 2)
                    pe.transpose(ps_m[0:2 * NT, slot, 0:P // 2].bitcast(FP16),
                                 max_parts[:, :, :].rearrange("p a t -> p (a t)"), ident_h[:, :]).then_inc(m_done, 1)
                else:
                    pe.wait_ge(o_copied, h * U + what + 2)
                    src = o_sb[what if U == 2 else par]
                    for c in range(4):
                        last = pe.transpose(ps_m[:, slot, c * P:(c + 1) * P], src[:, c * P:(c + 1) * P], ident[:, :])
                    last.then_inc(m_done, 1)

            def score_chunk(h, par, q):
                s, g = q // G, q % G
                kt, col = s % NT, (s // NT * G + g) * BANK
                before = q - SBANKS if q >= SBANKS else max(c for c in range(CH) if c % SBANKS == q) - CH
                pe.wait_ge(exp_done, h * CH + (SBANKS + before + 1))
                pe.matmul(ps_s[:, q % SBANKS, :], sk[par][0:ROW_MAX + 2, kt * P:(kt + 1) * P],
                          sq[par][0:ROW_MAX + 2, col:col + BANK], start=True, stop=True).then_inc(s_done, 1)

            def probs_v(h, par, s):
                kt = s % NT
                pe.wait_ge(exp_done, h * CH + (SBANKS + G * (s + 1)))
                if kt == 0:
                    pe.wait_ge(o_copied, h * U + (s // NT + 1))
                if s == 0:
                    pe.wait_ge(v_in, h + 1)
                for g in range(G):
                    last = pe.matmul(ps_o[g * W:(g + 1) * W, :], vh[par][:, kt, :], probs[:, (s * G + g) % SLOTS, :],
                                     start=(kt == 0), stop=(kt == NT - 1))
                last.then_inc(pv_done, 1)

            def step(h, par, s, between, before, loads_of):
                if s == 0:
                    pe.wait_ge(sstack_in[par], loads_of * LOAD)
                    pe.wait_ge(maxrow_in[par], loads_of * 16)
                between = list(between)
                for g in range(G):
                    score_chunk(h, par, s * G + g)
                    if between:
                        between.pop(0)()
                while between:
                    between.pop(0)()
                if before:
                    probs_v(*before)

            pe.sem_inc(pv_done, FREE_STEPS)
            for c in range(MCH):
                turn(c, c % 2, "m", (0, c), 0, 0, lambda ahead: 1)
            n = MCH
            for c in range(AHEAD):
                turn(n, n % 2, "m", (1, c), 0, 0, lambda ahead: 1)
                n += 1
                if c == 1:
                    turn(n, n % 2, "t", None, -1, 0, None)
                    n += 1
            pe.wait_ge(ones_set, 2)
            for s in range(SHIFT):
                step(0, 0, s, [], (0, 0, s - 1) if s else None, 1)

            def one(h, par, kind, loads):
                mine = rounds[kind]
                for r in range(STEPS):
                    between = [lambda i=i, k=k, w=w: turn(turn_base(h) + i, slot(h, par, i), k, w, h, par, loads)
                               for i, (at, k, w) in enumerate(mine) if at == r]
                    s = r + SHIFT
                    if s < STEPS:
                        step(h, par, s, between, (h, par, s - 1), None)
                    elif kind != "last":
                        s -= STEPS
                        before = (h, par, STEPS - 1) if s == 0 else (h + 1, 1 - par, s - 1)
                        step(h + 1, 1 - par, s, between, before, loads(1))
                    else:
                        if s == STEPS:
                            probs_v(h, par, STEPS - 1)
                        for b in between:
                            b()

            run_rounds(pe, one)

        @block.scalar
        def _(act):
            act.sem_inc(exp_done, SBANKS)
            act.sem_inc(o_copied, 1)

            def exps(h, s):
                for q in range(s * G, (s + 1) * G):
                    act.wait_ge(s_done, h * CH + (q + 1))
                    if q == s * G:
                        act.wait_ge(pv_done, h * STEPS + (s + 1))
                    act.activation(probs[:, q % SLOTS, :], ps_s[:, q % SBANKS, :], ACT.Exp,
                                   scale=exp_scale).then_inc(exp_done, 1)

            def copy_out(h, par, unit):
                act.wait_ge(pv_done, h * STEPS + (FREE_STEPS + (unit + 1) * NT))
                act.copy(o_sb[unit if U == 2 else par][:, :], ps_o[:, :]).then_inc(o_copied, 1)

            def one(h, par, kind, loads):
                for s in range(1, STEPS):
                    exps(h, s)
                    if s == NT:
                        copy_out(h, par, 0)
                if kind != "last":
                    exps(h + 1, 0)
                copy_out(h, par, U - 1)

            exps(0, 0)
            run_rounds(act, one)

        @block.vector
        def _(dve):
            if TERM_ROWS < ROW_MAX:
                for i in range(2):
                    for stack in (mq[i], mk[i]):
                        last = dve.memset(stack[0:ROW_MAX, :].bitcast(U32), 0)
                    last.then_inc(mcleared, 1)
                    for stack in (sq[i], sk[i]):
                        last = dve.memset(stack[0:ROW_MAX, :].bitcast(U32), 0)
                    last.then_inc(scleared, 1)
            dve.sem_inc(m_used, 2)

            def read_max(number, slot, of, c):
                dve.wait_ge(m_done, number + 1)
                dve.reduce_max(half_max[:, of, c // 2, c % 2:c % 2 + 1], ps_m[:, slot, :], AX.X).then_inc(m_used, 1)

            def split_max(number, of, h):
                dve.wait_ge(m_used, number + 3)
                dve.tensor_tensor(row_max[:, :], half_max[:, of, :, 0], half_max[:, of, :, 1],
                                  ALU.max).then_inc(split_step, 1)
                dve.wait_ge(split_step, h * 2 + 1)
                dve.tensor_scalar(max_parts[:, 0, :], row_max[:, :], 1 / sh.SUM_MAX, None, ALU.mult).then_inc(split_step, 1)
                dve.wait_ge(split_step, h * 2 + 2)
                dve.scalar_tensor_tensor(max_parts[:, 1, :], row_max[:, :], 1 / sh.SUM_MAX, max_parts[:, 0, :],
                                         ALU.mult, ALU.subtract).then_inc(parts_done, 1)

            def read_rows(number, slot, h):
                dve.wait_ge(m_done, number + 1)
                if not (type(h) is int and h == 0):
                    dve.wait_ge(maxrow_out, h * 16)
                dve.tensor_copy(max_rows[:, :], ps_m[0:2 * NT, slot, 0:P // 2].bitcast(FP16)).then_inc(m_used, 1)

            def read_out(number, slot, unit, h):
                dve.wait_ge(m_done, number + 1)
                dve.wait_ge(m_used, number + 2)
                src = ps_m[:, slot, 0:BANK].rearrange("p (c g w) -> p g c w", c=4, g=G)
                dve.reciprocal(rsum[:, :, :], src[:, :, :, HD]).then_inc(norm_step, 1)
                dve.wait_ge(norm_step, h * U + (unit + 1))
                t0 = unit * G * 4
                for g in range(G):
                    dst = attn_tok[:, t0 + 4 * g:t0 + 4 * g + 4, bass.ds(h * HD, HD)]
                    last = dve.tensor_tensor(dst, src[:, g, :, 0:HD],
                                             rsum[:, g, :].unsqueeze(2).to_broadcast([P, 4, HD]), ALU.mult)
                last.then_inc(m_used, 1)

            for c in range(MCH):
                read_max(c, c % 2, 0, c)
            split_max(MCH - 1, 0, 0)
            n = MCH
            for c in range(AHEAD):
                read_max(n, n % 2, 1, c)
                n += 1
                if c == 1:
                    read_rows(n, n % 2, 0)
                    n += 1

            def one(h, par, kind, loads):
                base = turn_base(h)
                for idx, (_, k, what) in enumerate(rounds[kind]):
                    if k == "m":
                        ahead, c = what
                        read_max(base + idx, slot(h, par, idx), (par + ahead) % 2, c)
                        if c == MCH - 1:
                            split_max(base + idx, (par + ahead) % 2, h + ahead)
                    elif k == "t":
                        read_rows(base + idx, slot(h, par, idx), h + 1)
                    else:
                        read_out(base + idx, slot(h, par, idx), what, h)

            run_rounds(dve, one)
            dve.wait_ge(m_used, turn_base(H - 1) + len(rounds["last"]) + 2)

def qkv_latent_phase(nc, prefix, sh, xnT, w, parts_q, parts_k, v_all, scales):
    with ExitStack() as ctx:
        sc = Scope(nc, ctx, prefix)
        RANK = w["kv_down"].shape[1]
        RING, VRING = 4, 2
        latT = sc.sb("latT", [RANK, N])
        part = [sc.sb(f"part{i}", [P, 2, BANK], FP16) for i in range(RING)]
        ps = sc.ps("ps", [P, RING, BANK])
        ps_lat = sc.ps("ps_lat", [RANK, 2, BANK])
        ps_v = sc.ps("ps_v", [P, VRING, BANK])
        lat_done, lat_copied = sc.sem("lat_done"), sc.sem("lat_copied")
        proj_done = sc.sem("proj_done")
        v_done, v_copied = sc.sem("v_done"), sc.sem("v_copied")
        high_done, low_done = sc.sem("high_done"), sc.sem("low_done")
        part_out = [sc.sem(f"part_out{i}") for i in range(RING)]
        units = [(which, half, c) for which in (1, 0) for half in range(sh.RH) for c in range(NC4)]
        n_v = NT * sh.R // BANK
        block = ctx.enter_context(nc.Block())

        @block.tensor
        def _(pe):
            for c in range(NC4):
                if c >= 2:
                    pe.wait_ge(lat_copied, c - 1)
                pe.matmul(ps_lat[:, c % 2, :], w["kv_down"][:, :], xnT[:, c * BANK:(c + 1) * BANK],
                          start=True, stop=True).then_inc(lat_done, 1)
            for u, (which, half, c) in enumerate(units):
                if u >= RING:
                    pe.wait_ge(low_done, u - RING + 1)
                cols = slice(half * P, (half + 1) * P)
                if which == 0:
                    last = pe.matmul(ps[:, u % RING, :], w["q"][:, cols], xnT[:, c * BANK:(c + 1) * BANK],
                                     start=True, stop=True)
                else:
                    pe.wait_ge(lat_copied, c + 1)
                    last = pe.matmul(ps[:, u % RING, :], w["k_up"][:, cols], latT[:, c * BANK:(c + 1) * BANK],
                                     start=True, stop=True)
                last.then_inc(proj_done, 1)
            for b in range(n_v):
                if b >= VRING:
                    pe.wait_ge(v_copied, b - VRING + 1)
                for i in range(2):
                    t = 2 * b + i
                    last = pe.matmul(ps_v[:, b % VRING, i * sh.R:(i + 1) * sh.R], latT[:, t * P:(t + 1) * P],
                                     w["v_up"][:, :], start=True, stop=True)
                last.then_inc(v_done, 1)

        @block.scalar
        def _(act):
            for c in range(NC4):
                act.wait_ge(lat_done, c + 1)
                act.copy(latT[:, c * BANK:(c + 1) * BANK], ps_lat[:, c % 2, :]).then_inc(lat_copied, 1)
            for u, (which, half, c) in enumerate(units):
                act.wait_ge(proj_done, u + 1)
                if u >= RING:
                    act.wait_ge(part_out[u % RING], 16 * (u // RING))
                act.activation(part[u % RING][:, 0, :], ps[:, u % RING, :], ACT.Copy,
                               scale=scales[:, which:which + 1]).then_inc(high_done, 1)
            for b in range(n_v):
                act.wait_ge(v_done, b + 1)
                act.copy(v_all[:, 2 * b:2 * b + 2, :].rearrange("p t r -> p (t r)"), ps_v[:, b % VRING, :])\
                   .then_inc(v_copied, 1)
            act.wait_ge(v_copied, n_v)

        @block.vector
        def _(dve):
            for u, (which, half, c) in enumerate(units):
                i = u % RING
                dve.wait_ge(high_done, u + 1)
                dve.scalar_tensor_tensor(part[i][:, 1, :], ps[:, i, :], scales[:, which:which + 1], part[i][:, 0, :],
                                         ALU.mult, ALU.subtract).then_inc(low_done, 1)

        @block.sync
        def _(sp):
            for u, (which, half, c) in enumerate(units):
                sp.wait_ge(low_done, u + 1)
                dst = (parts_q, parts_k)[which]
                sp.dma_start(dst[:, half * P:(half + 1) * P, c * BANK:(c + 1) * BANK].rearrange("a r n -> r a n"),
                             part[u % RING][:, :, :]).then_inc(part_out[u % RING], 16)
            for i in range(RING):
                sp.wait_ge(part_out[i], 16 * (len(units) // RING))


def qkv_rope_phase(nc, prefix, sh, xnT, w, cos_dram, sin_dram, parts_q, parts_k, v_all, scales):
    with ExitStack() as ctx:
        sc = Scope(nc, ctx, prefix)
        RING, PRING = 3, 2
        cos = sc.sb("cos", [P, N])
        sin = sc.sb("sin", [P, N])
        part = [sc.sb(f"part{i}", [P, 2, BANK], FP16) for i in range(RING)]
        with_cos = [sc.sb(f"with_cos{i}", [P, BANK]) for i in range(RING)]
        with_sin = [sc.sb(f"with_sin{i}", [P, BANK]) for i in range(RING)]
        rotated = with_cos
        ps = sc.ps("ps", [P, PRING, 2, BANK])
        ps_v = sc.ps("ps_v", [P, NC4, BANK])
        table_in = sc.sem("table_in")
        proj_done = sc.sem("proj_done")
        v_done, v_copied = sc.sem("v_done"), sc.sem("v_copied")
        table_used = sc.sem("table_used")
        rot_done = sc.sem("rot_done")
        high_done, low_done = sc.sem("high_done"), sc.sem("low_done")
        part_out = [sc.sem(f"part_out{i}") for i in range(RING)]
        units = [(which, c) for c in range(NC4) for which in range(2)]
        U = len(units)
        block = ctx.enter_context(nc.Block())

        @block.tensor
        def _(pe):
            for u, (which, c) in enumerate(units):
                if u >= PRING:
                    pe.wait_ge(table_used, u - PRING + 1)
                for i in range(2):
                    last = pe.matmul(ps[:, u % PRING, i, :], w["qkv"][:, which, i, :], xnT[:, c * BANK:(c + 1) * BANK],
                                     start=True, stop=True)
                last.then_inc(proj_done, 1)
            for t in range(NT):
                last = pe.matmul(ps_v[:, t // 4, (t % 4) * P:(t % 4 + 1) * P], xnT[:, t * P:(t + 1) * P], w["v"][:, :],
                                 start=True, stop=True)
                last.then_inc(v_done, 1)

        @block.vector
        def _(dve):
            dve.wait_ge(table_in, 32)
            for u in range(U + 2):
                if u < U:
                    which, c = units[u]
                    i, cols = u % RING, slice(c * BANK, (c + 1) * BANK)
                    dve.wait_ge(proj_done, u + 1)
                    if u >= RING:
                        dve.wait_ge(low_done, u - RING + 1)
                    dve.tensor_tensor(with_cos[i][:, :], ps[:, u % PRING, 0, :], cos[:, cols], ALU.mult)
                    dve.tensor_tensor(with_sin[i][:, :], ps[:, u % PRING, 1, :], sin[:, cols], ALU.mult)\
                       .then_inc(table_used, 1)
                if u >= 2:
                    i, which = (u - 2) % RING, units[u - 2][0]
                    dve.wait_ge(high_done, u - 1)
                    dve.scalar_tensor_tensor(part[i][:, 1, :], rotated[i][:, :], scales[:, which:which + 1],
                                             part[i][:, 0, :], ALU.mult, ALU.subtract).then_inc(low_done, 1)
                if u < U:
                    dve.wait_ge(table_used, u + 1)
                    i = u % RING
                    dve.tensor_tensor(rotated[i][:, :], with_cos[i][:, :], with_sin[i][:, :], ALU.add)\
                       .then_inc(rot_done, 1)

        @block.scalar
        def _(act):
            for u, (which, c) in enumerate(units):
                i = u % RING
                act.wait_ge(rot_done, u + 1)
                if u >= RING:
                    act.wait_ge(part_out[i], 16 * (u // RING))
                act.activation(part[i][:, 0, :], rotated[i][:, :], ACT.Copy,
                               scale=scales[:, which:which + 1]).then_inc(high_done, 1)
            for c in range(NC4):
                act.wait_ge(v_done, 4 * (c + 1))
                act.copy(v_all[:, 4 * c:4 * c + 4, :].rearrange("p t r -> p (t r)"), ps_v[:, c, :]).then_inc(v_copied, 1)
            act.wait_ge(v_copied, NC4)

        @block.sync
        def _(sp):
            sp.dma_start(cos[:, :], cos_dram).then_inc(table_in, 16)
            sp.dma_start(sin[:, :], sin_dram).then_inc(table_in, 16)
            for u, (which, c) in enumerate(units):
                sp.wait_ge(low_done, u + 1)
                dst = (parts_q, parts_k)[which]
                sp.dma_start(dst[:, :, c * BANK:(c + 1) * BANK].rearrange("a r n -> r a n"),
                             part[u % RING][:, :, :]).then_inc(part_out[u % RING], 16)
            for i in range(RING):
                sp.wait_ge(part_out[i], 16 * len([u for u in range(U) if u % RING == i]))


def attn_out_phase(nc, prefix, sh, attn_tok, w_o, x_sb, ident):
    with ExitStack() as ctx:
        sc = Scope(nc, ctx, prefix)
        RH = sh.RH
        attT = [sc.sb(f"attT{i}", [P, RH, BANK]) for i in range(2)]
        ps_t = sc.ps("ps_t", [P, 2, RH, BANK])
        ps_y = sc.ps("ps_y", [P, 2, BANK])
        tp_done, t_copied, y_done, x_done = sc.sem("tp_done"), sc.sem("t_copied"), sc.sem("y_done"), sc.sem("x_done")
        block = ctx.enter_context(nc.Block())

        @block.tensor
        def _(pe):
            for c in range(NC4 + 1):
                if c < NC4:
                    if c >= 2:
                        pe.wait_ge(t_copied, c - 1)
                    for i in range(4):
                        for r in range(RH):
                            last = pe.transpose(ps_t[:, c % 2, r, i * P:(i + 1) * P],
                                                attn_tok[:, 4 * c + i, r * P:(r + 1) * P], ident[:, :])
                    last.then_inc(tp_done, 1)
                if c:
                    pe.wait_ge(t_copied, c)
                    if c >= 3:
                        pe.wait_ge(x_done, c - 2)
                    for i in range(4):
                        for r in range(RH):
                            last = pe.matmul(ps_y[:, (c - 1) % 2, i * P:(i + 1) * P],
                                             attT[(c - 1) % 2][:, r, i * P:(i + 1) * P], w_o[:, r, :],
                                             start=(r == 0), stop=(r == RH - 1))
                    last.then_inc(y_done, 1)

        @block.scalar
        def _(act):
            for c in range(NC4):
                act.wait_ge(tp_done, c + 1)
                if c >= 2:
                    act.wait_ge(y_done, c - 1)
                act.copy(attT[c % 2][:, :, :], ps_t[:, c % 2, :, :]).then_inc(t_copied, 1)

        @block.vector
        def _(dve):
            for c in range(NC4):
                dve.wait_ge(y_done, c + 1)
                xs = x_sb[:, 4 * c:4 * c + 4, :].rearrange("p t d -> p (t d)")
                dve.tensor_tensor(xs, xs, ps_y[:, c % 2, :], ALU.add).then_inc(x_done, 1)
            dve.wait_ge(x_done, NC4)


class MoeShape:

    def __init__(self, name, experts, top, hidden):
        self.name, self.E, self.K, self.F = name, experts, top, hidden
        most = (N * top + experts * (P - 1)) // P
        self.TILES = -(-most // 4) * 4


def routing_phase(nc, prefix, ms, xnT, w_r, bias, softmax, place, weight, expert_row, ident, before, ones_bf,
                  arrivals):
    E, K, TILES = ms.E, ms.K, ms.TILES
    with ExitStack() as ctx:
        sc = Scope(nc, ctx, prefix)
        logits = sc.sb("logits", [P, NT, E])
        score = sc.sb("score", [P, NT, E])
        best = sc.sb("best", [P, NT, 8])
        best_at = sc.sb("best_at", [P, NT, 8], U32)
        at_f = sc.sb("at_f", [P, NT, K])
        iota_e = sc.sb("iota_e", [P, NT, E])
        iota_p = sc.sb("iota_p", [P, 1])
        onehot = sc.sb("onehot", [P, K, NT, E])
        taken = sc.sb("taken", [P, NT, E], BF16)
        stat = sc.sb("stat", [P, NT])
        inv = sc.sb("inv", [P, NT])
        first = sc.sb("first", [P, E, NT])
        upto = sc.sb("upto", [P, E, NT])
        count = sc.sb("count", [P, E, NT])
        ones_e = sc.sb("ones_e", [P, E])
        count_i = sc.sb("count_i", [P, E], I32)
        tiles_i = sc.sb("tiles_i", [P, E], I32)
        tiles_f = sc.sb("tiles_f", [P, E])
        tile_end = sc.sb("tile_end", [P, E])
        start = sc.sb("start", [P, E])
        rank = sc.sb("rank", [P, NT, E])
        picked = sc.sb("picked", [P, K, NT, E])
        place_f = sc.sb("place_f", [P, K, NT])
        le = sc.sb("le", [P, E])
        of_tile = sc.sb("of_tile", [P, 1])
        ps_l = sc.ps("ps_l", [P, NT, E])
        ps_b = sc.ps("ps_b", [P, NT, E])
        ps_c = sc.ps("ps_c", [P, NT, E])
        ps_e = sc.ps("ps_e", [1, P])
        consts = sc.sem("consts")
        logits_done = sc.sem("logits_done")
        exp_done, shifted = sc.sem("exp_done"), sc.sem("shifted")
        taken_done, counted = sc.sem("taken_done"), sc.sem("counted")
        tile_done, row_done = sc.sem("tile_done"), sc.sem("row_done")
        chain = sc.sem("chain")
        block = ctx.enter_context(nc.Block())
        per_token = lambda a: a.unsqueeze(2).to_broadcast([P, NT, E])

        @block.sync
        def _(sp):
            arrivals.wait(sp, f"{ms.name}_zeros", f"{ms.name}_shared")

        @block.gpsimd
        def _(pool):
            pool.iota(iota_e[:, :, :], pattern=[[0, NT], [1, E]], base=0, channel_multiplier=0,
                      allow_small_or_imprecise_dtypes=True)
            pool.iota(iota_p[:, :], pattern=[[0, 1]], base=0, channel_multiplier=1,
                      allow_small_or_imprecise_dtypes=True)
            pool.memset(ones_e[:, :], 1.0)
            pool.memset(first[:, :, :], 1.0).then_inc(consts, 1)
            pool.wait_ge(consts, 1)
            pool.memset(first[:, :, 0:1], 0.0).then_inc(consts, 1)

        @block.tensor
        def _(pe):
            for t in range(NT):
                last = pe.matmul(ps_l[:, t, :], xnT[:, t * P:(t + 1) * P], w_r[:, :], start=True, stop=True)
            last.then_inc(logits_done, 1)
            pe.wait_ge(taken_done, 1)
            pe.matmul(ps_b[:, :, :].rearrange("p t e -> p (t e)"), before[:, :], taken[:, :, :].rearrange("p t e -> p (t e)"),
                      start=True, stop=True)
            pe.matmul(ps_c[:, :, :].rearrange("p t e -> p (t e)"), ones_bf[:, :], taken[:, :, :].rearrange("p t e -> p (t e)"),
                      start=True, stop=True).then_inc(counted, 1)
            pe.wait_ge(tile_done, 1)
            pe.matmul(ps_e[:, :], of_tile[:, :], ident[:, :], start=True, stop=True).then_inc(row_done, 1)

        if softmax:
            @block.scalar
            def _(act):
                act.wait_ge(shifted, 1)
                act.activation(score[:, :, :], logits[:, :, :], ACT.Exp).then_inc(exp_done, 1)

        @block.vector
        def _(dve):
            steps = [0]

            def then(ins):
                steps[0] += 1
                ins.then_inc(chain, 1)
                dve.wait_ge(chain, steps[0])

            dve.wait_ge(consts, 2)
            dve.wait_ge(logits_done, 1)
            then(dve.tensor_tensor(logits[:, :, :], ps_l[:, :, :], bias[:, :].unsqueeze(1).to_broadcast([P, NT, E]), ALU.add))
            ranked = logits
            if softmax:
                then(dve.tensor_reduce(stat[:, :], logits[:, :, :], AX.X, ALU.max))
                dve.tensor_tensor(logits[:, :, :], logits[:, :, :], per_token(stat[:, :]), ALU.subtract).then_inc(shifted, 1)
                dve.wait_ge(exp_done, 1)
                then(dve.tensor_reduce(stat[:, :], score[:, :, :], AX.X, ALU.add))
                then(dve.reciprocal(inv[:, :], stat[:, :]))
                then(dve.tensor_tensor(score[:, :, :], score[:, :, :], per_token(inv[:, :]), ALU.mult))
                ranked = score
            for t in range(NT):
                last = dve.max(best[:, t, :], ranked[:, t, :])
            then(last)
            for t in range(NT):
                last = dve.max_index(best_at[:, t, :], best[:, t, :], ranked[:, t, :])
            then(last)
            if softmax:
                then(dve.tensor_reduce(stat[:, :], best[:, :, 0:K], AX.X, ALU.add))
                then(dve.tensor_scalar(stat[:, :], stat[:, :], 1e-12, None, ALU.max))
                then(dve.reciprocal(inv[:, :], stat[:, :]))
                then(dve.tensor_scalar(inv[:, :], inv[:, :], 0.5, None, ALU.mult))
                dve.tensor_tensor(weight[:, :, :], best[:, :, 0:K], inv[:, :].unsqueeze(2).to_broadcast([P, NT, K]), ALU.mult)
            then(dve.tensor_copy(at_f[:, :, :], best_at[:, :, 0:K]))
            for k in range(K):
                last = dve.tensor_tensor(onehot[:, k, :, :], iota_e[:, :, :], per_token(at_f[:, :, k]), ALU.is_equal)
            then(last)
            total = onehot[:, 0, :, :]
            if K == 1:
                dve.tensor_copy(taken[:, :, :], total).then_inc(taken_done, 1)
            else:
                then(dve.tensor_tensor(picked[:, 0, :, :], onehot[:, 0, :, :], onehot[:, 1, :, :], ALU.add))
                then(dve.tensor_tensor(picked[:, 1, :, :], onehot[:, 2, :, :], onehot[:, 3, :, :], ALU.add))
                dve.tensor_tensor(taken[:, :, :], picked[:, 0, :, :], picked[:, 1, :, :], ALU.add).then_inc(taken_done, 1)
            dve.wait_ge(counted, 1)
            then(dve.tensor_copy(count[:, :, :].rearrange("p e t -> p t e"), ps_c[:, :, :]))
            then(dve.tensor_tensor_scan(upto[:, :, :].rearrange("p e t -> p (e t)"), first[:, :, :].rearrange("p e t -> p (e t)"),
                                        count[:, :, :].rearrange("p e t -> p (e t)"), 0.0, ALU.mult, ALU.add))
            then(dve.tensor_scalar(count_i[:, :], upto[:, :, NT - 1], float(P - 1), None, ALU.add))
            then(dve.tensor_scalar(tiles_i[:, :], count_i[:, :], P.bit_length() - 1, None, ALU.logical_shift_right))
            then(dve.tensor_copy(tiles_f[:, :], tiles_i[:, :]))
            then(dve.tensor_tensor_scan(tile_end[:, :], ones_e[:, :], tiles_f[:, :], 0.0, ALU.mult, ALU.add))
            then(dve.tensor_scalar(le[:, :], tile_end[:, :], iota_p[:, 0:1], None, ALU.is_le))
            then(dve.tensor_reduce(of_tile[:, :], le[:, :], AX.X, ALU.add))
            dve.tensor_scalar(of_tile[:, :], of_tile[:, :], float(E - 1), None, ALU.min).then_inc(tile_done, 1)
            then(dve.tensor_tensor(start[:, :], tile_end[:, :], tiles_f[:, :], ALU.subtract))
            then(dve.tensor_scalar(start[:, :], start[:, :], float(P), None, ALU.mult))
            then(dve.tensor_tensor(rank[:, :, :], upto[:, :, :].rearrange("p e t -> p t e"),
                                   count[:, :, :].rearrange("p e t -> p t e"), ALU.subtract))
            then(dve.tensor_tensor(rank[:, :, :], rank[:, :, :], start[:, :].unsqueeze(1).to_broadcast([P, NT, E]), ALU.add))
            then(dve.tensor_tensor(rank[:, :, :], rank[:, :, :], ps_b[:, :, :], ALU.add))
            for k in range(K):
                last = dve.tensor_tensor(picked[:, k, :, :], onehot[:, k, :, :], rank[:, :, :], ALU.mult)
            then(last)
            then(dve.tensor_reduce(place_f[:, :, :], picked[:, :, :, :], AX.X, ALU.add))
            then(dve.tensor_copy(place[:, :, :], place_f[:, :, :]))
            dve.wait_ge(row_done, 1)
            then(dve.tensor_copy(expert_row[:, :], ps_e[0:1, 0:TILES]))



def dispatch_phase(nc, prefix, ms, xn, xnT, place, x_dram, shared, x_sb, arrivals):
    K = ms.K
    with ExitStack() as ctx:
        sc = Scope(nc, ctx, prefix)
        rows_out = sc.sem("rows_out")
        block_sems = {}
        if shared:
            FS = 4
            act_gate = [sc.sb(f"act_gate{i}", [P, BANK]) for i in range(2)]
            hidden = [sc.sb(f"hidden{i}", [P, FS, BANK]) for i in range(2)]
            ps_g = sc.ps("ps_g", [P, 2, BANK])
            ps_u = sc.ps("ps_u", [P, 2, BANK])
            ps_y = sc.ps("ps_y", [P, 2, BANK])
            gu_done = sc.sem("gu_done")
            silu_done = sc.sem("silu_done")
            hid_done = sc.sem("hid_done")
            y_done, x_done = sc.sem("y_done"), sc.sem("x_done")
        block = ctx.enter_context(nc.Block())

        @block.sync
        def _(sp):
            arrivals.wait(sp, f"{ms.name}_experts")

        @block.gpsimd
        def _(pool):
            for t in range(NT):
                for k in range(K):
                    pool.indirect_dma_start(x_dram, bass.IndirectOffsetOnAxis(ap=place[:, k, t:t + 1], axis=0),
                                            xn[:, t, :], None).then_inc(rows_out, 16)
            pool.wait_ge(rows_out, 16 * NT * K)

        if not shared:
            return

        @block.tensor
        def _(pe):
            def down(c):
                pe.wait_ge(hid_done, FS * (c + 1))
                if c >= 2:
                    pe.wait_ge(x_done, c - 1)
                for i in range(4):
                    for f in range(FS):
                        last = pe.matmul(ps_y[:, c % 2, i * P:(i + 1) * P], hidden[c % 2][:, f, i * P:(i + 1) * P],
                                         shared["down"][:, f, :], start=(f == 0), stop=(f == FS - 1))
                last.then_inc(y_done, 1)

            for c in range(NC4):
                for f in range(FS):
                    n = c * FS + f
                    if n >= 2:
                        pe.wait_ge(hid_done, n - 1)
                    cols = slice(c * BANK, (c + 1) * BANK)
                    pe.matmul(ps_g[:, n % 2, :], shared["gate"][:, f * P:(f + 1) * P], xnT[:, cols], start=True, stop=True)
                    pe.matmul(ps_u[:, n % 2, :], shared["up"][:, f * P:(f + 1) * P], xnT[:, cols],
                              start=True, stop=True).then_inc(gu_done, 1)
                    if f == 1 and c:
                        down(c - 1)
            down(NC4 - 1)

        @block.scalar
        def _(act):
            for n in range(NC4 * FS):
                act.wait_ge(gu_done, n + 1)
                if n >= 2:
                    act.wait_ge(hid_done, n - 1)
                act.activation(act_gate[n % 2][:, :], ps_g[:, n % 2, :], ACT.Silu).then_inc(silu_done, 1)

        @block.vector
        def _(dve):
            def add(c):
                dve.wait_ge(y_done, c + 1)
                xs = x_sb[:, 4 * c:4 * c + 4, :].rearrange("p t d -> p (t d)")
                dve.scalar_tensor_tensor(xs, ps_y[:, c % 2, :], 0.5, xs, ALU.mult, ALU.add).then_inc(x_done, 1)

            for n in range(NC4 * FS):
                c, f = n // FS, n % FS
                dve.wait_ge(silu_done, n + 1)
                if c >= 2 and f == 0:
                    dve.wait_ge(y_done, c - 1)
                dve.tensor_tensor(hidden[c % 2][:, f, :], ps_u[:, n % 2, :], act_gate[n % 2][:, :], ALU.mult)\
                   .then_inc(hid_done, 1)
                if f == 2 and c:
                    add(c - 1)
            add(NC4 - 1)
            dve.wait_ge(x_done, NC4)


def combine_phase(nc, prefix, ms, place, weight, y_dram, x_sb):
    K, RING = ms.K, 16
    with ExitStack() as ctx:
        sc = Scope(nc, ctx, prefix)
        got = sc.sb("got", [P, RING, D])
        row_in = [sc.sem(f"row_in{i}") for i in range(RING)]
        added = sc.sem("added")
        block = ctx.enter_context(nc.Block())

        @block.gpsimd
        def _(pool):
            for n in range(NT * K):
                t, k = n // K, n % K
                if n >= RING:
                    pool.wait_ge(added, n - RING + 1)
                pool.indirect_dma_start(got[:, n % RING, :], None, y_dram,
                                        bass.IndirectOffsetOnAxis(ap=place[:, k, t:t + 1], axis=0))\
                    .then_inc(row_in[n % RING], 16)

        @block.vector
        def _(dve):
            for n in range(NT * K):
                t, k = n // K, n % K
                dve.wait_ge(row_in[n % RING], 16 * (n // RING + 1))
                if k:
                    dve.wait_ge(added, n)
                w = weight[:, t, k:k + 1] if K > 1 else 0.5
                dve.scalar_tensor_tensor(x_sb[:, t, :], got[:, n % RING, :], w, x_sb[:, t, :], ALU.mult, ALU.add)\
                   .then_inc(added, 1)
            dve.wait_ge(added, NT * K)


def load_experts(eng, nc, expert_row, first, count):
    _, values = nc.values_load_multi_w_load_instructions(
        expert_row[0:1, bass.ds(first, count)], [eng.engine],
        skip_runtime_bounds_check_because="routing clamps every tile's expert to 0 .. E - 1")
    return values


def swiglu_experts_phase(nc, prefix, ms, w, expert_row, x_dram, y_dram, ident):
    GROUPS = ms.TILES // 4
    SIZE = 3 * P
    with ExitStack() as ctx:
        sc = Scope(nc, ctx, prefix)
        x_in = [sc.sb(f"x_in{i}", [P, 4, D]) for i in range(2)]
        xT = [sc.sb(f"xT{i}", [P, BANK]) for i in range(2)]
        wt = [sc.sb(f"wt{i}", [P, 4, SIZE]) for i in range(4)]
        act_gate = [sc.sb(f"act_gate{i}", [P, BANK]) for i in range(2)]
        hidden = [sc.sb(f"hidden{i}", [P, BANK]) for i in range(2)]
        y = [sc.sb(f"y{i}", [P, 4, D]) for i in range(2)]
        ps_t = sc.ps("ps_t", [P, 2, BANK])
        ps_g = sc.ps("ps_g", [P, 2, BANK])
        ps_u = sc.ps("ps_u", [P, 2, BANK])
        ps_y = sc.ps("ps_y", [P, 2, BANK])
        loaded = [sc.sem(f"loaded{i}") for i in range(2)]
        stored = [sc.sem(f"stored{i}") for i in range(2)]
        t_done = sc.sem("t_done")
        gu_done = sc.sem("gu_done")
        y_done = sc.sem("y_done")
        xT_done = sc.sem("xT_done")
        silu_done = sc.sem("silu_done")
        y_copied = sc.sem("y_copied")
        staged = sc.sem("staged")
        hid_done = sc.sem("hid_done")
        block = ctx.enter_context(nc.Block())
        x_g = x_dram.rearrange("(g i p) d -> g p i d", i=4, p=P)
        y_g = y_dram.rearrange("(g i p) d -> g p i d", i=4, p=P)

        def run_bodies(eng, one, after=0):
            for g in range(4):
                one(g, g, g // 2)
            with eng.Fori(1, GROUPS // 4 - 1) as i:
                for m in range(4):
                    one(i * 4 + m, m, i * 2 + m // 2)
            for g in range(GROUPS - 4, GROUPS + after):
                one(g, g % 4, g // 2)

        def there(g, ahead):
            return type(g) is not int or 0 <= g + ahead < GROUPS

        @block.sync
        def _(sp):
            def load(g, par):
                sp.dma_start(x_in[par][:, :, :], x_g[bass.ds(g, 1), :, :, :].rearrange("o p i d -> (o p) i d"))\
                  .then_inc(loaded[par], 16)

            def store(g, par):
                sp.wait_ge(y_copied, g + 3)
                sp.dma_start(y_g[bass.ds(g, 1), :, :, :].rearrange("o p i d -> (o p) i d"), y[par][:, :, :])\
                  .then_inc(stored[par], 16)

            load(0, 0)
            load(1, 1)

            def one(g, m, half):
                if there(g, 2):
                    sp.wait_ge(t_done, g + 1)
                    load(g + 2, m % 2)
                if there(g, -3):
                    store(g - 3, (m + 1) % 2)

            run_bodies(sp, one, after=3)
            for par in range(2):
                sp.wait_ge(stored[par], 16 * (GROUPS // 2))

        @block.tensor
        def _(pe):
            def transposes(g, par, uses):
                pe.wait_ge(loaded[par], uses * 16 + 16)
                pe.wait_ge(xT_done, g + 1)
                for i in range(4):
                    last = pe.transpose(ps_t[:, par, i * P:(i + 1) * P], x_in[par][:, i, :], ident[:, :])
                last.then_inc(t_done, 1)

            def gate_up(g, m):
                par = m % 2
                pe.wait_ge(xT_done, g + 3)
                pe.wait_ge(staged, g + 1)
                pe.wait_ge(hid_done, g + 1)
                for i in range(4):
                    cols = slice(i * P, (i + 1) * P)
                    pe.matmul(ps_g[:, par, cols], wt[m][:, i, 0:P], xT[par][:, cols], start=True, stop=True)
                    last = pe.matmul(ps_u[:, par, cols], wt[m][:, i, P:2 * P], xT[par][:, cols], start=True, stop=True)
                last.then_inc(gu_done, 1)

            def down(g, m):
                par = m % 2
                pe.wait_ge(hid_done, g + 3)
                pe.wait_ge(y_copied, g + 1)
                for i in range(4):
                    cols = slice(i * P, (i + 1) * P)
                    last = pe.matmul(ps_y[:, par, cols], hidden[par][:, cols], wt[m][:, i, 2 * P:SIZE], start=True, stop=True)
                last.then_inc(y_done, 1)

            pe.sem_inc(gu_done, 2)
            pe.sem_inc(y_done, 2)
            transposes(0, 0, 0)
            transposes(1, 1, 0)
            gate_up(0, 0)

            def one(g, m, half):
                if there(g, 2):
                    transposes(g + 2, m % 2, half + 1)
                if there(g, 1):
                    gate_up(g + 1, (m + 1) % 4)
                down(g, m)

            run_bodies(pe, one)

        @block.scalar
        def _(act):
            act.sem_inc(xT_done, 2)
            act.sem_inc(y_copied, 2)

            def copy_xT(g, par):
                act.wait_ge(t_done, g + 1)
                act.wait_ge(gu_done, g + 1)
                act.copy(xT[par][:, :], ps_t[:, par, :]).then_inc(xT_done, 1)

            def silu(g, par):
                act.wait_ge(gu_done, g + 3)
                act.wait_ge(hid_done, g + 1)
                act.activation(act_gate[par][:, :], ps_g[:, par, :], ACT.Silu).then_inc(silu_done, 1)

            def copy_y(g, par, uses):
                act.wait_ge(y_done, g + 3)
                if not (type(uses) is int and uses == 0):
                    act.wait_ge(stored[par], uses * 16)
                act.copy(y[par][:, :, :].rearrange("p i d -> p (i d)"), ps_y[:, par, :]).then_inc(y_copied, 1)

            copy_xT(0, 0)
            copy_xT(1, 1)
            silu(0, 0)

            def one(g, m, half):
                if there(g, -1):
                    copy_y(g - 1, (m + 1) % 2, half - (m + 1) % 2)
                if there(g, 2):
                    copy_xT(g + 2, m % 2)
                if there(g, 1):
                    silu(g + 1, (m + 1) % 2)

            run_bodies(act, one, after=1)

        @block.vector
        def _(dve):
            dve.sem_inc(hid_done, 2)

            def stage(g, m, experts):
                if not (type(g) is int and g < 4):
                    dve.wait_ge(y_done, g - 1)
                for i, e in enumerate(experts):
                    last = dve.tensor_copy(wt[m][:, i, :], w["experts"][:, bass.ds(e * SIZE, SIZE)])
                last.then_inc(staged, 1)

            def product(g, par):
                dve.wait_ge(silu_done, g + 1)
                dve.wait_ge(y_done, g + 1)
                dve.tensor_tensor(hidden[par][:, :], ps_u[:, par, :], act_gate[par][:, :], ALU.mult)\
                   .then_inc(hid_done, 1)

            def one(g, m, experts):
                product(g, m % 2)
                if experts:
                    stage(g + 3, (m + 3) % 4, experts)

            e = load_experts(dve, nc, expert_row, 0, 28)
            for g in range(3):
                stage(g, g, e[4 * g:4 * g + 4])
            for g in range(4):
                one(g, g, e[4 * g + 12:4 * g + 16])
            with dve.Fori(1, GROUPS // 4 - 1) as i:
                e = load_experts(dve, nc, expert_row, i * 16 + 12, 16)
                for m in range(4):
                    one(i * 4 + m, m, e[4 * m:4 * m + 4])
            e = load_experts(dve, nc, expert_row, 4 * (GROUPS - 1), 4)
            for g in range(GROUPS - 4, GROUPS):
                one(g, g % 4, e if g == GROUPS - 4 else None)


def gelu_experts_phase(nc, prefix, ms, w, expert_row, x_dram, y_dram, ident):
    TILES, F1, F2 = ms.TILES, 4, 2
    SIZE1 = F1 * P + F1
    SIZE2 = F1 * F2 * P + F2
    with ExitStack() as ctx:
        sc = Scope(nc, ctx, prefix)
        x_in = [sc.sb(f"x_in{i}", [P, D]) for i in range(2)]
        xT = [sc.sb(f"xT{i}", [P, P]) for i in range(2)]
        w1 = [sc.sb(f"w1{i}", [P, SIZE1]) for i in range(2)]
        w2 = [sc.sb(f"w2{i}", [P, SIZE2]) for i in range(2)]
        w3 = [sc.sb(f"w3{i}", [P, F2, D]) for i in range(2)]
        b3 = [sc.sb(f"b3{i}", [1, D]) for i in range(2)]
        h1 = [sc.sb(f"h1{i}", [P, F1, P]) for i in range(2)]
        h2 = [sc.sb(f"h2{i}", [P, F2, P]) for i in range(2)]
        y = [sc.sb(f"y{i}", [P, D]) for i in range(2)]
        ones = sc.sb("ones", [1, P])
        ps_t = sc.ps("ps_t", [P, 2, BANK])
        ps_1 = sc.ps("ps_1", [P, 2, BANK])
        ps_2 = sc.ps("ps_2", [P, 2, BANK])
        ps_y = sc.ps("ps_y", [P, 2, BANK])
        loaded = [sc.sem(f"loaded{i}") for i in range(2)]
        stored = [sc.sem(f"stored{i}") for i in range(2)]
        ones_set = sc.sem("ones_set")
        t_done, h1_done, h2_done, y_done = (sc.sem(n) for n in ("t_done", "h1_done", "h2_done", "y_done"))
        xT_done, g1_done, g2_done = (sc.sem(n) for n in ("xT_done", "g1_done", "g2_done"))
        w1_staged, w2_staged, w3_staged = (sc.sem(n) for n in ("w1_staged", "w2_staged", "w3_staged"))
        y_copied = sc.sem("y_copied")
        block = ctx.enter_context(nc.Block())
        x_t = x_dram.rearrange("(t p) d -> t p d", p=P)
        y_t = y_dram.rearrange("(t p) d -> t p d", p=P)

        def run_bodies(eng, one, after=0):
            for t in range(4):
                one(t, t % 2, t // 2)
            with eng.Fori(2, TILES // 2 - 1) as i:
                for par in range(2):
                    one(i * 2 + par, par, i)
            for t in range(TILES - 2, TILES + after):
                one(t, t % 2, t // 2)

        def there(t, ahead):
            return type(t) is not int or 0 <= t + ahead < TILES

        @block.sync
        def _(sp):
            def load(t, par):
                sp.dma_start(x_in[par][:, :], x_t[bass.ds(t, 1), :, :].rearrange("o p d -> (o p) d")).then_inc(loaded[par], 16)

            def one(t, par, i):
                if there(t, -4):
                    sp.wait_ge(y_copied, t - 1)
                    sp.dma_start(y_t[bass.ds(t - 4, 1), :, :].rearrange("o p d -> (o p) d"), y[par][:, :])\
                      .then_inc(stored[par], 16)
                if there(t, 2):
                    sp.wait_ge(t_done, t + 1)
                    load(t + 2, par)

            load(0, 0)
            load(1, 1)
            run_bodies(sp, one, after=4)
            for par in range(2):
                sp.wait_ge(stored[par], 16 * (TILES // 2))

        @block.tensor
        def _(pe):
            def transpose(t, par, uses):
                pe.wait_ge(loaded[par], uses * 16 + 16)
                pe.wait_ge(xT_done, t + 1)
                pe.transpose(ps_t[:, par, 0:P], x_in[par][:, :], ident[:, :]).then_inc(t_done, 1)

            def first(t, par):
                pe.wait_ge(xT_done, t + 3)
                pe.wait_ge(w1_staged, t + 1)
                pe.wait_ge(g1_done, t * F1 + F1)
                for f in range(F1):
                    pe.matmul(ps_1[:, par, f * P:(f + 1) * P], w1[par][:, f * P:(f + 1) * P], xT[par][:, :],
                              start=True, stop=True).then_inc(h1_done, 1)

            def second(t, par):
                pe.wait_ge(w2_staged, t + 1)
                pe.wait_ge(g2_done, t * F2 + F2)
                for o in range(F2):
                    for f in range(F1):
                        if o == 0:
                            pe.wait_ge(g1_done, t * F1 + (2 * F1 + f + 1))
                        at = f * F2 * P + o * P
                        last = pe.matmul(ps_2[:, par, o * P:(o + 1) * P], w2[par][:, at:at + P], h1[par][:, f, :],
                                         start=(f == 0), stop=(f == F1 - 1))
                    last.then_inc(h2_done, 1)

            def third(t, par):
                pe.wait_ge(w3_staged, t + 1)
                pe.wait_ge(y_copied, t + 1)
                pe.matmul(ps_y[:, par, 0:D], ones[:, :], b3[par][:, :], start=True, stop=False)
                for f in range(F2):
                    pe.wait_ge(g2_done, t * F2 + (2 * F2 + f + 1))
                    last = pe.matmul(ps_y[:, par, 0:D], h2[par][:, f, :], w3[par][:, f, :],
                                     start=False, stop=(f == F2 - 1))
                last.then_inc(y_done, 1)

            def one(t, par, i):
                if there(t, 1):
                    first(t + 1, 1 - par)
                if there(t, 2):
                    transpose(t + 2, par, i + 1)
                if there(t, 0):
                    second(t, par)
                if there(t, -1):
                    third(t - 1, 1 - par)

            pe.sem_inc(h1_done, 2 * F1)
            pe.sem_inc(h2_done, 2 * F2)
            pe.sem_inc(y_done, 2)
            pe.wait_ge(ones_set, 1)
            transpose(0, 0, 0)
            transpose(1, 1, 0)
            first(0, 0)
            run_bodies(pe, one, after=1)

        @block.scalar
        def _(act):
            act.sem_inc(xT_done, 2)
            act.sem_inc(g1_done, 2 * F1)
            act.sem_inc(g2_done, 2 * F2)

            def copy_xT(t, par):
                act.wait_ge(t_done, t + 1)
                act.wait_ge(h1_done, t * F1 + F1)
                act.copy(xT[par][:, :], ps_t[:, par, 0:P]).then_inc(xT_done, 1)

            def gelu1(t, par):
                act.wait_ge(h2_done, t * F2 + F2)
                act.wait_ge(h1_done, t * F1 + 3 * F1)
                for f in range(F1):
                    act.activation(h1[par][:, f, :], ps_1[:, par, f * P:(f + 1) * P], ACT.Gelu,
                                   bias=w1[par][:, F1 * P + f:F1 * P + f + 1]).then_inc(g1_done, 1)

            def gelu2(t, par):
                act.wait_ge(y_done, t + 1)
                act.wait_ge(h2_done, t * F2 + 3 * F2)
                for f in range(F2):
                    at = F1 * F2 * P + f
                    act.activation(h2[par][:, f, :], ps_2[:, par, f * P:(f + 1) * P], ACT.Gelu,
                                   bias=w2[par][:, at:at + 1]).then_inc(g2_done, 1)

            def one(t, par, i):
                if there(t, 1):
                    gelu1(t + 1, 1 - par)
                if there(t, 2):
                    copy_xT(t + 2, par)
                gelu2(t, par)

            copy_xT(0, 0)
            copy_xT(1, 1)
            gelu1(0, 0)
            run_bodies(act, one)

        @block.vector
        def _(dve):
            dve.memset(ones[:, :], 1.0).then_inc(ones_set, 1)
            dve.sem_inc(y_copied, 2)

            def stage1(t, par, e):
                dve.wait_ge(g1_done, t * F1 + F1)
                dve.tensor_copy(w1[par][:, :], w["w1"][:, bass.ds(e * SIZE1, SIZE1)]).then_inc(w1_staged, 1)

            def stage2(t, par, e):
                dve.wait_ge(g2_done, t * F2 + F2)
                dve.tensor_copy(w2[par][:, :], w["w2"][:, bass.ds(e * SIZE2, SIZE2)]).then_inc(w2_staged, 1)

            def stage3(t, par, e):
                dve.wait_ge(y_done, t + 1)
                dve.tensor_copy(b3[par][:, :], w["b3"][:, bass.ds(e * D, D)])
                dve.tensor_copy(w3[par][:, :, :].rearrange("p f d -> p (f d)"),
                                w["w3"][:, bass.ds(e * F2 * D, F2 * D)]).then_inc(w3_staged, 1)

            def copy_y(t, par, uses):
                dve.wait_ge(y_done, t + 3)
                if not (type(uses) is int and uses == 0):
                    dve.wait_ge(stored[par], uses * 16)
                dve.tensor_copy(y[par][:, :], ps_y[:, par, 0:D]).then_inc(y_copied, 1)

            def one(t, par, i, experts):
                if there(t, 2):
                    stage1(t + 2, par, experts[2])
                if there(t, -2):
                    copy_y(t - 2, par, i - 1)
                if there(t, 1):
                    stage2(t + 1, 1 - par, experts[1])
                if there(t, 0):
                    stage3(t, par, experts[0])

            e = load_experts(dve, nc, expert_row, 0, 6)
            stage1(0, 0, e[0])
            stage1(1, 1, e[1])
            stage2(0, 0, e[0])
            for t in range(4):
                one(t, t % 2, t // 2, e[t:t + 3])
            with dve.Fori(2, TILES // 2 - 1) as i:
                e = load_experts(dve, nc, expert_row, i * 2, 4)
                for par in range(2):
                    one(i * 2 + par, par, i, e[par:par + 3])
            e = load_experts(dve, nc, expert_row, TILES - 2, 2)
            for t in range(TILES - 2, TILES + 2):
                one(t, t % 2, t // 2, e[t - (TILES - 2):])
            dve.wait_ge(y_copied, TILES + 2)



L0_ATTN = AttnShape(8, 32, 2)
L1_ATTN = AttnShape(16, 8, 1)
L0_MOE = MoeShape("L0", 8, 1, 512)
L1_MOE = MoeShape("L1", 32, 4, 128)


def moe_layer(nc, prefix, ms, w, x_sb, ident, before, ones_bf, x_dram, y_dram, arrivals, start_loads):
    clear_semaphores(nc)
    with ExitStack() as ctx:
        sc = Scope(nc, ctx, prefix)
        xn = sc.sb("xn", [P, NT, D])
        xnT = sc.sb("xnT", [P, N])
        place = sc.sb("place", [P, ms.K, NT], U32)
        weight = sc.sb("weight", [P, NT, ms.K])
        expert_row = sc.sb("expert_row", [1, ms.TILES], I32)
        softmax = ms.K > 1
        rows = slice(0, ms.TILES * P)

        def sync_program(sp):
            start_loads(sp)
            arrivals.wait(sp, f"{ms.name}_router")

        layernorm_phase(nc, prefix + "n", x_sb, xn, xnT, ident, sync_program)
        routing_phase(nc, prefix + "r", ms, xnT, w["router"], w["router_bias"], softmax, place, weight, expert_row,
                      ident, before, ones_bf, arrivals)
        dispatch_phase(nc, prefix + "d", ms, xn, xnT, place, x_dram[rows, :], w.get("shared"), x_sb, arrivals)
        experts = swiglu_experts_phase if softmax else gelu_experts_phase
        experts(nc, prefix + "e", ms, w, expert_row, x_dram[rows, :], y_dram[rows, :], ident)
        combine_phase(nc, prefix + "c", ms, place, weight, y_dram[rows, :], x_sb)


def build(nc, a, out, only=None):
    x_dram = nc.dram_tensor("x_by_expert", [L1_MOE.TILES * P, D], F32, kind="Internal").ap()
    y_dram = nc.dram_tensor("y_by_expert", [L1_MOE.TILES * P, D], F32, kind="Internal").ap()
    max_dram = nc.dram_tensor("max_rows", [2 * NT, P], FP16, kind="Internal").ap()
    parts = {}
    for n, sh in ((0, L0_ATTN), (1, L1_ATTN)):
        parts[n] = [nc.dram_tensor(f"parts_{s}{n}", [2, sh.R, N], FP16, kind="Internal").ap() for s in "qk"]
    ZERO = 4
    do = lambda name: only is None or name in only
    Scope.used = []
    with ExitStack() as ctx:
        sc = Scope(nc, ctx, "all")
        x_sb = sc.sb("x", [P, NT, D])
        ident = sc.sb("ident", [P, P])
        ident_h = sc.sb("ident_h", [P, P], FP16)
        before = sc.sb("before", [P, P], BF16)
        ones_bf = sc.sb("ones_bf", [P, P], BF16)
        ones = sc.sb("ones", [P, P])

        zeros = sc.sb("zeros", [P, ZERO * D])
        arrivals = Arrivals(nc)

        def constants():
            with ExitStack() as inner:
                s2 = Scope(nc, inner, "const")
                x_in, made, zeros_set = s2.sem("x_in"), s2.sem("made"), s2.sem("zeros_set")
                block = inner.enter_context(nc.Block())

                @block.sync
                def _(sp):
                    sp.dma_start(x_sb[:, :, :], a["x"].rearrange("(t p) d -> p t d", p=P)).then_inc(x_in, 16)
                    start_L0_loads(sp, zeros_set)
                    sp.wait_ge(x_in, 16)

                @block.vector
                def _(dve):
                    dve.memset(zeros[:, :], 0.0).then_inc(zeros_set, 1)

                @block.gpsimd
                def _(pool):
                    pool.memset(ident[:, :], 0.0)
                    pool.memset(ident_h[:, :], 0.0)
                    pool.memset(ones_bf[:, :], 1.0)
                    pool.memset(ones[:, :], 1.0)
                    pool.memset(before[:, :], 1.0).then_inc(made, 1)
                    pool.wait_ge(made, 1)
                    for m in (ident, ident_h):
                        pool.affine_select(out=m[:, :], in_=m[:, :], compare_op=ALU.not_equal, fill=1.0, base=0,
                                           pattern=[[-1, P]], channel_multiplier=1)
                    pool.affine_select(out=before[:, :], in_=before[:, :], compare_op=ALU.is_gt, fill=0.0, base=0,
                                       pattern=[[1, P]], channel_multiplier=-1).then_inc(made, 1)
                    pool.wait_ge(made, 2)
                    pool.wait_ge(zeros_set, 1)

        def start_zeros(sp, name, first, last):
            for z in range(first // ZERO, last // ZERO):
                arrivals.start(sp, name, x_dram[z * ZERO * P:(z + 1) * ZERO * P, :].rearrange("(p i) d -> p (i d)", p=P),
                               zeros[:, :])


        def attention(prefix, n, sh, qkv, q_weights, k_weights, w_o, scale, sync_program):
            clear_semaphores(nc)
            with ExitStack() as inner:
                s2 = Scope(nc, inner, prefix)
                v_all = s2.sb("v_all", [P, NT, sh.R])
                scales = s2.sb("scales", [P, 3])
                with ExitStack() as norm:
                    s3 = Scope(nc, norm, prefix + "n")
                    xn = s3.sb("xn", [P, NT, D])
                    xnT = s3.sb("xnT", [P, N])
                    layernorm_phase(nc, prefix + "l", x_sb, xn, xnT, ident, sync_program)
                    scales_phase(nc, prefix + "c", sh, q_weights, k_weights, scale, ones, scales)
                    qkv(prefix + "q", xnT, v_all, scales)
                attn_tok = s2.sb("attn_tok", [P, NT, sh.R])
                scores_phase(nc, prefix + "s", sh, parts[n][0], parts[n][1], max_dram, v_all, attn_tok, ident, ident_h, scales[:, 2:3])
                attn_out_phase(nc, prefix + "o", sh, attn_tok, w_o, x_sb, ident)

        w0 = {"w1": sc.sb("w1", [P, L0_MOE.E * 516]), "w2": sc.sb("w2", [P, L0_MOE.E * 1026]),
              "w3": sc.sb("w3", [P, L0_MOE.E * 2 * D]), "b3": sc.sb("b3", [1, L0_MOE.E * D]),
              "router": sc.sb("router0", [P, L0_MOE.E]), "router_bias": sc.sb("router_bias0", [P, L0_MOE.E])}
        aw0 = {"q": sc.sb("wq", [P, L0_ATTN.R]), "kv_down": sc.sb("kv_down", [P, 64]),
               "k_up": sc.sb("k_up", [64, L0_ATTN.R]), "v_up": sc.sb("v_up", [64, L0_ATTN.R]),
               "o": sc.sb("wo0", [P, 2, D])}

        def start_L0_loads(sp, zeros_set):
            w0_first = w0["w1"][:, :]
            for name, dst, src in (("L0_router", w0["router"][:, :], a["L0_router"]),
                                   ("L0_router", w0["router_bias"][:, :], a["L0_router_bias"].partition_broadcast(P)),
                                   ("L0_experts", w0_first, a["L0_w1"]), ("L0_experts", w0["w2"][:, :], a["L0_w2"]),
                                   ("L0_experts", w0["w3"][:, :], a["L0_w3"]), ("L0_experts", w0["b3"][:, :], a["L0_b3"])):
                if name == "L0_experts" and dst is w0_first:
                    sp.wait_ge(zeros_set, 1)
                    start_zeros(sp, "L0_zeros", 0, L0_MOE.TILES)
                arrivals.start(sp, name, dst, src)

        def start_L0_more(sp):
            for dst, src in ((aw0["q"][:, :], a["L0_wq"]), (aw0["kv_down"][:, :], a["L0_kv_down"]),
                             (aw0["k_up"][:, :], a["L0_k_up"]), (aw0["v_up"][:, :], a["L0_v_up"]),
                             (aw0["o"][:, :, :], a["L0_wo"].rearrange("(r p) d -> p r d", p=P))):
                arrivals.start(sp, "L0_attention", dst, src)

        constants()
        moe = lambda p, loads: moe_layer(nc, p, L0_MOE, w0, x_sb, ident, before, ones_bf, x_dram, y_dram, arrivals, loads)
        if do("m1"):
            moe("m1", start_L0_more)
        if do("a1"):
            attention("a1", 0, L0_ATTN, lambda p, xnT, v, scales: qkv_latent_phase(nc, p, L0_ATTN, xnT, aw0, *parts[0], v, scales),
                      [aw0["q"][:, :]], [aw0["kv_down"][:, :], aw0["k_up"][:, :]], aw0["o"], 32 ** -0.5, lambda sp: arrivals.wait(sp, "L0_attention"))

        shared = {"gate": sc.sb("sgate", [P, 4 * P]), "up": sc.sb("sup", [P, 4 * P]), "down": sc.sb("sdown", [P, 4, D])}
        w1 = {"experts": sc.sb("experts", [P, L1_MOE.E * 3 * P]), "router": sc.sb("router1", [P, L1_MOE.E]),
              "router_bias": sc.sb("router_bias1", [P, L1_MOE.E]), "shared": shared}
        aw1 = {"qkv": sc.sb("wqkv", [P, 2, 2, P]), "v": sc.sb("wv", [P, P]), "o": sc.sb("wo1", [P, 1, D])}

        def start_L1_loads(sp):
            for name, dst, src in (("L1_router", w1["router"][:, :], a["L1_router"]),
                                   ("L1_router", w1["router_bias"][:, :], a["L1_router_bias"].partition_broadcast(P)),
                                   ("L1_shared", shared["gate"][:, :], a["L1_sgate"]),
                                   ("L1_shared", shared["up"][:, :], a["L1_sup"]),
                                   ("L1_shared", shared["down"][:, :, :], a["L1_sdown"].rearrange("(f p) d -> p f d", p=P)),
                                   ("L1_experts", w1["experts"][:, :], a["L1_experts"]),
                                   ("L1_attention", aw1["qkv"][:, :, :, :].rearrange("p a b c -> p (a b c)"), a["L1_wqk"]),
                                   ("L1_attention", aw1["v"][:, :], a["L1_wv"]),
                                   ("L1_attention", aw1["o"][:, 0, :], a["L1_wo"])):
                arrivals.start(sp, name, dst, src)
            start_zeros(sp, "L1_zeros", L0_MOE.TILES, L1_MOE.TILES)

        if do("m2"):
            moe("m2", start_L1_loads)
        else:
            with nc.Block() as block:
                block.sync(start_L1_loads)
        nothing = lambda sp: None
        moe = lambda p: moe_layer(nc, p, L1_MOE, w1, x_sb, ident, before, ones_bf, x_dram, y_dram, arrivals, nothing)
        if do("m3"):
            moe("m3")
        if do("a2"):
            attention("a2", 1, L1_ATTN,
                      lambda p, xnT, v, scales: qkv_rope_phase(nc, p, L1_ATTN, xnT, aw1, a["cos"], a["sin"], *parts[1], v,
                                                               scales),
                      [aw1["qkv"][:, 0, 0, :]], [aw1["qkv"][:, 1, 0, :]], aw1["o"], 8 ** -0.5, lambda sp: arrivals.wait(sp, "L1_attention"))
        if do("m4"):
            moe("m4")
        with ExitStack() as last:
            stored = Scope(nc, last, "out").sem("stored")
            block = last.enter_context(nc.Block())

            @block.sync
            def _(sp):
                sp.dma_start(out.rearrange("(t p) d -> p t d", p=P), x_sb[:, :, :]).then_inc(stored, 16)
                sp.wait_ge(stored, 16)


def lay_out(i):
    f = lambda v: np.ascontiguousarray(np.asarray(v))
    i = {k: np.asarray(v) for k, v in i.items()}
    a = {"x": f(i["L0_attn_x"].reshape(N, D))}
    a["L0_router"] = f(i["L0_ffn_Wr"])
    a["L0_router_bias"] = f(i["L0_ffn_br"])
    w1 = i["L0_ffn_W1"].transpose(1, 0, 2)
    w2 = i["L0_ffn_W2"].reshape(8, 4, P, 256).transpose(2, 0, 1, 3).reshape(P, 8, 1024)
    b1 = i["L0_ffn_b1"].reshape(8, 4, P).transpose(2, 0, 1)
    b2 = i["L0_ffn_b2"].reshape(8, 2, P).transpose(2, 0, 1)
    a["L0_w1"] = f(np.concatenate([w1, b1], axis=2).reshape(P, -1))
    a["L0_w2"] = f(np.concatenate([w2, b2], axis=2).reshape(P, -1))
    a["L0_w3"] = f(i["L0_ffn_W3"].reshape(8, 2, P, D).transpose(2, 0, 1, 3).reshape(P, -1))
    a["L0_b3"] = f(i["L0_ffn_b3"].reshape(1, -1))
    a["L0_wq"] = f(i["L0_attn_Wq"].T)
    a["L0_kv_down"] = f(i["L0_attn_Wkv_down"].T)
    a["L0_k_up"] = f(i["L0_attn_Wk_up"].T)
    a["L0_v_up"] = f(i["L0_attn_Wv_up"].T)
    a["L0_wo"] = f(i["L0_attn_Wo"].T)
    a["L1_router"] = f(i["L1_ffn_router_w"].T)
    a["L1_router_bias"] = f(i["L1_ffn_router_bias"])
    gate, up = i["L1_ffn_gate_w"].transpose(2, 0, 1), i["L1_ffn_up_w"].transpose(2, 0, 1)
    down = i["L1_ffn_down_w"].transpose(2, 0, 1)
    a["L1_experts"] = f(np.concatenate([gate, up, down], axis=2).reshape(P, -1))
    a["L1_sgate"] = f(i["L1_ffn_sgate_w"].T)
    a["L1_sup"] = f(i["L1_ffn_sup_w"].T)
    a["L1_sdown"] = f(i["L1_ffn_sdown_w"].T)
    qkv = i["L1_attn_Wqkv"].reshape(P, 3, 16, 2, 4)
    a["L1_wqk"] = f(np.stack([qkv[:, :2], qkv[:, :2, :, ::-1]], axis=2).reshape(P, -1))
    a["L1_wv"] = f(qkv[:, 2].reshape(P, P))
    a["L1_wo"] = f(i["L1_attn_Wo"])
    inv_freq = (1.0 / 10000.0 ** (np.arange(0, 8, 2, dtype=np.float32) / np.float32(8))).astype(np.float32)
    angle = np.outer(np.arange(N, dtype=np.float32), inv_freq).astype(np.float32).T
    a["cos"] = f(np.tile(np.cos(angle), (32, 1)).astype(np.float32))
    a["sin"] = f(np.tile(np.concatenate([-np.sin(angle), np.sin(angle)]), (16, 1)).astype(np.float32))
    return a


def kernel(**inputs):
    import numpy as _np
    import concourse.bacc as _bacc
    from concourse import mybir as _mybir
    from concourse.bass_utils import run_bass_kernel_spmd as _run

    nc = _bacc.Bacc("TRN2", target_bir_lowering=False, num_devices=1)
    arrays = {f"in_{k}": v for k, v in lay_out(inputs).items()}
    aps = {k[3:]: nc.dram_tensor(k, v.shape, _mybir.dt.from_np(v.dtype), kind="ExternalInput").ap()
           for k, v in arrays.items()}
    out = nc.dram_tensor("out_0", (N, D), F32, kind="ExternalOutput").ap()
    build(nc, aps, out)
    r = _run(nc, [arrays], core_ids=[0])
    return r.results[0]["out_0"].reshape(1, N, D)
```

```python
import numpy as np
import concourse.bass as bass
from concourse import mybir
from contextlib import ExitStack

F32 = mybir.dt.float32
BF16 = mybir.dt.bfloat16
FP16 = mybir.dt.float16
I32 = mybir.dt.int32
U32 = mybir.dt.uint32
ALU = mybir.AluOpType
ACT = mybir.ActivationFunctionType
AX = mybir.AxisListType

P = 128
N = 2048
D = 128
NT = N // P
BANK = 512
NC4 = N // BANK
EPS = 1e-5


class Scope:

    used = []

    def __init__(self, nc, ctx, prefix):
        self.nc, self.ctx, self.prefix = nc, ctx, prefix

    def sb(self, name, shape, dt=F32):
        return self.ctx.enter_context(self.nc.sbuf_tensor(f"{self.prefix}_{name}", shape, dt))

    def ps(self, name, shape, dt=F32):
        return self.ctx.enter_context(self.nc.psum_tensor(f"{self.prefix}_{name}", shape, dt))

    def sem(self, name):
        s = self.nc.alloc_semaphore(f"{self.prefix}_{name}")
        Scope.used.append(s)
        return s


def clear_semaphores(nc):
    nc.clear_and_free_semaphores(Scope.used)
    nc.all_engine_barrier()
    Scope.used = []


class Arrivals:

    def __init__(self, nc):
        self.nc, self.sems, self.counts = nc, {}, {}

    def start(self, engine, name, dst, src):
        if name not in self.sems:
            self.sems[name] = self.nc.alloc_semaphore(f"arrived_{name}")
            self.counts[name] = 0
        self.counts[name] += 16
        engine.dma_start(dst, src).then_inc(self.sems[name], 16)

    def wait(self, engine, *names):
        for name in names:
            if name in self.sems:
                engine.wait_ge(self.sems[name], self.counts[name])


class AttnShape:

    def __init__(self, heads, hd, units):
        self.H, self.HD = heads, hd
        self.R = heads * hd
        self.RH = self.R // P
        self.U = units
        self.G = NC4 // units
        self.W = P // self.G
        self.STEPS = units * NT
        self.CH = self.STEPS * self.G
        self.MPS = 32 // self.STEPS
        self.terms = [(0, 0), (0, 1), (1, 0)] + ([(1, 1)] if hd * 4 <= 96 else [])
        self.ROW_MAX = 96
        self.SUM_MAX = 2.0 ** 15


class ScoreScales:

    def __init__(self, sc, sh, weights, scale, ones, scales):
        self.sh, self.weights, self.scale, self.ones, self.scales = sh, weights, scale, ones, scales
        W = len(weights)
        self.square = [sc.sb(f"square{i}", [P, w.shape[1]]) for i, w in enumerate(weights)]
        self.total = sc.sb("total", [P, W])
        self.norm = sc.sb("norm", [P, W])
        self.bound = sc.sb("bound", [P, 2])
        self.power = sc.sb("power", [P, 2])
        self.two_over = sc.sb("two_over", [P, 2])
        self.ps = sc.ps("ps_norm", [P, W])
        self.step = sc.sem("step")
        self.totals_done = sc.sem("totals_done")
        self.summed, self.rooted = sc.sem("summed"), sc.sem("rooted")

    def pe(self, pe):
        pe.wait_ge(self.totals_done, 1)
        pe.matmul(self.ps[:, :], self.ones[:, :], self.total[:, :], start=True, stop=True).then_inc(self.summed, 1)

    def act(self, act):
        act.wait_ge(self.summed, 1)
        act.activation(self.norm[:, :], self.ps[:, :], ACT.Sqrt).then_inc(self.rooted, 1)

    def dve(self, dve):
        count = [0]

        def then(ins):
            count[0] += 1
            ins.then_inc(self.step, 1)
            dve.wait_ge(self.step, count[0])

        then(dve.memset(self.total[:, :], 0.0))
        for i, w in enumerate(self.weights):
            K = w.shape[0]
            then(dve.tensor_tensor(self.square[i][0:K, :], w, w, ALU.mult))
            last = dve.tensor_reduce(self.total[0:K, i:i + 1], self.square[i][0:K, :], AX.X, ALU.add)
        last.then_inc(self.totals_done, 1)
        dve.wait_ge(self.rooted, 1)
        norm, bound, power, two_over = self.norm, self.bound, self.power, self.two_over
        if len(self.weights) == 3:
            then(dve.tensor_tensor(norm[:, 1:2], norm[:, 1:2], norm[:, 2:3], ALU.mult))
        then(dve.tensor_scalar(bound[:, :], norm[:, 0:2], float(1.01 * D ** 0.5), float(2.0 ** -60), ALU.mult, ALU.max))
        EXPONENT = 0x7F800000
        as_int = lambda t: t[:, :].bitcast(I32)
        dve.tensor_scalar(as_int(power), as_int(bound), EXPONENT, None, ALU.bitwise_and)
        then(dve.tensor_scalar(as_int(two_over), as_int(bound), EXPONENT, EXPONENT, ALU.bitwise_and, ALU.bitwise_xor))
        dve.tensor_scalar(self.scales[:, 0:2], two_over[:, :], self.sh.SUM_MAX / 4, None, ALU.mult)
        then(dve.tensor_scalar(power[:, :], power[:, :], 2 / self.sh.SUM_MAX, None, ALU.mult))
        then(dve.scalar_tensor_tensor(self.scales[:, 2:3], power[:, 0:1], float(self.scale), power[:, 1:2],
                                      ALU.mult, ALU.mult))


def scores_phase(nc, prefix, sh, parts_q, parts_k, max_dram, v_all, attn_tok, ident, ident_h, exp_scale):
    H, HD, G, W, U, STEPS, CH = sh.H, sh.HD, sh.G, sh.W, sh.U, sh.STEPS, sh.CH
    MCH, SLOTS, SBANKS, SHIFT = 32, 8, 3, 3
    TURNS = MCH + 1 + U
    AHEAD = 12 if sh.MPS == 2 else 8
    LEAD = MCH + AHEAD + 1
    with ExitStack() as ctx:
        sc = Scope(nc, ctx, prefix)
        ROW_MAX = sh.ROW_MAX
        TERM_ROWS = len(sh.terms) * HD
        LOAD = 2 * 16 * len(sh.terms)
        mq = [sc.sb(f"mq{i}", [P, N], FP16) for i in range(2)]
        mk = [sc.sb(f"mk{i}", [P, N], FP16) for i in range(2)]
        sq = [sc.sb(f"sq{i}", [P, N], FP16) for i in range(2)]
        sk = [sc.sb(f"sk{i}", [P, N], FP16) for i in range(2)]
        vh = [sc.sb(f"vh{i}", [P, NT, W]) for i in range(2)]
        probs = sc.sb("probs", [P, SLOTS, BANK])
        half_max = sc.sb("half_max", [P, 2, NT, 2])
        row_max = sc.sb("row_max", [P, NT])
        max_parts = sc.sb("max_parts", [P, 2, NT], FP16)
        max_rows = sc.sb("max_rows", [2 * NT, P], FP16)
        o_sb = [sc.sb(f"o_sb{i}", [P, BANK]) for i in range(2)]
        rsum = sc.sb("rsum", [P, G, 4])
        ps_m = sc.ps("ps_m", [P, 2, 2 * BANK])
        ps_s = sc.ps("ps_s", [P, SBANKS, BANK])
        ps_o = sc.ps("ps_o", [P, BANK])

        mcleared = sc.sem("mcleared")
        scleared = sc.sem("scleared")
        ones_set = sc.sem("ones_set")
        mstack_in = [sc.sem(f"mstack_in{i}") for i in range(2)]
        sstack_in = [sc.sem(f"sstack_in{i}") for i in range(2)]
        maxrow_out = sc.sem("maxrow_out")
        maxrow_in = [sc.sem(f"maxrow_in{i}") for i in range(2)]
        v_in = sc.sem("v_in")
        m_done = sc.sem("m_done")
        m_used = sc.sem("m_used")
        s_done = sc.sem("s_done")
        exp_done = sc.sem("exp_done")
        pv_done = sc.sem("pv_done")
        o_copied = sc.sem("o_copied")
        parts_done = sc.sem("parts_done")
        split_step = sc.sem("split_step")
        own_step = sc.sem("own_step")
        norm_step = sc.sem("norm_step")
        block = ctx.enter_context(nc.Block())
        FREE_STEPS = SLOTS // G

        def round_turns(with_next, with_second):
            out = []
            for r in range(STEPS):
                if U == 2 and r == NT + 2 - SHIFT:
                    out.append((r, "x", 0))
                if r == STEPS - 1:
                    out.append((r, "x", U - 1))
                for c in range(r * sh.MPS, (r + 1) * sh.MPS):
                    if c < MCH - AHEAD:
                        if with_next:
                            out.append((r, "m", (1, AHEAD + c)))
                    else:
                        if with_second:
                            out.append((r, "m", (2, c - (MCH - AHEAD))))
                        if with_next and c == MCH - AHEAD + 1:
                            out.append((r, "t", None))
            return out

        rounds = {"loop": round_turns(True, True), "second last": round_turns(True, False),
                  "last": round_turns(False, False)}
        assert len(rounds["loop"]) == TURNS

        def turn_base(h):
            if type(h) is int and h == H - 1:
                return LEAD + (H - 2) * TURNS + len(rounds["second last"])
            return LEAD + h * TURNS

        def slot(h, par, idx):
            return (turn_base(h if type(h) is int else par) + idx) % 2

        def t_turn(h):
            if type(h) is int and h == 0:
                return MCH + 2
            where = [k for _, k, _ in rounds["loop"] if k != "skip"]
            idx = where.index("t")
            if type(h) is int and h == H - 1:
                idx = [k for _, k, _ in rounds["second last"]].index("t")
            return turn_base(h - 1) + idx

        def run_rounds(eng, one):
            with eng.Fori(0, H // 2 - 1) as i:
                for par in range(2):
                    one(i * 2 + par, par, "loop", lambda ahead, par=par: i + (par + ahead) // 2 + 1)
            for h, kind in ((H - 2, "second last"), (H - 1, "last")):
                one(h, h % 2, kind, lambda ahead, h=h: (h + ahead) // 2 + 1)

        @block.sync
        def _(sp):
            def load(stack_q, stack_k, h, sem):
                for r, (a, b) in enumerate(sh.terms):
                    rows = slice(r * HD, (r + 1) * HD)
                    sp.dma_start(stack_q[rows, :], parts_q[a, bass.ds(h * HD, HD), :]).then_inc(sem, 16)
                    sp.dma_start(stack_k[rows, :], parts_k[b, bass.ds(h * HD, HD), :]).then_inc(sem, 16)

            def load_max_stack(h, par):
                load(mq[par], mk[par], h, mstack_in[par])

            def load_score_stack(h, par):
                load(sq[par], sk[par], h, sstack_in[par])

            def load_max_rows(h, par):
                sp.wait_ge(m_used, 2 + t_turn(h) + 1)
                sp.dma_start(max_dram, max_rows[:, :]).then_inc(maxrow_out, 16)
                sp.wait_ge(maxrow_out, (h + 1) * 16)
                sp.dma_start(sq[par][ROW_MAX:ROW_MAX + 2, :],
                             max_dram.rearrange("(a t) n -> a (t n)", a=2)).then_inc(maxrow_in[par], 16)

            if TERM_ROWS < ROW_MAX:
                sp.wait_ge(mcleared, 1)
            load_max_stack(0, 0)
            if TERM_ROWS < ROW_MAX:
                sp.wait_ge(scleared, 1)
            load_score_stack(0, 0)
            if TERM_ROWS < ROW_MAX:
                sp.wait_ge(mcleared, 2)
            load_max_stack(1, 1)
            if TERM_ROWS < ROW_MAX:
                sp.wait_ge(scleared, 2)
            load_max_rows(0, 0)

            def one(h, par, kind, loads):
                if kind != "last":
                    sp.wait_ge(s_done, h * CH + 1)
                    load_score_stack(h + 1, 1 - par)
                if kind == "loop":
                    sp.wait_ge(m_done, turn_base(h) + 1)
                    load_max_stack(h + 2, par)
                if kind != "last":
                    load_max_rows(h + 1, 1 - par)

            run_rounds(sp, one)

        @block.gpsimd
        def _(pool):
            for i in range(2):
                pool.memset(sk[i][ROW_MAX:ROW_MAX + 2, :], -sh.SUM_MAX).then_inc(own_step, 1)
                pool.wait_ge(own_step, 2 * i + 1)
                pool.memset(vh[i][:, :, HD:], 0.0).then_inc(own_step, 1)
                pool.wait_ge(own_step, 2 * i + 2)
                pool.memset(vh[i][:, :, HD:HD + 1], 1.0).then_inc(ones_set, 1)
                pool.wait_ge(ones_set, i + 1)

            def copy_v(h, par):
                pool.tensor_copy(vh[par][:, :, 0:HD], v_all[:, :, bass.ds(h * HD, HD)]).then_inc(v_in, 1)

            copy_v(0, 0)
            copy_v(1, 1)

            def one(h, par, kind, loads):
                if kind == "loop":
                    pool.wait_ge(pv_done, FREE_STEPS + (h + 1) * STEPS)
                    copy_v(h + 2, par)

            run_rounds(pool, one)

        @block.tensor
        def _(pe):
            def turn(number, slot, kind, what, h, par, loads):
                pe.wait_ge(m_used, number + 1)
                if kind == "m":
                    ahead, c = what
                    of = (par + ahead) % 2
                    if c == 0:
                        pe.wait_ge(mstack_in[of], loads(ahead) * LOAD)
                    t, half = c // 2, c % 2
                    for b in range(2):
                        col = (2 * half + b) * BANK
                        last = pe.matmul(ps_m[:, slot, b * BANK:(b + 1) * BANK],
                                         mq[of][0:ROW_MAX, t * P:(t + 1) * P],
                                         mk[of][0:ROW_MAX, col:col + BANK], start=True, stop=True)
                    last.then_inc(m_done, 1)
                elif kind == "t":
                    pe.wait_ge(parts_done, h + 2)
                    pe.transpose(ps_m[0:2 * NT, slot, 0:P // 2].bitcast(FP16),
                                 max_parts[:, :, :].rearrange("p a t -> p (a t)"), ident_h[:, :]).then_inc(m_done, 1)
                else:
                    pe.wait_ge(o_copied, h * U + what + 2)
                    src = o_sb[what if U == 2 else par]
                    for c in range(4):
                        last = pe.transpose(ps_m[:, slot, c * P:(c + 1) * P], src[:, c * P:(c + 1) * P], ident[:, :])
                    last.then_inc(m_done, 1)

            def score_chunk(h, par, q):
                s, g = q // G, q % G
                kt, col = s % NT, (s // NT * G + g) * BANK
                before = q - SBANKS if q >= SBANKS else max(c for c in range(CH) if c % SBANKS == q) - CH
                pe.wait_ge(exp_done, h * CH + (SBANKS + before + 1))
                pe.matmul(ps_s[:, q % SBANKS, :], sk[par][0:ROW_MAX + 2, kt * P:(kt + 1) * P],
                          sq[par][0:ROW_MAX + 2, col:col + BANK], start=True, stop=True).then_inc(s_done, 1)

            def probs_v(h, par, s):
                kt = s % NT
                pe.wait_ge(exp_done, h * CH + (SBANKS + G * (s + 1)))
                if kt == 0:
                    pe.wait_ge(o_copied, h * U + (s // NT + 1))
                if s == 0:
                    pe.wait_ge(v_in, h + 1)
                for g in range(G):
                    last = pe.matmul(ps_o[g * W:(g + 1) * W, :], vh[par][:, kt, :], probs[:, (s * G + g) % SLOTS, :],
                                     start=(kt == 0), stop=(kt == NT - 1))
                last.then_inc(pv_done, 1)

            def step(h, par, s, between, before, loads_of):
                if s == 0:
                    pe.wait_ge(sstack_in[par], loads_of * LOAD)
                    pe.wait_ge(maxrow_in[par], loads_of * 16)
                between = list(between)
                for g in range(G):
                    score_chunk(h, par, s * G + g)
                    if between:
                        between.pop(0)()
                while between:
                    between.pop(0)()
                if before:
                    probs_v(*before)

            pe.sem_inc(pv_done, FREE_STEPS)
            for c in range(MCH):
                turn(c, c % 2, "m", (0, c), 0, 0, lambda ahead: 1)
            n = MCH
            for c in range(AHEAD):
                turn(n, n % 2, "m", (1, c), 0, 0, lambda ahead: 1)
                n += 1
                if c == 1:
                    turn(n, n % 2, "t", None, -1, 0, None)
                    n += 1
            pe.wait_ge(ones_set, 2)
            for s in range(SHIFT):
                step(0, 0, s, [], (0, 0, s - 1) if s else None, 1)

            def one(h, par, kind, loads):
                mine = rounds[kind]
                for r in range(STEPS):
                    between = [lambda i=i, k=k, w=w: turn(turn_base(h) + i, slot(h, par, i), k, w, h, par, loads)
                               for i, (at, k, w) in enumerate(mine) if at == r]
                    s = r + SHIFT
                    if s < STEPS:
                        step(h, par, s, between, (h, par, s - 1), None)
                    elif kind != "last":
                        s -= STEPS
                        before = (h, par, STEPS - 1) if s == 0 else (h + 1, 1 - par, s - 1)
                        step(h + 1, 1 - par, s, between, before, loads(1))
                    else:
                        if s == STEPS:
                            probs_v(h, par, STEPS - 1)
                        for b in between:
                            b()

            run_rounds(pe, one)

        @block.scalar
        def _(act):
            act.sem_inc(exp_done, SBANKS)
            act.sem_inc(o_copied, 1)

            def exps(h, s):
                for q in range(s * G, (s + 1) * G):
                    act.wait_ge(s_done, h * CH + (q + 1))
                    if q == s * G:
                        act.wait_ge(pv_done, h * STEPS + (s + 1))
                    act.activation(probs[:, q % SLOTS, :], ps_s[:, q % SBANKS, :], ACT.Exp,
                                   scale=exp_scale).then_inc(exp_done, 1)

            def copy_out(h, par, unit):
                act.wait_ge(pv_done, h * STEPS + (FREE_STEPS + (unit + 1) * NT))
                act.copy(o_sb[unit if U == 2 else par][:, :], ps_o[:, :]).then_inc(o_copied, 1)

            def one(h, par, kind, loads):
                for s in range(1, STEPS):
                    exps(h, s)
                    if s == NT:
                        copy_out(h, par, 0)
                if kind != "last":
                    exps(h + 1, 0)
                copy_out(h, par, U - 1)

            exps(0, 0)
            run_rounds(act, one)

        @block.vector
        def _(dve):
            if TERM_ROWS < ROW_MAX:
                for i in range(2):
                    for stack in (mq[i], mk[i]):
                        last = dve.memset(stack[0:ROW_MAX, :].bitcast(U32), 0)
                    last.then_inc(mcleared, 1)
                    for stack in (sq[i], sk[i]):
                        last = dve.memset(stack[0:ROW_MAX, :].bitcast(U32), 0)
                    last.then_inc(scleared, 1)
            dve.sem_inc(m_used, 2)

            def read_max(number, slot, of, c):
                dve.wait_ge(m_done, number + 1)
                dve.reduce_max(half_max[:, of, c // 2, c % 2:c % 2 + 1], ps_m[:, slot, :], AX.X).then_inc(m_used, 1)

            def split_max(number, of, h):
                dve.wait_ge(m_used, number + 3)
                dve.tensor_tensor(row_max[:, :], half_max[:, of, :, 0], half_max[:, of, :, 1],
                                  ALU.max).then_inc(split_step, 1)
                dve.wait_ge(split_step, h * 2 + 1)
                dve.tensor_scalar(max_parts[:, 0, :], row_max[:, :], 1 / sh.SUM_MAX, None, ALU.mult).then_inc(split_step, 1)
                dve.wait_ge(split_step, h * 2 + 2)
                dve.scalar_tensor_tensor(max_parts[:, 1, :], row_max[:, :], 1 / sh.SUM_MAX, max_parts[:, 0, :],
                                         ALU.mult, ALU.subtract).then_inc(parts_done, 1)

            def read_rows(number, slot, h):
                dve.wait_ge(m_done, number + 1)
                if not (type(h) is int and h == 0):
                    dve.wait_ge(maxrow_out, h * 16)
                dve.tensor_copy(max_rows[:, :], ps_m[0:2 * NT, slot, 0:P // 2].bitcast(FP16)).then_inc(m_used, 1)

            def read_out(number, slot, unit, h):
                dve.wait_ge(m_done, number + 1)
                dve.wait_ge(m_used, number + 2)
                src = ps_m[:, slot, 0:BANK].rearrange("p (c g w) -> p g c w", c=4, g=G)
                dve.reciprocal(rsum[:, :, :], src[:, :, :, HD]).then_inc(norm_step, 1)
                dve.wait_ge(norm_step, h * U + (unit + 1))
                t0 = unit * G * 4
                dst = attn_tok[:, t0:t0 + 4 * G, bass.ds(h * HD, HD)].rearrange("p (g c) w -> p g c w", g=G)
                dve.tensor_tensor(dst, src[:, :, :, 0:HD], rsum[:, :, :].unsqueeze(3).to_broadcast([P, G, 4, HD]),
                                  ALU.mult).then_inc(m_used, 1)

            for c in range(MCH):
                read_max(c, c % 2, 0, c)
            split_max(MCH - 1, 0, 0)
            n = MCH
            for c in range(AHEAD):
                read_max(n, n % 2, 1, c)
                n += 1
                if c == 1:
                    read_rows(n, n % 2, 0)
                    n += 1

            def one(h, par, kind, loads):
                base = turn_base(h)
                for idx, (_, k, what) in enumerate(rounds[kind]):
                    if k == "m":
                        ahead, c = what
                        read_max(base + idx, slot(h, par, idx), (par + ahead) % 2, c)
                        if c == MCH - 1:
                            split_max(base + idx, (par + ahead) % 2, h + ahead)
                    elif k == "t":
                        read_rows(base + idx, slot(h, par, idx), h + 1)
                    else:
                        read_out(base + idx, slot(h, par, idx), what, h)

            run_rounds(dve, one)
            dve.wait_ge(m_used, turn_base(H - 1) + len(rounds["last"]) + 2)




class Step:

    def pe(self, pe, c):
        pass

    def act(self, act, c):
        pass

    def dve(self, dve, c):
        pass

    def pool(self, pool, c):
        pass

    def sync(self, sp, c):
        pass

    def sync_end(self, sp):
        pass

    def wait_x(self, eng, c):
        pass


class LoadedX(Step):

    def __init__(self, x_in):
        self.x_in = x_in

    def wait_x(self, eng, c):
        eng.wait_ge(self.x_in[c], 16)


class Combine(Step):

    def __init__(self, sc, ms, place, weight, y_dram, x_sb):
        self.RING = 16
        self.K, self.place, self.weight, self.y_dram, self.x_sb = ms.K, place, weight, y_dram, x_sb
        self.got = sc.sb("got", [P, self.RING, D])
        self.row_in = [sc.sem(f"row_in{i}") for i in range(self.RING)]
        self.added = sc.sem("added")

    def rows(self, c):
        return [(n, n // self.K, n % self.K) for n in range(4 * c * self.K, 4 * (c + 1) * self.K)]

    def pool(self, pool, c):
        for n, t, k in self.rows(c):
            if n >= self.RING:
                pool.wait_ge(self.added, n - self.RING + 1)
            pool.indirect_dma_start(self.got[:, n % self.RING, :], None, self.y_dram,
                                    bass.IndirectOffsetOnAxis(ap=self.place[:, k, t:t + 1], axis=0))\
                .then_inc(self.row_in[n % self.RING], 16)

    def dve(self, dve, c):
        for n, t, k in self.rows(c):
            dve.wait_ge(self.row_in[n % self.RING], 16 * (n // self.RING + 1))
            if k:
                dve.wait_ge(self.added, n)
            w = self.weight[:, t, k:k + 1] if self.K > 1 else 0.5
            dve.scalar_tensor_tensor(self.x_sb[:, t, :], self.got[:, n % self.RING, :], w, self.x_sb[:, t, :],
                                     ALU.mult, ALU.add).then_inc(self.added, 1)

    def wait_x(self, eng, c):
        eng.wait_ge(self.added, 4 * (c + 1) * self.K)


class AttnOut(Step):

    def __init__(self, sc, sh, attn_tok, w_o, x_sb, ident):
        self.sh, self.attn_tok, self.w_o, self.x_sb, self.ident = sh, attn_tok, w_o, x_sb, ident
        self.attT = [sc.sb(f"attT{i}", [P, sh.RH, BANK]) for i in range(2)]
        self.ps_t = sc.ps("ps_t", [P, 2, sh.RH, BANK])
        self.ps_y = sc.ps("ps_y", [P, 2, BANK])
        self.tp_done, self.t_copied = sc.sem("tp_done"), sc.sem("t_copied")
        self.y_done, self.x_done = sc.sem("y_done"), sc.sem("x_done")

    def transposes(self, pe, c):
        if c >= 2:
            pe.wait_ge(self.t_copied, c - 1)
        for i in range(4):
            for r in range(self.sh.RH):
                last = pe.transpose(self.ps_t[:, c % 2, r, i * P:(i + 1) * P],
                                    self.attn_tok[:, 4 * c + i, r * P:(r + 1) * P], self.ident[:, :])
        last.then_inc(self.tp_done, 1)

    def pe(self, pe, c):
        if c == 0:
            self.transposes(pe, 0)
        if c + 1 < NC4:
            self.transposes(pe, c + 1)
        pe.wait_ge(self.t_copied, c + 1)
        if c >= 2:
            pe.wait_ge(self.x_done, c - 1)
        for i in range(4):
            for r in range(self.sh.RH):
                last = pe.matmul(self.ps_y[:, c % 2, i * P:(i + 1) * P], self.attT[c % 2][:, r, i * P:(i + 1) * P],
                                 self.w_o[:, r, :], start=(r == 0), stop=(r == self.sh.RH - 1))
        last.then_inc(self.y_done, 1)

    def act(self, act, c):
        act.wait_ge(self.tp_done, c + 1)
        if c >= 2:
            act.wait_ge(self.y_done, c - 1)
        act.copy(self.attT[c % 2][:, :, :], self.ps_t[:, c % 2, :, :]).then_inc(self.t_copied, 1)

    def dve(self, dve, c):
        dve.wait_ge(self.y_done, c + 1)
        xs = self.x_sb[:, 4 * c:4 * c + 4, :].rearrange("p t d -> p (t d)")
        dve.tensor_tensor(xs, xs, self.ps_y[:, c % 2, :], ALU.add).then_inc(self.x_done, 1)

    def wait_x(self, eng, c):
        eng.wait_ge(self.x_done, c + 1)


class Norm:

    def __init__(self, sc, x_sb, xn, xnT, ident):
        self.x_sb, self.xn, self.xnT, self.ident = x_sb, xn, xnT, ident
        self.stats = sc.sb("stats", [P, NT, 6])
        self.meanvar = sc.sb("meanvar", [P, NT, 2])
        self.std = sc.sb("std", [P, NT])
        self.rstd = sc.sb("rstd", [P, NT])
        self.eps = sc.sb("eps", [P, 1])
        self.warm = sc.sb("warm", [P, 1])
        self.tp = sc.ps("tp", [P, BANK])
        self.eps_set = sc.sem("eps_set")
        self.stats_done = sc.sem("stats_done")
        self.var_done = sc.sem("var_done")
        self.std_done = sc.sem("std_done")
        self.rstd_done = sc.sem("rstd_done")
        self.xn_done = sc.sem("xn_done")
        self.nt_done = sc.sem("nt_done")
        self.xnT_done = sc.sem("xnT_done")

    def dve_start(self, dve):
        dve.memset(self.eps[:, :], EPS).then_inc(self.eps_set, 1)

    def act_start(self, act):
        act.wait_ge(self.eps_set, 1)
        act.activation(self.warm[:, :], self.eps[:, :], ACT.Sqrt)

    def dve_stats(self, dve, c):
        for t in range(4 * c, 4 * c + 4):
            dve.bn_stats(self.stats[:, t, :], self.x_sb[:, t, :]).then_inc(self.stats_done, 1)
        for t in range(4 * c, 4 * c + 4):
            dve.wait_ge(self.stats_done, t + 1)
            dve.bn_aggr(self.meanvar[:, t, :], self.stats[:, t, :]).then_inc(self.var_done, 1)

    def act_std(self, act, c):
        tiles = slice(4 * c, 4 * c + 4)
        act.wait_ge(self.var_done, 4 * (c + 1))
        act.activation(self.std[:, tiles], self.meanvar[:, tiles, 1], ACT.Sqrt, bias=self.eps[:, 0:1])\
           .then_inc(self.std_done, 1)

    def dve_scale(self, dve, c):
        tiles = slice(4 * c, 4 * c + 4)
        dve.wait_ge(self.std_done, c + 1)
        dve.reciprocal(self.rstd[:, tiles], self.std[:, tiles]).then_inc(self.rstd_done, 1)
        dve.wait_ge(self.rstd_done, c + 1)
        for t in range(4 * c, 4 * c + 4):
            dve.tensor_scalar(self.xn[:, t, :], self.x_sb[:, t, :], self.meanvar[:, t, 0:1], self.rstd[:, t:t + 1],
                              ALU.subtract, ALU.mult).then_inc(self.xn_done, 1)

    def pe(self, pe, c):
        if c:
            pe.wait_ge(self.xnT_done, c)
        for t in range(4 * c, 4 * c + 4):
            pe.wait_ge(self.xn_done, t + 1)
            last = pe.transpose(self.tp[:, (t % 4) * P:(t % 4 + 1) * P], self.xn[:, t, :], self.ident[:, :])
        last.then_inc(self.nt_done, 1)

    def act_copy(self, act, c):
        act.wait_ge(self.nt_done, c + 1)
        act.copy(self.xnT[:, c * BANK:(c + 1) * BANK], self.tp[:, :]).then_inc(self.xnT_done, 1)


class RouterLogits(Step):

    def __init__(self, sc, ms, norm, w_r, bias, logits):
        self.ms, self.norm, self.w_r, self.bias, self.logits = ms, norm, w_r, bias, logits
        self.ps_l = sc.ps("ps_l", [P, NT, ms.E])
        self.logits_done, self.biased = sc.sem("logits_done"), sc.sem("biased")

    def pe(self, pe, c):
        pe.wait_ge(self.norm.xnT_done, c + 1)
        for t in range(4 * c, 4 * c + 4):
            last = pe.matmul(self.ps_l[:, t, :], self.norm.xnT[:, t * P:(t + 1) * P], self.w_r[:, :], start=True, stop=True)
        last.then_inc(self.logits_done, 1)

    def dve(self, dve, c):
        if c == NC4 - 1:
            dve.wait_ge(self.logits_done, NC4)
            dve.tensor_tensor(self.logits, self.ps_l[:, :, :], self.bias[:, :].unsqueeze(1).to_broadcast([P, NT, self.ms.E]),
                              ALU.add).then_inc(self.biased, 1)
            dve.wait_ge(self.biased, 1)


class LatentQkv(Step):

    def __init__(self, sc, sh, norm, w, parts_q, parts_k, v_all, scales):
        self.sh, self.norm, self.w, self.v_all, self.scales = sh, norm, w, v_all, scales
        self.parts = (parts_q, parts_k)
        self.units = [(which, half) for which in (0, 1) for half in range(sh.RH)]
        self.U = len(self.units)
        self.latT = sc.sb("latT", [w["kv_down"].shape[1], N])
        self.part = [sc.sb(f"part{i}", [P, 2, BANK], FP16) for i in range(self.U)]
        self.ps = sc.ps("ps", [P, self.U, BANK])
        self.ps_lat = sc.ps("ps_lat", [w["kv_down"].shape[1], BANK])
        self.ps_v = sc.ps("ps_v", [P, 4, sh.R])
        self.lat_done, self.lat_copied = sc.sem("lat_done"), sc.sem("lat_copied")
        self.proj_done = sc.sem("proj_done")
        self.v_done, self.v_copied = sc.sem("v_done"), sc.sem("v_copied")
        self.high_done, self.low_done = sc.sem("high_done"), sc.sem("low_done")
        self.part_out = [sc.sem(f"part_out{i}") for i in range(self.U)]

    def pe(self, pe, c):
        chunk = slice(c * BANK, (c + 1) * BANK)
        w, xnT, latT = self.w, self.norm.xnT, self.latT
        pe.wait_ge(self.norm.xnT_done, c + 1)
        if c:
            pe.wait_ge(self.lat_copied, c)
        pe.matmul(self.ps_lat[:, :], w["kv_down"][:, :], xnT[:, chunk], start=True, stop=True).then_inc(self.lat_done, 1)
        for i, (which, half) in enumerate(self.units):
            if c:
                pe.wait_ge(self.low_done, (c - 1) * self.U + i + 1)
            cols = slice(half * P, (half + 1) * P)
            if which == 0:
                pe.matmul(self.ps[:, i, :], w["q"][:, cols], xnT[:, chunk], start=True, stop=True)\
                  .then_inc(self.proj_done, 1)
            else:
                pe.wait_ge(self.lat_copied, c + 1)
                pe.matmul(self.ps[:, i, :], w["k_up"][:, cols], latT[:, chunk], start=True, stop=True)\
                  .then_inc(self.proj_done, 1)
        if c:
            pe.wait_ge(self.v_copied, c)
        for i in range(4):
            t = 4 * c + i
            last = pe.matmul(self.ps_v[:, i, :], latT[:, t * P:(t + 1) * P], w["v_up"][:, :], start=True, stop=True)
        last.then_inc(self.v_done, 1)

    def act(self, act, c):
        act.wait_ge(self.lat_done, c + 1)
        act.copy(self.latT[:, c * BANK:(c + 1) * BANK], self.ps_lat[:, :]).then_inc(self.lat_copied, 1)
        for i, (which, half) in enumerate(self.units):
            act.wait_ge(self.proj_done, c * self.U + i + 1)
            if c:
                act.wait_ge(self.part_out[i], 16 * c)
            act.activation(self.part[i][:, 0, :], self.ps[:, i, :], ACT.Copy, scale=self.scales[:, which:which + 1])\
               .then_inc(self.high_done, 1)
        act.wait_ge(self.v_done, c + 1)
        act.copy(self.v_all[:, 4 * c:4 * c + 4, :], self.ps_v[:, :, :]).then_inc(self.v_copied, 1)
        if c == NC4 - 1:
            act.wait_ge(self.v_copied, NC4)

    def dve(self, dve, c):
        for i, (which, half) in enumerate(self.units):
            dve.wait_ge(self.high_done, c * self.U + i + 1)
            dve.scalar_tensor_tensor(self.part[i][:, 1, :], self.ps[:, i, :], self.scales[:, which:which + 1],
                                     self.part[i][:, 0, :], ALU.mult, ALU.subtract).then_inc(self.low_done, 1)

    def sync(self, sp, c):
        for i, (which, half) in enumerate(self.units):
            sp.wait_ge(self.low_done, c * self.U + i + 1)
            sp.dma_start(self.parts[which][:, half * P:(half + 1) * P, c * BANK:(c + 1) * BANK].rearrange("a r n -> r a n"),
                         self.part[i][:, :, :]).then_inc(self.part_out[i], 16)

    def sync_end(self, sp):
        for i in range(self.U):
            sp.wait_ge(self.part_out[i], 16 * NC4)


class RopeQkv(Step):

    def __init__(self, sc, sh, norm, w, cos_dram, sin_dram, parts_q, parts_k, v_all, scales):
        self.sh, self.norm, self.w, self.v_all, self.scales = sh, norm, w, v_all, scales
        self.parts = (parts_q, parts_k)
        self.tables = (cos_dram, sin_dram)
        self.table = [sc.sb(f"table{i}", [P, N]) for i in range(2)]
        self.part = [sc.sb(f"part{i}", [P, 2, BANK], FP16) for i in range(2)]
        self.product = [[sc.sb(f"product{i}{j}", [P, BANK]) for j in range(2)] for i in range(2)]
        self.rotated = [sc.sb(f"rotated{i}", [P, BANK]) for i in range(2)]
        self.ps = sc.ps("ps", [P, 2, 2, BANK])
        self.ps_v = sc.ps("ps_v", [P, 4, sh.R])
        self.table_in = sc.sem("table_in")
        self.proj_done = sc.sem("proj_done")
        self.v_done, self.v_copied = sc.sem("v_done"), sc.sem("v_copied")
        self.product_done = sc.sem("product_done")
        self.rot_done = sc.sem("rot_done")
        self.high_done, self.low_done = sc.sem("high_done"), sc.sem("low_done")
        self.part_out = [sc.sem(f"part_out{i}") for i in range(2)]

    def pe(self, pe, c):
        pe.wait_ge(self.norm.xnT_done, c + 1)
        for which in range(2):
            if c:
                pe.wait_ge(self.product_done, 2 * (c - 1) + which + 1)
            for i in range(2):
                last = pe.matmul(self.ps[:, which, i, :], self.w["qkv"][:, which, i, :],
                                 self.norm.xnT[:, c * BANK:(c + 1) * BANK], start=True, stop=True)
            last.then_inc(self.proj_done, 1)
        if c:
            pe.wait_ge(self.v_copied, c)
        for i in range(4):
            t = 4 * c + i
            last = pe.matmul(self.ps_v[:, i, :], self.norm.xnT[:, t * P:(t + 1) * P], self.w["v"][:, :],
                             start=True, stop=True)
        last.then_inc(self.v_done, 1)

    def dve(self, dve, c):
        if c == 0:
            dve.wait_ge(self.table_in, 32)
        chunk = slice(c * BANK, (c + 1) * BANK)
        for which in range(2):
            dve.wait_ge(self.proj_done, 2 * c + which + 1)
            dve.tensor_tensor(self.product[which][0][:, :], self.ps[:, which, 0, :], self.table[0][:, chunk], ALU.mult)
            dve.tensor_tensor(self.product[which][1][:, :], self.ps[:, which, 1, :], self.table[1][:, chunk], ALU.mult)\
               .then_inc(self.product_done, 1)
        for which in range(2):
            dve.wait_ge(self.product_done, 2 * c + which + 1)
            dve.tensor_tensor(self.rotated[which][:, :], self.product[which][0][:, :], self.product[which][1][:, :],
                              ALU.add).then_inc(self.rot_done, 1)
        for which in range(2):
            dve.wait_ge(self.high_done, 2 * c + which + 1)
            dve.scalar_tensor_tensor(self.part[which][:, 1, :], self.rotated[which][:, :], self.scales[:, which:which + 1],
                                     self.part[which][:, 0, :], ALU.mult, ALU.subtract).then_inc(self.low_done, 1)

    def act(self, act, c):
        act.wait_ge(self.v_done, c + 1)
        act.copy(self.v_all[:, 4 * c:4 * c + 4, :], self.ps_v[:, :, :]).then_inc(self.v_copied, 1)
        for which in range(2):
            act.wait_ge(self.rot_done, 2 * c + which + 1)
            if c:
                act.wait_ge(self.part_out[which], 16 * c)
            act.activation(self.part[which][:, 0, :], self.rotated[which][:, :], ACT.Copy,
                           scale=self.scales[:, which:which + 1]).then_inc(self.high_done, 1)
        if c == NC4 - 1:
            act.wait_ge(self.v_copied, NC4)

    def sync(self, sp, c):
        if c == 0:
            for table, dram in zip(self.table, self.tables):
                sp.dma_start(table[:, :], dram).then_inc(self.table_in, 16)
        for which in range(2):
            sp.wait_ge(self.low_done, 2 * c + which + 1)
            sp.dma_start(self.parts[which][:, :, c * BANK:(c + 1) * BANK].rearrange("a r n -> r a n"),
                         self.part[which][:, :, :]).then_inc(self.part_out[which], 16)

    def sync_end(self, sp):
        for which in range(2):
            sp.wait_ge(self.part_out[which], 16 * NC4)


def stream_phase(nc, ctx, source, norm, sink, sync_start=None, sink_lag=2, sink_first=False):
    assert sink_lag == 2 or not sink_first
    block = ctx.enter_context(nc.Block())

    def turns():
        for c in range(NC4 + sink_lag):
            there = lambda k: k if 0 <= k < NC4 else None
            yield there(c), there(c - 1), there(c - sink_lag)

    @block.sync
    def _(sp):
        if sync_start:
            sync_start(sp)
        for c in range(NC4):
            sink.sync(sp, c)
        sink.sync_end(sp)

    @block.gpsimd
    def _(pool):
        for c in range(NC4):
            source.pool(pool, c)

    @block.tensor
    def _(pe):
        for new, normed, taken in turns():
            if new is not None:
                source.pe(pe, new)
            if sink_first and taken is not None:
                sink.pe(pe, taken)
            if normed is not None:
                norm.pe(pe, normed)
            if not sink_first and taken is not None:
                sink.pe(pe, taken)

    @block.scalar
    def _(act):
        norm.act_start(act)
        for new, normed, taken in turns():
            if new is not None:
                source.act(act, new)
            if normed is not None:
                norm.act_std(act, normed)
            if sink_first and taken is not None:
                sink.act(act, taken)
            if normed is not None:
                norm.act_copy(act, normed)
            if not sink_first and taken is not None:
                sink.act(act, taken)

    @block.vector
    def _(dve):
        norm.dve_start(dve)
        for new, normed, taken in turns():
            if normed is not None:
                norm.dve_scale(dve, normed)
            if new is not None:
                source.dve(dve, new)
                source.wait_x(dve, new)
                norm.dve_stats(dve, new)
            if taken is not None:
                sink.dve(dve, taken)


def store_phase(nc, ctx, source, x_sb, out):
    stored = Scope(nc, ctx, "out").sem("stored")
    block = ctx.enter_context(nc.Block())

    @block.sync
    def _(sp):
        for c in range(NC4):
            source.wait_x(sp, c)
            sp.dma_start(out[c * BANK:(c + 1) * BANK, :].rearrange("(t p) d -> p t d", p=P), x_sb[:, 4 * c:4 * c + 4, :])\
              .then_inc(stored, 16)
        sp.wait_ge(stored, 16 * NC4)

    @block.gpsimd
    def _(pool):
        for c in range(NC4):
            source.pool(pool, c)

    @block.tensor
    def _(pe):
        for c in range(NC4):
            source.pe(pe, c)

    @block.scalar
    def _(act):
        for c in range(NC4):
            source.act(act, c)

    @block.vector
    def _(dve):
        for c in range(NC4):
            source.dve(dve, c)


class MoeShape:

    def __init__(self, name, experts, top, hidden):
        self.name, self.E, self.K, self.F = name, experts, top, hidden
        most = (N * top + experts * (P - 1)) // P
        self.TILES = -(-most // 4) * 4


def routing_phase(nc, prefix, ms, logits, softmax, place, lane, tile, weight, expert_row, ident, before, ones_bf,
                  xn, xn_dram, arrivals, sync_start):
    E, K, TILES = ms.E, ms.K, ms.TILES
    with ExitStack() as ctx:
        sc = Scope(nc, ctx, prefix)
        score = sc.sb("score", [P, NT, E])
        best = sc.sb("best", [P, NT, 8])
        best_at = sc.sb("best_at", [P, NT, 8], U32)
        at_f = sc.sb("at_f", [P, NT, K])
        iota_e = sc.sb("iota_e", [P, NT, E])
        iota_p = sc.sb("iota_p", [P, 1])
        onehot = sc.sb("onehot", [P, K, NT, E])
        taken = sc.sb("taken", [P, NT, E], BF16)
        stat = sc.sb("stat", [P, NT])
        inv = sc.sb("inv", [P, NT])
        first = sc.sb("first", [P, E, NT])
        upto = sc.sb("upto", [P, E, NT])
        count = sc.sb("count", [P, E, NT])
        ones_e = sc.sb("ones_e", [P, E])
        count_i = sc.sb("count_i", [P, E], I32)
        tiles_i = sc.sb("tiles_i", [P, E], I32)
        tiles_f = sc.sb("tiles_f", [P, E])
        tile_end = sc.sb("tile_end", [P, E])
        start = sc.sb("start", [P, E])
        rank = sc.sb("rank", [P, NT, E])
        picked = sc.sb("picked", [P, K, NT, E])
        place_f = sc.sb("place_f", [P, K, NT])
        le = sc.sb("le", [P, E])
        of_tile = sc.sb("of_tile", [P, 1])
        ps_b = sc.ps("ps_b", [P, NT, E])
        ps_c = sc.ps("ps_c", [P, NT, E])
        ps_e = sc.ps("ps_e", [1, P])
        split_i = sc.sb("split_i", [P, 2, K, NT], U32)
        consts, xn_out = sc.sem("consts"), sc.sem("xn_out")
        exp_done, shifted = sc.sem("exp_done"), sc.sem("shifted")
        taken_done, counted = sc.sem("taken_done"), sc.sem("counted")
        tile_done, row_done = sc.sem("tile_done"), sc.sem("row_done")
        warm = sc.sb("warm", [P, 1])
        chain = sc.sem("chain")
        block = ctx.enter_context(nc.Block())
        per_token = lambda a: a.unsqueeze(2).to_broadcast([P, NT, E])

        @block.sync
        def _(sp):
            sp.dma_start(xn_dram.rearrange("(t p) d -> p t d", p=P), xn[:, :, :]).then_inc(xn_out, 16)
            if sync_start:
                sync_start(sp)
            arrivals.wait(sp, f"{ms.name}_shared", "L0_attention", "L1_attention", "L1_router")
            sp.wait_ge(xn_out, 16)

        @block.gpsimd
        def _(pool):
            pool.iota(iota_e[:, :, :], pattern=[[0, NT], [1, E]], base=0, channel_multiplier=0,
                      allow_small_or_imprecise_dtypes=True)
            pool.iota(iota_p[:, :], pattern=[[0, 1]], base=0, channel_multiplier=1,
                      allow_small_or_imprecise_dtypes=True)
            pool.memset(ones_e[:, :], 1.0)
            pool.memset(first[:, :, :], 1.0).then_inc(consts, 1)
            pool.wait_ge(consts, 1)
            pool.memset(first[:, :, 0:1], 0.0).then_inc(consts, 1)

        @block.tensor
        def _(pe):
            pe.wait_ge(taken_done, 1)
            pe.matmul(ps_b[:, :, :].rearrange("p t e -> p (t e)"), before[:, :], taken[:, :, :].rearrange("p t e -> p (t e)"),
                      start=True, stop=True)
            pe.matmul(ps_c[:, :, :].rearrange("p t e -> p (t e)"), ones_bf[:, :], taken[:, :, :].rearrange("p t e -> p (t e)"),
                      start=True, stop=True).then_inc(counted, 1)
            pe.wait_ge(tile_done, 1)
            pe.matmul(ps_e[:, :], of_tile[:, :], ident[:, :], start=True, stop=True).then_inc(row_done, 1)

        if softmax:
            @block.scalar
            def _(act):
                act.wait_ge(consts, 2)
                act.activation(warm[:, :], ones_e[:, 0:1], ACT.Exp)
                act.wait_ge(shifted, 1)
                act.activation(score[:, :, :], logits, ACT.Exp).then_inc(exp_done, 1)

        @block.vector
        def _(dve):
            steps = [0]

            def then(ins):
                steps[0] += 1
                ins.then_inc(chain, 1)
                dve.wait_ge(chain, steps[0])

            dve.wait_ge(consts, 2)
            ranked = logits
            if softmax:
                then(dve.tensor_reduce(stat[:, :], logits, AX.X, ALU.max))
                dve.tensor_tensor(logits, logits, per_token(stat[:, :]), ALU.subtract).then_inc(shifted, 1)
                dve.wait_ge(exp_done, 1)
                then(dve.tensor_reduce(stat[:, :], score[:, :, :], AX.X, ALU.add))
                then(dve.reciprocal(inv[:, :], stat[:, :]))
                then(dve.tensor_tensor(score[:, :, :], score[:, :, :], per_token(inv[:, :]), ALU.mult))
                ranked = score[:, :, :]
            for t in range(NT):
                last = dve.max(best[:, t, :], ranked[:, t, :])
            then(last)
            for t in range(NT):
                last = dve.max_index(best_at[:, t, :], best[:, t, :], ranked[:, t, :])
            then(last)
            if softmax:
                then(dve.tensor_reduce(stat[:, :], best[:, :, 0:K], AX.X, ALU.add))
                then(dve.tensor_scalar(stat[:, :], stat[:, :], 1e-12, None, ALU.max))
                then(dve.reciprocal(inv[:, :], stat[:, :]))
                then(dve.tensor_scalar(inv[:, :], inv[:, :], 0.5, None, ALU.mult))
                dve.tensor_tensor(weight[:, :, :], best[:, :, 0:K], inv[:, :].unsqueeze(2).to_broadcast([P, NT, K]), ALU.mult)
            then(dve.tensor_copy(at_f[:, :, :], best_at[:, :, 0:K]))
            for k in range(K):
                last = dve.tensor_tensor(onehot[:, k, :, :], iota_e[:, :, :], per_token(at_f[:, :, k]), ALU.is_equal)
            then(last)
            total = onehot[:, 0, :, :]
            if K == 1:
                dve.tensor_copy(taken[:, :, :], total).then_inc(taken_done, 1)
            else:
                then(dve.tensor_tensor(picked[:, 0, :, :], onehot[:, 0, :, :], onehot[:, 1, :, :], ALU.add))
                then(dve.tensor_tensor(picked[:, 1, :, :], onehot[:, 2, :, :], onehot[:, 3, :, :], ALU.add))
                dve.tensor_tensor(taken[:, :, :], picked[:, 0, :, :], picked[:, 1, :, :], ALU.add).then_inc(taken_done, 1)
            dve.wait_ge(counted, 1)
            then(dve.tensor_copy(count[:, :, :].rearrange("p e t -> p t e"), ps_c[:, :, :]))
            then(dve.tensor_tensor_scan(upto[:, :, :].rearrange("p e t -> p (e t)"), first[:, :, :].rearrange("p e t -> p (e t)"),
                                        count[:, :, :].rearrange("p e t -> p (e t)"), 0.0, ALU.mult, ALU.add))
            then(dve.tensor_scalar(count_i[:, :], upto[:, :, NT - 1], float(P - 1), None, ALU.add))
            then(dve.tensor_scalar(tiles_i[:, :], count_i[:, :], P.bit_length() - 1, None, ALU.logical_shift_right))
            then(dve.tensor_copy(tiles_f[:, :], tiles_i[:, :]))
            then(dve.tensor_tensor_scan(tile_end[:, :], ones_e[:, :], tiles_f[:, :], 0.0, ALU.mult, ALU.add))
            then(dve.tensor_scalar(le[:, :], tile_end[:, :], iota_p[:, 0:1], None, ALU.is_le))
            then(dve.tensor_reduce(of_tile[:, :], le[:, :], AX.X, ALU.add))
            dve.tensor_scalar(of_tile[:, :], of_tile[:, :], float(E - 1), None, ALU.min).then_inc(tile_done, 1)
            then(dve.tensor_tensor(start[:, :], tile_end[:, :], tiles_f[:, :], ALU.subtract))
            then(dve.tensor_scalar(start[:, :], start[:, :], float(P), None, ALU.mult))
            then(dve.tensor_tensor(rank[:, :, :], upto[:, :, :].rearrange("p e t -> p t e"),
                                   count[:, :, :].rearrange("p e t -> p t e"), ALU.subtract))
            then(dve.tensor_tensor(rank[:, :, :], rank[:, :, :], start[:, :].unsqueeze(1).to_broadcast([P, NT, E]), ALU.add))
            then(dve.tensor_tensor(rank[:, :, :], rank[:, :, :], ps_b[:, :, :], ALU.add))
            for k in range(K):
                last = dve.tensor_tensor(picked[:, k, :, :], onehot[:, k, :, :], rank[:, :, :], ALU.mult)
            then(last)
            then(dve.tensor_reduce(place_f[:, :, :], picked[:, :, :, :], AX.X, ALU.add))
            then(dve.tensor_copy(place[:, 0:K, :], place_f[:, :, :]))
            dve.tensor_scalar(split_i[:, 0, :, :], place[:, 0:K, :], P - 1, None, ALU.bitwise_and)
            then(dve.tensor_scalar(split_i[:, 1, :, :], place[:, 0:K, :], P.bit_length() - 1, None, ALU.logical_shift_right))
            dve.tensor_copy(lane[:, 0:K, :], split_i[:, 0, :, :])
            then(dve.tensor_copy(tile[:, 0:K, :], split_i[:, 1, :, :]))
            dve.wait_ge(row_done, 1)
            then(dve.tensor_copy(expert_row[:, 0:TILES], ps_e[0:1, 0:TILES]))



class Gathers:

    def __init__(self, sc, ms, ring, unit, far, xn_dram, token_at):
        self.ring, self.unit, self.far, self.xn_dram, self.token_at = ring, unit, far, xn_dram, token_at
        self.x_in = [sc.sb(f"x_in{i}", [P, unit, D]) for i in range(ring)]
        self.x_places = sc.sb("x_places", [P, ms.TILES, D]) if far else None
        self.gathered = [sc.sem(f"gathered{i}") for i in range(ring)]
        self.brought = [sc.sem(f"brought{i}") for i in range(ring)] if far else None

    def units(self, pool, first, last, t_done):
        for u in range(first, last):
            slot = u % self.ring
            if u >= self.ring:
                if self.far:
                    pool.wait_ge(self.gathered[slot], (u // self.ring) * (16 * self.unit))
                else:
                    pool.wait_ge(t_done, u - self.ring + 1)
            for i in range(self.unit):
                t = u * self.unit + i
                rows = self.x_places[:, t, :] if self.far else self.x_in[slot][:, i, :]
                pool.indirect_dma_start(rows, None, self.xn_dram,
                                        bass.IndirectOffsetOnAxis(ap=self.token_at[:, t:t + 1], axis=0))\
                    .then_inc(self.gathered[slot], 16)

    def bring(self, sp, u, t_done):
        slot, turn = u % self.ring, u // self.ring
        sp.wait_ge(self.gathered[slot], (turn + 1) * (16 * self.unit))
        if turn:
            sp.wait_ge(t_done, u - self.ring + 1)
        sp.dma_start(self.x_in[slot][:, :, :], self.x_places[:, u * self.unit:(u + 1) * self.unit, :])\
          .then_inc(self.brought[slot], 16)

    def wait(self, eng, slot, uses):
        if self.far:
            eng.wait_ge(self.brought[slot], uses * 16 + 16)
        else:
            eng.wait_ge(self.gathered[slot], uses * (16 * self.unit) + 16 * self.unit)


class Inverse:

    def __init__(self, sc, ms, lane, tile, token_at):
        self.ms, self.lane, self.tile, self.token_at = ms, lane, tile, token_at
        self.iota = sc.sb("iota", [P, P])
        self.iota_h = sc.sb("iota_h", [P, ms.TILES], FP16)
        self.token = sc.sb("token", [P, NT])
        self.lanes = sc.sb("lanes", [P, 2, 4, P], FP16)
        self.tiles = sc.sb("tiles", [P, 2, 4, ms.TILES], FP16)
        self.ps = sc.ps("ps_inv", [P, ms.TILES])
        self.iota_set = sc.sem("iota_set")
        self.hot_done = sc.sem("hot_done")
        self.hot_used = sc.sem("hot_used")
        self.inverted = sc.sem("inverted")
        self.steps = [(c, k) for k in range(ms.K) for c in range(NC4)]

    def pool(self, pool):
        pool.iota(self.iota[:, :], pattern=[[1, self.iota.shape[1]]], base=0, channel_multiplier=0,
                  allow_small_or_imprecise_dtypes=True).then_inc(self.iota_set, 1)
        pool.iota(self.token[:, :], pattern=[[P, NT]], base=0, channel_multiplier=1,
                  allow_small_or_imprecise_dtypes=True).then_inc(self.iota_set, 1)
        pool.iota(self.iota_h[:, :], pattern=[[1, self.ms.TILES]], base=0, channel_multiplier=0,
                  allow_small_or_imprecise_dtypes=True).then_inc(self.iota_set, 1)

    def dve(self, dve, first, last):
        for n in range(first, min(last, len(self.steps))):
            c, k = self.steps[n]
            if n == 0:
                dve.wait_ge(self.iota_set, 3)
            if n >= 2:
                dve.wait_ge(self.hot_used, n - 1)
            for i in range(4):
                t = 4 * c + i
                dve.tensor_scalar(self.lanes[:, n % 2, i, :], self.iota[:, :], self.lane[:, k, t:t + 1],
                                  self.token[:, t:t + 1], ALU.is_equal, ALU.mult)
            shape = [P, 4, self.ms.TILES]
            dve.tensor_tensor(self.tiles[:, n % 2, :, :], self.iota_h[:, :].unsqueeze(1).to_broadcast(shape),
                              self.tile[:, k, 4 * c:4 * c + 4].unsqueeze(2).to_broadcast(shape), ALU.is_equal)\
               .then_inc(self.hot_done, 1)
            if n == len(self.steps) - 1:
                dve.wait_ge(self.hot_used, n + 1)
                dve.tensor_copy(self.token_at[:, 0:self.ms.TILES], self.ps[:, :]).then_inc(self.inverted, 1)

    def pe(self, pe, first, last):
        for n in range(first, min(last, len(self.steps))):
            pe.wait_ge(self.hot_done, n + 1)
            for i in range(4):
                mm = pe.matmul(self.ps[:, :], self.lanes[:, n % 2, i, :], self.tiles[:, n % 2, i, :],
                               start=(n == 0 and i == 0), stop=(n == len(self.steps) - 1 and i == 3))
            mm.then_inc(self.hot_used, 1)


def dispatch_phase(nc, prefix, ms, xnT, lane, tile, token_at, gathers, first_units, shared, x_sb, arrivals, score_scales):
    with ExitStack() as ctx:
        sc = Scope(nc, ctx, prefix)
        inverse = Inverse(sc, ms, lane, tile, token_at)
        if shared:
            FS = 4
            act_gate = [sc.sb(f"act_gate{i}", [P, BANK]) for i in range(2)]
            hidden = [sc.sb(f"hidden{i}", [P, FS, BANK]) for i in range(2)]
            ps_g = sc.ps("ps_g", [P, 2, BANK])
            ps_u = sc.ps("ps_u", [P, 2, BANK])
            ps_y = sc.ps("ps_y", [P, 2, BANK])
            gu_done = sc.sem("gu_done")
            silu_done = sc.sem("silu_done")
            hid_done = sc.sem("hid_done")
            y_done, x_done = sc.sem("y_done"), sc.sem("x_done")
        scales = score_scales(sc) if score_scales else None
        block = ctx.enter_context(nc.Block())

        @block.sync
        def _(sp):
            arrivals.wait(sp, f"{ms.name}_experts")

        @block.gpsimd
        def _(pool):
            inverse.pool(pool)
            pool.wait_ge(inverse.inverted, 1)
            gathers.units(pool, 0, first_units, None)

        if scales:
            @block.tensor
            def _(pe):
                inverse.pe(pe, 0, len(inverse.steps))
                scales.pe(pe)

            @block.scalar
            def _(act):
                scales.act(act)

            @block.vector
            def _(dve):
                inverse.dve(dve, 0, len(inverse.steps))
                scales.dve(dve)

        if not shared:
            return

        @block.tensor
        def _(pe):
            def down(c):
                pe.wait_ge(hid_done, FS * (c + 1))
                if c >= 2:
                    pe.wait_ge(x_done, c - 1)
                for i in range(4):
                    for f in range(FS):
                        last = pe.matmul(ps_y[:, c % 2, i * P:(i + 1) * P], hidden[c % 2][:, f, i * P:(i + 1) * P],
                                         shared["down"][:, f, :], start=(f == 0), stop=(f == FS - 1))
                last.then_inc(y_done, 1)

            for c in range(NC4):
                for f in range(FS):
                    n = c * FS + f
                    if n:
                        inverse.pe(pe, 2 * (n - 1), 2 * n)
                    if n >= 2:
                        pe.wait_ge(hid_done, n - 1)
                    cols = slice(c * BANK, (c + 1) * BANK)
                    pe.matmul(ps_g[:, n % 2, :], shared["gate"][:, f * P:(f + 1) * P], xnT[:, cols], start=True, stop=True)
                    pe.matmul(ps_u[:, n % 2, :], shared["up"][:, f * P:(f + 1) * P], xnT[:, cols],
                              start=True, stop=True).then_inc(gu_done, 1)
                    if f == 1 and c:
                        down(c - 1)
            down(NC4 - 1)

        @block.scalar
        def _(act):
            for n in range(NC4 * FS):
                act.wait_ge(gu_done, n + 1)
                if n >= 2:
                    act.wait_ge(hid_done, n - 1)
                act.activation(act_gate[n % 2][:, :], ps_g[:, n % 2, :], ACT.Silu).then_inc(silu_done, 1)

        @block.vector
        def _(dve):
            def add(c):
                dve.wait_ge(y_done, c + 1)
                xs = x_sb[:, 4 * c:4 * c + 4, :].rearrange("p t d -> p (t d)")
                dve.scalar_tensor_tensor(xs, ps_y[:, c % 2, :], 0.5, xs, ALU.mult, ALU.add).then_inc(x_done, 1)

            for n in range(NC4 * FS):
                c, f = n // FS, n % FS
                inverse.dve(dve, 2 * n, 2 * n + 2)
                dve.wait_ge(silu_done, n + 1)
                if c >= 2 and f == 0:
                    dve.wait_ge(y_done, c - 1)
                dve.tensor_tensor(hidden[c % 2][:, f, :], ps_u[:, n % 2, :], act_gate[n % 2][:, :], ALU.mult)\
                   .then_inc(hid_done, 1)
                if f == 2 and c:
                    add(c - 1)
            add(NC4 - 1)
            dve.wait_ge(x_done, NC4)


def load_experts(eng, nc, expert_row, first, count):
    _, values = nc.values_load_multi_w_load_instructions(
        expert_row[0:1, bass.ds(first, count)], [eng.engine],
        skip_runtime_bounds_check_because="routing clamps every tile's expert to 0 .. E - 1")
    return values


def swiglu_experts_phase(nc, prefix, ms, w, expert_row, gathers, first_units, y_dram, ident):
    GROUPS = ms.TILES // 4
    SIZE = 3 * P
    with ExitStack() as ctx:
        sc = Scope(nc, ctx, prefix)
        xT = [sc.sb(f"xT{i}", [P, BANK]) for i in range(2)]
        wt = [sc.sb(f"wt{i}", [P, 4, SIZE]) for i in range(4)]
        act_gate = [sc.sb(f"act_gate{i}", [P, BANK]) for i in range(2)]
        hidden = [sc.sb(f"hidden{i}", [P, BANK]) for i in range(2)]
        y = [sc.sb(f"y{i}", [P, 4, D]) for i in range(2)]
        ps_t = sc.ps("ps_t", [P, 2, BANK])
        ps_g = sc.ps("ps_g", [P, 2, BANK])
        ps_u = sc.ps("ps_u", [P, 2, BANK])
        ps_y = sc.ps("ps_y", [P, 2, BANK])
        stored = [sc.sem(f"stored{i}") for i in range(2)]
        t_done = sc.sem("t_done")
        gu_done = sc.sem("gu_done")
        y_done = sc.sem("y_done")
        xT_done = sc.sem("xT_done")
        silu_done = sc.sem("silu_done")
        y_copied = sc.sem("y_copied")
        staged = sc.sem("staged")
        hid_done = sc.sem("hid_done")
        block = ctx.enter_context(nc.Block())
        y_g = y_dram.rearrange("(g i p) d -> g p i d", i=4, p=P)

        def run_bodies(eng, one, after=0):
            for g in range(4):
                one(g, g, g // 2, g // 4)
            with eng.Fori(1, GROUPS // 4 - 1) as i:
                for m in range(4):
                    one(i * 4 + m, m, i * 2 + m // 2, i)
            for g in range(GROUPS - 4, GROUPS + after):
                one(g, g % 4, g // 2, g // 4)

        def there(g, ahead):
            return type(g) is not int or 0 <= g + ahead < GROUPS

        @block.sync
        def _(sp):
            def store(g, par):
                sp.wait_ge(y_copied, g + 3)
                sp.dma_start(y_g[bass.ds(g, 1), :, :, :].rearrange("o p i d -> (o p) i d"), y[par][:, :, :])\
                  .then_inc(stored[par], 16)

            for g in range(3):
                gathers.bring(sp, g, t_done)
            for g in range(GROUPS + 2):
                if g + 3 < GROUPS:
                    gathers.bring(sp, g + 3, t_done)
                if g >= 2:
                    store(g - 2, g % 2)
            for par in range(2):
                sp.wait_ge(stored[par], 16 * (GROUPS // 2))

        @block.gpsimd
        def _(pool):
            gathers.units(pool, first_units, ms.TILES // gathers.unit, t_done)

        @block.tensor
        def _(pe):
            def transposes(g, m, turn):
                par = m % 2
                gathers.wait(pe, m, turn)
                pe.wait_ge(xT_done, g + 1)
                for i in range(4):
                    last = pe.transpose(ps_t[:, par, i * P:(i + 1) * P], gathers.x_in[m][:, i, :], ident[:, :])
                last.then_inc(t_done, 1)

            def gate_up(g, m):
                par = m % 2
                pe.wait_ge(xT_done, g + 3)
                pe.wait_ge(staged, g + 1)
                pe.wait_ge(hid_done, g + 1)
                for i in range(4):
                    cols = slice(i * P, (i + 1) * P)
                    pe.matmul(ps_g[:, par, cols], wt[m][:, i, 0:P], xT[par][:, cols], start=True, stop=True)
                    last = pe.matmul(ps_u[:, par, cols], wt[m][:, i, P:2 * P], xT[par][:, cols], start=True, stop=True)
                last.then_inc(gu_done, 1)

            def down(g, m):
                par = m % 2
                pe.wait_ge(hid_done, g + 3)
                pe.wait_ge(y_copied, g + 1)
                for i in range(4):
                    cols = slice(i * P, (i + 1) * P)
                    last = pe.matmul(ps_y[:, par, cols], hidden[par][:, cols], wt[m][:, i, 2 * P:SIZE], start=True, stop=True)
                last.then_inc(y_done, 1)

            pe.sem_inc(gu_done, 2)
            pe.sem_inc(y_done, 2)
            transposes(0, 0, 0)
            transposes(1, 1, 0)
            gate_up(0, 0)

            def one(g, m, half, turn):
                if there(g, 2):
                    transposes(g + 2, (m + 2) % 4, turn + (m + 2) // 4)
                if there(g, 1):
                    gate_up(g + 1, (m + 1) % 4)
                down(g, m)

            run_bodies(pe, one)

        @block.scalar
        def _(act):
            act.sem_inc(xT_done, 2)
            act.sem_inc(y_copied, 2)

            def copy_xT(g, par):
                act.wait_ge(t_done, g + 1)
                act.wait_ge(gu_done, g + 1)
                act.copy(xT[par][:, :], ps_t[:, par, :]).then_inc(xT_done, 1)

            def silu(g, par):
                act.wait_ge(gu_done, g + 3)
                act.wait_ge(hid_done, g + 1)
                act.activation(act_gate[par][:, :], ps_g[:, par, :], ACT.Silu).then_inc(silu_done, 1)

            def copy_y(g, par, uses):
                act.wait_ge(y_done, g + 3)
                if not (type(uses) is int and uses == 0):
                    act.wait_ge(stored[par], uses * 16)
                act.copy(y[par][:, :, :].rearrange("p i d -> p (i d)"), ps_y[:, par, :]).then_inc(y_copied, 1)

            copy_xT(0, 0)
            copy_xT(1, 1)
            silu(0, 0)

            def one(g, m, half, turn):
                if there(g, -1):
                    copy_y(g - 1, (m + 1) % 2, half - (m + 1) % 2)
                if there(g, 2):
                    copy_xT(g + 2, m % 2)
                if there(g, 1):
                    silu(g + 1, (m + 1) % 2)

            run_bodies(act, one, after=1)

        @block.vector
        def _(dve):
            dve.sem_inc(hid_done, 2)

            def stage(g, m, experts):
                if not (type(g) is int and g < 4):
                    dve.wait_ge(y_done, g - 1)
                for i, e in enumerate(experts):
                    last = dve.tensor_copy(wt[m][:, i, :], w["experts"][:, bass.ds(e * SIZE, SIZE)])
                last.then_inc(staged, 1)

            def product(g, par):
                dve.wait_ge(silu_done, g + 1)
                dve.wait_ge(y_done, g + 1)
                dve.tensor_tensor(hidden[par][:, :], ps_u[:, par, :], act_gate[par][:, :], ALU.mult)\
                   .then_inc(hid_done, 1)

            def one(g, m, experts):
                product(g, m % 2)
                if experts:
                    stage(g + 3, (m + 3) % 4, experts)

            e = load_experts(dve, nc, expert_row, 0, 28)
            for g in range(3):
                stage(g, g, e[4 * g:4 * g + 4])
            for g in range(4):
                one(g, g, e[4 * g + 12:4 * g + 16])
            with dve.Fori(1, GROUPS // 4 - 1) as i:
                e = load_experts(dve, nc, expert_row, i * 16 + 12, 16)
                for m in range(4):
                    one(i * 4 + m, m, e[4 * m:4 * m + 4])
            e = load_experts(dve, nc, expert_row, 4 * (GROUPS - 1), 4)
            for g in range(GROUPS - 4, GROUPS):
                one(g, g % 4, e if g == GROUPS - 4 else None)


def gelu_experts_phase(nc, prefix, ms, w, expert_row, gathers, first_units, y_dram, ident):
    TILES, F1, F2 = ms.TILES, 4, 2
    SIZE1 = F1 * P + F1
    SIZE2 = F1 * F2 * P + F2
    with ExitStack() as ctx:
        sc = Scope(nc, ctx, prefix)
        xT = [sc.sb(f"xT{i}", [P, P]) for i in range(2)]
        w1 = [sc.sb(f"w1{i}", [P, SIZE1]) for i in range(2)]
        w2 = [sc.sb(f"w2{i}", [P, SIZE2]) for i in range(2)]
        w3 = [sc.sb(f"w3{i}", [P, F2, D]) for i in range(2)]
        b3 = [sc.sb(f"b3{i}", [1, D]) for i in range(2)]
        h1 = [sc.sb(f"h1{i}", [P, F1, P]) for i in range(2)]
        h2 = [sc.sb(f"h2{i}", [P, F2, P]) for i in range(2)]
        y = [sc.sb(f"y{i}", [P, D]) for i in range(2)]
        ones = sc.sb("ones", [1, P])
        ps_t = sc.ps("ps_t", [P, 2, BANK])
        ps_1 = sc.ps("ps_1", [P, 2, BANK])
        ps_2 = sc.ps("ps_2", [P, 2, BANK])
        ps_y = sc.ps("ps_y", [P, 2, BANK])
        stored = [sc.sem(f"stored{i}") for i in range(2)]
        ones_set = sc.sem("ones_set")
        t_done, h1_done, h2_done, y_done = (sc.sem(n) for n in ("t_done", "h1_done", "h2_done", "y_done"))
        xT_done, g1_done, g2_done = (sc.sem(n) for n in ("xT_done", "g1_done", "g2_done"))
        w1_staged, w2_staged, w3_staged = (sc.sem(n) for n in ("w1_staged", "w2_staged", "w3_staged"))
        y_copied = sc.sem("y_copied")
        block = ctx.enter_context(nc.Block())
        y_t = y_dram.rearrange("(t p) d -> t p d", p=P)

        def run_bodies(eng, one, after=0):
            for t in range(4):
                one(t, t % 2, t // 2)
            with eng.Fori(2, TILES // 2 - 1) as i:
                for par in range(2):
                    one(i * 2 + par, par, i)
            for t in range(TILES - 2, TILES + after):
                one(t, t % 2, t // 2)

        def there(t, ahead):
            return type(t) is not int or 0 <= t + ahead < TILES

        @block.sync
        def _(sp):
            def one(t, par, i):
                sp.wait_ge(y_copied, t + 3)
                sp.dma_start(y_t[bass.ds(t, 1), :, :].rearrange("o p d -> (o p) d"), y[par][:, :]).then_inc(stored[par], 16)

            run_bodies(sp, one)
            for par in range(2):
                sp.wait_ge(stored[par], 16 * (TILES // 2))

        @block.gpsimd
        def _(pool):
            gathers.units(pool, first_units, ms.TILES // gathers.unit, t_done)

        @block.tensor
        def _(pe):
            def transpose(t, par, uses):
                gathers.wait(pe, par, uses)
                pe.wait_ge(xT_done, t + 1)
                pe.transpose(ps_t[:, par, 0:P], gathers.x_in[par][:, 0, :], ident[:, :]).then_inc(t_done, 1)

            def first(t, par):
                pe.wait_ge(xT_done, t + 3)
                pe.wait_ge(w1_staged, t + 1)
                pe.wait_ge(g1_done, t * F1 + F1)
                for f in range(F1):
                    pe.matmul(ps_1[:, par, f * P:(f + 1) * P], w1[par][:, f * P:(f + 1) * P], xT[par][:, :],
                              start=True, stop=True).then_inc(h1_done, 1)

            def second(t, par):
                pe.wait_ge(w2_staged, t + 1)
                pe.wait_ge(g2_done, t * F2 + F2)
                for o in range(F2):
                    for f in range(F1):
                        if o == 0:
                            pe.wait_ge(g1_done, t * F1 + (2 * F1 + f + 1))
                        at = f * F2 * P + o * P
                        last = pe.matmul(ps_2[:, par, o * P:(o + 1) * P], w2[par][:, at:at + P], h1[par][:, f, :],
                                         start=(f == 0), stop=(f == F1 - 1))
                    last.then_inc(h2_done, 1)

            def third(t, par):
                pe.wait_ge(w3_staged, t + 1)
                pe.wait_ge(y_copied, t + 1)
                pe.matmul(ps_y[:, par, 0:D], ones[:, :], b3[par][:, :], start=True, stop=False)
                for f in range(F2):
                    pe.wait_ge(g2_done, t * F2 + (2 * F2 + f + 1))
                    last = pe.matmul(ps_y[:, par, 0:D], h2[par][:, f, :], w3[par][:, f, :],
                                     start=False, stop=(f == F2 - 1))
                last.then_inc(y_done, 1)

            def one(t, par, i):
                if there(t, 1):
                    first(t + 1, 1 - par)
                if there(t, 2):
                    transpose(t + 2, par, i + 1)
                if there(t, 0):
                    second(t, par)
                if there(t, -1):
                    third(t - 1, 1 - par)

            pe.sem_inc(h1_done, 2 * F1)
            pe.sem_inc(h2_done, 2 * F2)
            pe.sem_inc(y_done, 2)
            pe.wait_ge(ones_set, 1)
            transpose(0, 0, 0)
            transpose(1, 1, 0)
            first(0, 0)
            run_bodies(pe, one, after=1)

        @block.scalar
        def _(act):
            act.sem_inc(xT_done, 2)
            act.sem_inc(g1_done, 2 * F1)
            act.sem_inc(g2_done, 2 * F2)

            def copy_xT(t, par):
                act.wait_ge(t_done, t + 1)
                act.wait_ge(h1_done, t * F1 + F1)
                act.copy(xT[par][:, :], ps_t[:, par, 0:P]).then_inc(xT_done, 1)

            def gelu1(t, par):
                act.wait_ge(h2_done, t * F2 + F2)
                act.wait_ge(h1_done, t * F1 + 3 * F1)
                for f in range(F1):
                    act.activation(h1[par][:, f, :], ps_1[:, par, f * P:(f + 1) * P], ACT.Gelu,
                                   bias=w1[par][:, F1 * P + f:F1 * P + f + 1]).then_inc(g1_done, 1)

            def gelu2(t, par):
                act.wait_ge(y_done, t + 1)
                act.wait_ge(h2_done, t * F2 + 3 * F2)
                for f in range(F2):
                    at = F1 * F2 * P + f
                    act.activation(h2[par][:, f, :], ps_2[:, par, f * P:(f + 1) * P], ACT.Gelu,
                                   bias=w2[par][:, at:at + 1]).then_inc(g2_done, 1)

            def one(t, par, i):
                if there(t, 1):
                    gelu1(t + 1, 1 - par)
                if there(t, 2):
                    copy_xT(t + 2, par)
                gelu2(t, par)

            copy_xT(0, 0)
            copy_xT(1, 1)
            gelu1(0, 0)
            run_bodies(act, one)

        @block.vector
        def _(dve):
            dve.memset(ones[:, :], 1.0).then_inc(ones_set, 1)
            dve.sem_inc(y_copied, 2)

            def stage1(t, par, e):
                dve.wait_ge(g1_done, t * F1 + F1)
                dve.tensor_copy(w1[par][:, :], w["w1"][:, bass.ds(e * SIZE1, SIZE1)]).then_inc(w1_staged, 1)

            def stage2(t, par, e):
                dve.wait_ge(g2_done, t * F2 + F2)
                dve.tensor_copy(w2[par][:, :], w["w2"][:, bass.ds(e * SIZE2, SIZE2)]).then_inc(w2_staged, 1)

            def stage3(t, par, e):
                dve.wait_ge(y_done, t + 1)
                dve.tensor_copy(b3[par][:, :], w["b3"][:, bass.ds(e * D, D)])
                dve.tensor_copy(w3[par][:, :, :].rearrange("p f d -> p (f d)"),
                                w["w3"][:, bass.ds(e * F2 * D, F2 * D)]).then_inc(w3_staged, 1)

            def copy_y(t, par, uses):
                dve.wait_ge(y_done, t + 3)
                if not (type(uses) is int and uses == 0):
                    dve.wait_ge(stored[par], uses * 16)
                dve.tensor_copy(y[par][:, :], ps_y[:, par, 0:D]).then_inc(y_copied, 1)

            def one(t, par, i, experts):
                if there(t, 2):
                    stage1(t + 2, par, experts[2])
                if there(t, -2):
                    copy_y(t - 2, par, i - 1)
                if there(t, 1):
                    stage2(t + 1, 1 - par, experts[1])
                if there(t, 0):
                    stage3(t, par, experts[0])

            e = load_experts(dve, nc, expert_row, 0, 6)
            stage1(0, 0, e[0])
            stage1(1, 1, e[1])
            stage2(0, 0, e[0])
            for t in range(4):
                one(t, t % 2, t // 2, e[t:t + 3])
            with dve.Fori(2, TILES // 2 - 1) as i:
                e = load_experts(dve, nc, expert_row, i * 2, 4)
                for par in range(2):
                    one(i * 2 + par, par, i, e[par:par + 3])
            e = load_experts(dve, nc, expert_row, TILES - 2, 2)
            for t in range(TILES - 2, TILES + 2):
                one(t, t % 2, t // 2, e[t - (TILES - 2):])
            dve.wait_ge(y_copied, TILES + 2)



L0_ATTN = AttnShape(8, 32, 2)
L1_ATTN = AttnShape(16, 8, 1)
L0_MOE = MoeShape("L0", 8, 1, 512)
L1_MOE = MoeShape("L1", 32, 4, 128)


GROUPS_AHEAD = 7


def build(nc, a, out, sections=6):
    xn_dram = nc.dram_tensor("xn_rows", [N, D], F32, kind="Internal").ap()
    y_dram = nc.dram_tensor("y_by_expert", [L1_MOE.TILES * P, D], F32, kind="Internal").ap()
    max_dram = nc.dram_tensor("max_rows", [2 * NT, P], FP16, kind="Internal").ap()
    parts = {}
    for n, sh in ((0, L0_ATTN), (1, L1_ATTN)):
        parts[n] = [nc.dram_tensor(f"parts_{s}{n}", [2, sh.R, N], FP16, kind="Internal").ap() for s in "qk"]
    W1, W2, W3 = 4 * P + 4, 8 * P + 2, 2 * D
    Scope.used = []
    with ExitStack() as ctx:
        sc = Scope(nc, ctx, "all")
        x_sb = sc.sb("x", [P, NT, D])
        xn = sc.sb("xn", [P, NT, D])
        xnT = sc.sb("xnT", [P, N])
        logits = sc.sb("logits", [P, NT * L1_MOE.E])
        place = sc.sb("place", [P, L1_MOE.K, NT], U32)
        lane = sc.sb("lane", [P, L1_MOE.K, NT])
        tile = sc.sb("tile", [P, L1_MOE.K, NT], FP16)
        token_at = sc.sb("token_at", [P, L1_MOE.TILES], U32)
        weight = sc.sb("weight", [P, NT, L1_MOE.K])
        expert_row = sc.sb("expert_row", [1, L1_MOE.TILES], I32)
        ident = sc.sb("ident", [P, P])
        ident_h = sc.sb("ident_h", [P, P], FP16)
        before = sc.sb("before", [P, P], BF16)
        ones_bf = sc.sb("ones_bf", [P, P], BF16)
        ones = sc.sb("ones", [P, P])
        score_scale = [sc.sb(f"score_scale{i}", [P, 3]) for i in range(2)]
        experts = sc.sb("experts", [P, L0_MOE.E * (W1 + W2 + W3)])
        w3_at = L0_MOE.E * (W1 + W2)
        w0 = {"w1": experts[:, 0:L0_MOE.E * W1], "w2": experts[:, L0_MOE.E * W1:w3_at],
              "w3": experts[:, w3_at:], "b3": sc.sb("b3", [1, L0_MOE.E * D]),
              "router": sc.sb("router0", [P, L0_MOE.E]), "router_bias": sc.sb("router_bias0", [P, L0_MOE.E])}
        aw0 = {"q": sc.sb("wq", [P, L0_ATTN.R]), "kv_down": sc.sb("kv_down", [P, 64]),
               "k_up": sc.sb("k_up", [64, L0_ATTN.R]), "v_up": sc.sb("v_up", [64, L0_ATTN.R]),
               "o": sc.sb("wo0", [P, 2, D])}
        shared = {"gate": sc.sb("sgate", [P, 4 * P]), "up": sc.sb("sup", [P, 4 * P]), "down": sc.sb("sdown", [P, 4, D])}
        w1 = {"experts": experts[:, 0:L1_MOE.E * 3 * P], "router": sc.sb("router1", [P, L1_MOE.E]),
              "router_bias": sc.sb("router_bias1", [P, L1_MOE.E]), "shared": shared}
        aw1 = {"qkv": sc.sb("wqkv", [P, 2, 2, P]), "v": sc.sb("wv", [P, P]), "o": sc.sb("wo1", [P, 1, D])}
        arrivals = Arrivals(nc)

        def start_all(sp, pairs):
            for name, dst, src in pairs:
                arrivals.start(sp, name, dst, src)

        def start_L0_experts(sp):
            start_all(sp, (("L0_experts", w0["w1"], a["L0_w1"]), ("L0_experts", w0["w2"], a["L0_w2"]),
                           ("L0_experts", w0["w3"], a["L0_w3"]), ("L0_experts", w0["b3"][:, :], a["L0_b3"])))

        def start_L1_others(sp):
            start_all(sp, (("L1_router", w1["router"][:, :], a["L1_router"]),
                           ("L1_router", w1["router_bias"][:, :], a["L1_router_bias"].partition_broadcast(P)),
                           ("L1_attention", aw1["qkv"][:, :, :, :].rearrange("p a b c -> p (a b c)"), a["L1_wqk"]),
                           ("L1_attention", aw1["v"][:, :], a["L1_wv"]),
                           ("L1_attention", aw1["o"][:, 0, :], a["L1_wo"]),
                           ("L1_shared", shared["gate"][:, :], a["L1_sgate"]),
                           ("L1_shared", shared["up"][:, :], a["L1_sup"]),
                           ("L1_shared", shared["down"][:, :, :], a["L1_sdown"].rearrange("(f p) d -> p f d", p=P))))

        def moe(prefix, ms, w, score_scales=None, sync_start=None):
            routing_phase(nc, prefix + "r", ms, logits_of(ms), ms.K > 1, place, lane, tile, weight, expert_row,
                          ident, before, ones_bf, xn, xn_dram, arrivals, sync_start)
            phase, ring, unit, first_units = (swiglu_experts_phase, 4, 4, GROUPS_AHEAD) if ms.K > 1 else (gelu_experts_phase, 2, 1, 0)
            with ExitStack() as inner:
                gathers = Gathers(Scope(nc, inner, prefix + "g"), ms, ring, unit, ms.K > 1, xn_dram, token_at)
                dispatch_phase(nc, prefix + "d", ms, xnT, lane, tile, token_at, gathers, first_units, w.get("shared"),
                               x_sb, arrivals, score_scales)
                phase(nc, prefix + "e", ms, w, expert_row, gathers, first_units, y_dram[0:ms.TILES * P, :], ident)
            clear_semaphores(nc)

        def logits_of(ms):
            return logits[:, 0:NT * ms.E].rearrange("p (t e) -> p t e", e=ms.E)

        def combine(s, ms):
            return Combine(s, ms, place, weight, y_dram[0:ms.TILES * P, :], x_sb)

        def router(s, ms, norm, w):
            return RouterLogits(s, ms, norm, w["router"], w["router_bias"], logits_of(ms))

        def finish(source_of):
            with ExitStack() as inner:
                store_phase(nc, inner, source_of(Scope(nc, inner, "fin")), x_sb, out)

        def attention(prefix, n, sh, ms, qkv_of, w_o, last, next_ms, next_w):
            with ExitStack() as inner:
                s2 = Scope(nc, inner, prefix)
                v_all = s2.sb("v_all", [P, NT, sh.R])
                with ExitStack() as phase:
                    s3 = Scope(nc, phase, prefix + "q")
                    norm = Norm(s3, x_sb, xn, xnT, ident)
                    stream_phase(nc, phase, combine(s3, ms), norm, qkv_of(s3, norm, v_all),
                                 sink_lag=1 if ms.K > 1 else 2, sink_first=ms.K == 1)
                attn_tok = s2.sb("attn_tok", [P, NT, sh.R])
                scores_phase(nc, prefix + "s", sh, parts[n][0], parts[n][1], max_dram, v_all, attn_tok, ident, ident_h,
                             score_scale[n][:, 2:3])
                clear_semaphores(nc)
                if last:
                    finish(lambda s: AttnOut(s, sh, attn_tok, w_o, x_sb, ident))
                else:
                    with ExitStack() as phase:
                        s3 = Scope(nc, phase, prefix + "o")
                        norm = Norm(s3, x_sb, xn, xnT, ident)
                        stream_phase(nc, phase, AttnOut(s3, sh, attn_tok, w_o, x_sb, ident), norm,
                                     router(s3, next_ms, norm, next_w),
                                     start_L1_others if n == 0 else None)

        x_in = [nc.alloc_semaphore(f"x_in{c}") for c in range(NC4)]
        with ExitStack() as inner:
            s2 = Scope(nc, inner, "const")
            made = s2.sem("made")
            block = inner.enter_context(nc.Block())

            @block.sync
            def _(sp):
                for c in range(NC4):
                    sp.dma_start(x_sb[:, 4 * c:4 * c + 4, :], a["x"][c * BANK:(c + 1) * BANK, :]
                                 .rearrange("(t p) d -> p t d", p=P)).then_inc(x_in[c], 16)
                start_all(sp, (("L0_router", w0["router"][:, :], a["L0_router"]),
                               ("L0_router", w0["router_bias"][:, :], a["L0_router_bias"].partition_broadcast(P))))
                arrivals.wait(sp, "L0_router")

            @block.gpsimd
            def _(pool):
                pool.memset(ident[:, :], 0.0)
                pool.memset(ident_h[:, :], 0.0)
                pool.memset(ones_bf[:, :], 1.0)
                pool.memset(ones[:, :], 1.0)
                pool.memset(before[:, :], 1.0).then_inc(made, 1)
                pool.wait_ge(made, 1)
                for m in (ident, ident_h):
                    pool.affine_select(out=m[:, :], in_=m[:, :], compare_op=ALU.not_equal, fill=1.0, base=0,
                                       pattern=[[-1, P]], channel_multiplier=1)
                pool.affine_select(out=before[:, :], in_=before[:, :], compare_op=ALU.is_gt, fill=0.0, base=0,
                                   pattern=[[1, P]], channel_multiplier=-1).then_inc(made, 1)
                pool.wait_ge(made, 2)

        def start_L0_rest(sp):
            start_L0_experts(sp)
            start_all(sp, [("L0_attention", dst, src) for dst, src in (
                (aw0["q"][:, :], a["L0_wq"]), (aw0["kv_down"][:, :], a["L0_kv_down"]), (aw0["k_up"][:, :], a["L0_k_up"]),
                (aw0["v_up"][:, :], a["L0_v_up"]), (aw0["o"][:, :, :], a["L0_wo"].rearrange("(r p) d -> p r d", p=P)))])

        with ExitStack() as phase:
            s3 = Scope(nc, phase, "m1n")
            norm = Norm(s3, x_sb, xn, xnT, ident)
            stream_phase(nc, phase, LoadedX(x_in), norm, router(s3, L0_MOE, norm, w0), start_L0_rest)
        k_factors = [aw0["kv_down"][:, :], aw0["k_up"][:, :]]
        moe("m1", L0_MOE, w0, lambda s: ScoreScales(s, L0_ATTN, [aw0["q"][:, :]] + k_factors, 32 ** -0.5, ones,
                                                    score_scale[0]))
        if sections == 1:
            return finish(lambda s: combine(s, L0_MOE))
        attention("a1", 0, L0_ATTN, L0_MOE,
                  lambda s, norm, v_all: LatentQkv(s, L0_ATTN, norm, aw0, *parts[0], v_all, score_scale[0]),
                  aw0["o"], sections == 2, L0_MOE, w0)
        if sections == 2:
            return
        moe("m2", L0_MOE, w0, lambda s: ScoreScales(s, L1_ATTN, [aw1["qkv"][:, which, 0, :] for which in range(2)],
                                                    8 ** -0.5, ones, score_scale[1]))
        if sections == 3:
            return finish(lambda s: combine(s, L0_MOE))

        with ExitStack() as phase:
            s3 = Scope(nc, phase, "m3n")
            norm = Norm(s3, x_sb, xn, xnT, ident)
            stream_phase(nc, phase, combine(s3, L0_MOE), norm, router(s3, L1_MOE, norm, w1))
        moe("m3", L1_MOE, w1, sync_start=lambda sp: start_all(sp, [("L1_experts", w1["experts"], a["L1_experts"])]))
        if sections == 4:
            return finish(lambda s: combine(s, L1_MOE))
        attention("a2", 1, L1_ATTN, L1_MOE,
                  lambda s, norm, v_all: RopeQkv(s, L1_ATTN, norm, aw1, a["cos"], a["sin"], *parts[1], v_all,
                                                 score_scale[1]),
                  aw1["o"], sections == 5, L1_MOE, w1)
        if sections == 5:
            return
        moe("m4", L1_MOE, w1)
        finish(lambda s: combine(s, L1_MOE))


def lay_out(i):
    f = lambda v: np.ascontiguousarray(np.asarray(v))
    i = {k: np.asarray(v) for k, v in i.items()}
    a = {"x": f(i["L0_attn_x"].reshape(N, D))}
    a["L0_router"] = f(i["L0_ffn_Wr"])
    a["L0_router_bias"] = f(i["L0_ffn_br"])
    w1 = i["L0_ffn_W1"].transpose(1, 0, 2)
    w2 = i["L0_ffn_W2"].reshape(8, 4, P, 256).transpose(2, 0, 1, 3).reshape(P, 8, 1024)
    b1 = i["L0_ffn_b1"].reshape(8, 4, P).transpose(2, 0, 1)
    b2 = i["L0_ffn_b2"].reshape(8, 2, P).transpose(2, 0, 1)
    a["L0_w1"] = f(np.concatenate([w1, b1], axis=2).reshape(P, -1))
    a["L0_w2"] = f(np.concatenate([w2, b2], axis=2).reshape(P, -1))
    a["L0_w3"] = f(i["L0_ffn_W3"].reshape(8, 2, P, D).transpose(2, 0, 1, 3).reshape(P, -1))
    a["L0_b3"] = f(i["L0_ffn_b3"].reshape(1, -1))
    a["L0_wq"] = f(i["L0_attn_Wq"].T)
    a["L0_kv_down"] = f(i["L0_attn_Wkv_down"].T)
    a["L0_k_up"] = f(i["L0_attn_Wk_up"].T)
    a["L0_v_up"] = f(i["L0_attn_Wv_up"].T)
    a["L0_wo"] = f(i["L0_attn_Wo"].T)
    a["L1_router"] = f(i["L1_ffn_router_w"].T)
    a["L1_router_bias"] = f(i["L1_ffn_router_bias"])
    gate, up = i["L1_ffn_gate_w"].transpose(2, 0, 1), i["L1_ffn_up_w"].transpose(2, 0, 1)
    down = i["L1_ffn_down_w"].transpose(2, 0, 1)
    a["L1_experts"] = f(np.concatenate([gate, up, down], axis=2).reshape(P, -1))
    a["L1_sgate"] = f(i["L1_ffn_sgate_w"].T)
    a["L1_sup"] = f(i["L1_ffn_sup_w"].T)
    a["L1_sdown"] = f(i["L1_ffn_sdown_w"].T)
    qkv = i["L1_attn_Wqkv"].reshape(P, 3, 16, 2, 4)
    a["L1_wqk"] = f(np.stack([qkv[:, :2], qkv[:, :2, :, ::-1]], axis=2).reshape(P, -1))
    a["L1_wv"] = f(qkv[:, 2].reshape(P, P))
    a["L1_wo"] = f(i["L1_attn_Wo"])
    inv_freq = (1.0 / 10000.0 ** (np.arange(0, 8, 2, dtype=np.float32) / np.float32(8))).astype(np.float32)
    angle = np.outer(np.arange(N, dtype=np.float32), inv_freq).astype(np.float32).T
    a["cos"] = f(np.tile(np.cos(angle), (32, 1)).astype(np.float32))
    a["sin"] = f(np.tile(np.concatenate([-np.sin(angle), np.sin(angle)]), (16, 1)).astype(np.float32))
    return a


def kernel(**inputs):
    import numpy as _np
    import concourse.bacc as _bacc
    from concourse import mybir as _mybir
    from concourse.bass_utils import run_bass_kernel_spmd as _run

    nc = _bacc.Bacc("TRN2", target_bir_lowering=False, num_devices=1)
    arrays = {f"in_{k}": v for k, v in lay_out(inputs).items()}
    aps = {k[3:]: nc.dram_tensor(k, v.shape, _mybir.dt.from_np(v.dtype), kind="ExternalInput").ap()
           for k, v in arrays.items()}
    out = nc.dram_tensor("out_0", (N, D), F32, kind="ExternalOutput").ap()
    build(nc, aps, out)
    r = _run(nc, [arrays], core_ids=[0])
    return r.results[0]["out_0"].reshape(1, N, D)
```
